# Optimizing a Trainium2 kernel written in Bass

```python
import numpy as np
import jax
import jax.numpy as jnp

def _softmax(x, axis=-1):
    return jax.nn.softmax(x, axis=axis)

def _gelu(x):
    return jax.nn.gelu(x, approximate=True)

def _silu(x):
    return jax.nn.silu(x)

def _sigmoid(x):
    return jax.nn.sigmoid(x)

def _layernorm(x, axis=-1, eps=1e-05):
    m = jnp.mean(x, axis=axis, keepdims=True)
    v = jnp.var(x, axis=axis, keepdims=True)
    return (x - m) / jnp.sqrt(v + eps)

def _scatter_add(tgt, idx, src, axis=0):
    return tgt.at[idx].add(src)

def _segment_sum(src, seg, n):
    return jax.ops.segment_sum(src, seg, n)
kernel_name = 'mk_adaln_attn_ffn_d2_seqx_r8_13c2ce'

def setup_inputs(seed: int=0):
    np.random.seed(seed)
    _w = jnp.asarray

    def _rec_inputs():
        import jax
        import jax.numpy as jnp
        _rk = jax.random.key(seed)
        x = -0.000125 + 0.9999 * jax.random.normal(jax.random.fold_in(_rk, 1), (4, 256, 256), jnp.float32)
        _lenS = 256 - jax.random.randint(jax.random.fold_in(_rk, 7), (4,), 0, max(1, 256 // 4) + 1, jnp.int32)
        _lenS2 = 256 - jax.random.randint(jax.random.fold_in(_rk, 8), (4,), 0, max(1, 256 // 4) + 1, jnp.int32)
        fside_BxSxS_0 = -1.52775e-05 + 0.999936 * jax.random.normal(jax.random.fold_in(_rk, 11), (4, 256, 256), jnp.float32)
        cond_512 = -5.03954e-05 + 1.00559 * jax.random.normal(jax.random.fold_in(_rk, 12), (4, 64), jnp.float32)
        return (x, fside_BxSxS_0, cond_512)
    x, fside_BxSxS_0, cond_512 = _rec_inputs()

    def _L0_cond_setup():
        import jax, jax.numpy as jnp
        from jax import lax
        import numpy as np
        B, T, C, TD = (8, 256, 256, 64)

        def _bi_wkv(r, k, v, w, u, time_emb):
            tf = jax.nn.sigmoid(jnp.sum(time_emb, axis=-1))[:, None, None]
            decay = jnp.exp(-jnp.exp(w.astype(jnp.float32)))[None, :] * (0.5 + 0.5 * tf[:, :, 0])
            kf = k.astype(jnp.float32)
            vf = v.astype(jnp.float32)
            ek = jnp.exp(jnp.minimum(kf, 30.0))
            ekv = ek * vf

            def step(carry, x):
                a, b = carry
                ekv_t, ek_t = x
                a = a * decay + ekv_t
                b = b * decay + ek_t
                return ((a, b), (a, b))
            ekv_t = jnp.swapaxes(ekv, 0, 1)
            ek_t = jnp.swapaxes(ek, 0, 1)
            init = (jnp.zeros_like(decay), jnp.zeros_like(decay))
            _, (nf, df) = lax.scan(step, init, (ekv_t, ek_t))
            _, (nb, db) = lax.scan(step, init, (ekv_t, ek_t), reverse=True)
            nf = jnp.swapaxes(nf, 0, 1)
            df = jnp.swapaxes(df, 0, 1)
            nb = jnp.swapaxes(nb, 0, 1)
            db = jnp.swapaxes(db, 0, 1)
            euk = jnp.exp(jnp.minimum(u.astype(jnp.float32)[None, None, :] + kf, 30.0))
            num = nf + nb - ekv + euk * vf
            den = df + db - ek + euk
            base = jax.nn.sigmoid(r.astype(jnp.float32)) * (num / jnp.maximum(den, 1e-08))
            out = base * (0.8 + 0.2 * tf)
            return out.astype(r.dtype)
        key = jax.random.key(seed)
        ks = jax.random.split(key, 6)
        return {'r': jax.random.normal(ks[0], (B, T, C), dtype=jnp.float32), 'k': jax.random.normal(ks[1], (B, T, C), dtype=jnp.float32), 'v': jax.random.normal(ks[2], (B, T, C), dtype=jnp.float32), 'w': jax.random.normal(ks[3], (C,), dtype=jnp.float32), 'u': jax.random.normal(ks[4], (C,), dtype=jnp.float32), 'time_emb': jax.random.normal(ks[5], (B, TD), dtype=jnp.float32)}
    _L0_cond_all = _L0_cond_setup()
    _L0_cond_in = {k: v for k, v in _L0_cond_all.items() if k in ('w', 'u')}
    del _L0_cond_all

    def _L0_attn_setup():
        import jax, jax.numpy as jnp
        import numpy as np
        NH = 16
        key = jax.random.key(seed)
        ks = jax.random.split(key, 5)
        B, T, D = (2, 256, 256)
        scale = 0.02
        return {'x': jax.random.normal(ks[0], (B, T, D), dtype=jnp.float32), 'Wq': jax.random.normal(ks[1], (D, D), dtype=jnp.float32) * scale, 'Wk': jax.random.normal(ks[2], (D, D), dtype=jnp.float32) * scale, 'Wv': jax.random.normal(ks[3], (D, D), dtype=jnp.float32) * scale, 'Wo': jax.random.normal(ks[4], (D, D), dtype=jnp.float32) * scale}
    _L0_attn_all = _L0_attn_setup()
    _L0_attn_in = {k: v for k, v in _L0_attn_all.items() if k in ('Wq', 'Wk', 'Wv', 'Wo')}
    del _L0_attn_all

    def _L0_cond2_setup():
        import jax, jax.numpy as jnp
        from jax import lax
        import numpy as np
        B, T, C, TD = (8, 256, 256, 64)

        def _bi_wkv(r, k, v, w, u, time_emb):
            tf = jax.nn.sigmoid(jnp.sum(time_emb, axis=-1))[:, None, None]
            decay = jnp.exp(-jnp.exp(w.astype(jnp.float32)))[None, :] * (0.5 + 0.5 * tf[:, :, 0])
            kf = k.astype(jnp.float32)
            vf = v.astype(jnp.float32)
            ek = jnp.exp(jnp.minimum(kf, 30.0))
            ekv = ek * vf

            def step(carry, x):
                a, b = carry
                ekv_t, ek_t = x
                a = a * decay + ekv_t
                b = b * decay + ek_t
                return ((a, b), (a, b))
            ekv_t = jnp.swapaxes(ekv, 0, 1)
            ek_t = jnp.swapaxes(ek, 0, 1)
            init = (jnp.zeros_like(decay), jnp.zeros_like(decay))
            _, (nf, df) = lax.scan(step, init, (ekv_t, ek_t))
            _, (nb, db) = lax.scan(step, init, (ekv_t, ek_t), reverse=True)
            nf = jnp.swapaxes(nf, 0, 1)
            df = jnp.swapaxes(df, 0, 1)
            nb = jnp.swapaxes(nb, 0, 1)
            db = jnp.swapaxes(db, 0, 1)
            euk = jnp.exp(jnp.minimum(u.astype(jnp.float32)[None, None, :] + kf, 30.0))
            num = nf + nb - ekv + euk * vf
            den = df + db - ek + euk
            base = jax.nn.sigmoid(r.astype(jnp.float32)) * (num / jnp.maximum(den, 1e-08))
            out = base * (0.8 + 0.2 * tf)
            return out.astype(r.dtype)
        key = jax.random.key(seed)
        ks = jax.random.split(key, 6)
        return {'r': jax.random.normal(ks[0], (B, T, C), dtype=jnp.float32), 'k': jax.random.normal(ks[1], (B, T, C), dtype=jnp.float32), 'v': jax.random.normal(ks[2], (B, T, C), dtype=jnp.float32), 'w': jax.random.normal(ks[3], (C,), dtype=jnp.float32), 'u': jax.random.normal(ks[4], (C,), dtype=jnp.float32), 'time_emb': jax.random.normal(ks[5], (B, TD), dtype=jnp.float32)}
    _L0_cond2_all = _L0_cond2_setup()
    _L0_cond2_in = {k: v for k, v in _L0_cond2_all.items() if k in ('w', 'u')}
    del _L0_cond2_all

    def _L0_ffn_setup():
        import jax, jax.numpy as jnp
        import numpy as np
        B, S, D, E, TOPK, H = (8, 256, 256, 8, 2, 16)
        DH = D // H
        FH = D // H
        ROUTE_LEN = 256
        key = jax.random.key(seed)
        ks = jax.random.split(key, 8)
        s = 0.02
        return {'x': jax.random.normal(ks[0], (B, S, D), jnp.float32), 'switch_w': jax.random.normal(ks[1], (E, D * ROUTE_LEN), jnp.float32) * s, 'switch_b': jnp.zeros((E,), jnp.float32), 'w1': jax.random.normal(ks[2], (E, FH, DH), jnp.float32) * s, 'b1': jnp.zeros((E, FH), jnp.float32), 'w2': jax.random.normal(ks[3], (E, DH, FH), jnp.float32) * s, 'b2': jnp.zeros((E, DH), jnp.float32), 'w3': jax.random.normal(ks[4], (D, D), jnp.float32) * s, 'b3': jnp.zeros((D,), jnp.float32)}
    _L0_ffn_all = _L0_ffn_setup()
    _L0_ffn_in = {k: v for k, v in _L0_ffn_all.items() if k in ('switch_w', 'switch_b', 'w1', 'b1', 'w2', 'b2', 'w3', 'b3')}
    del _L0_ffn_all

    def _L1_cond_setup():
        import jax, jax.numpy as jnp
        from jax import lax
        import numpy as np
        B, T, C, TD = (8, 256, 256, 64)

        def _bi_wkv(r, k, v, w, u, time_emb):
            tf = jax.nn.sigmoid(jnp.sum(time_emb, axis=-1))[:, None, None]
            decay = jnp.exp(-jnp.exp(w.astype(jnp.float32)))[None, :] * (0.5 + 0.5 * tf[:, :, 0])
            kf = k.astype(jnp.float32)
            vf = v.astype(jnp.float32)
            ek = jnp.exp(jnp.minimum(kf, 30.0))
            ekv = ek * vf

            def step(carry, x):
                a, b = carry
                ekv_t, ek_t = x
                a = a * decay + ekv_t
                b = b * decay + ek_t
                return ((a, b), (a, b))
            ekv_t = jnp.swapaxes(ekv, 0, 1)
            ek_t = jnp.swapaxes(ek, 0, 1)
            init = (jnp.zeros_like(decay), jnp.zeros_like(decay))
            _, (nf, df) = lax.scan(step, init, (ekv_t, ek_t))
            _, (nb, db) = lax.scan(step, init, (ekv_t, ek_t), reverse=True)
            nf = jnp.swapaxes(nf, 0, 1)
            df = jnp.swapaxes(df, 0, 1)
            nb = jnp.swapaxes(nb, 0, 1)
            db = jnp.swapaxes(db, 0, 1)
            euk = jnp.exp(jnp.minimum(u.astype(jnp.float32)[None, None, :] + kf, 30.0))
            num = nf + nb - ekv + euk * vf
            den = df + db - ek + euk
            base = jax.nn.sigmoid(r.astype(jnp.float32)) * (num / jnp.maximum(den, 1e-08))
            out = base * (0.8 + 0.2 * tf)
            return out.astype(r.dtype)
        key = jax.random.key(seed)
        ks = jax.random.split(key, 6)
        return {'r': jax.random.normal(ks[0], (B, T, C), dtype=jnp.float32), 'k': jax.random.normal(ks[1], (B, T, C), dtype=jnp.float32), 'v': jax.random.normal(ks[2], (B, T, C), dtype=jnp.float32), 'w': jax.random.normal(ks[3], (C,), dtype=jnp.float32), 'u': jax.random.normal(ks[4], (C,), dtype=jnp.float32), 'time_emb': jax.random.normal(ks[5], (B, TD), dtype=jnp.float32)}
    _L1_cond_all = _L1_cond_setup()
    _L1_cond_in = {k: v for k, v in _L1_cond_all.items() if k in ('w', 'u')}
    del _L1_cond_all

    def _L1_attn_setup():
        import jax, jax.numpy as jnp
        import numpy as np
        B, T, C = (4, 256, 256)
        H = 32
        N = C // H
        N_LAYER = 12
        LAYER_ID = 6
        EPS = 1e-05 * 144
        key = jax.random.key(seed)
        ks = jax.random.split(key, 8)
        r01 = LAYER_ID / N_LAYER
        r1a0 = 1.0 - LAYER_ID / N_LAYER
        ddd = jnp.arange(C, dtype=jnp.float32) / C
        time_maa_k = (ddd ** r1a0).reshape(1, 1, C)
        time_maa_v = time_maa_k + 0.3 * r01
        time_maa_r = (ddd ** (0.5 * r1a0)).reshape(1, 1, C)
        time_maa_g = time_maa_r
        h = jnp.arange(H, dtype=jnp.float32) / (H - 1)
        time_decay = (-6.0 + 5.0 * h ** (0.7 + 0.3 * r01)).reshape(H, 1)
        zigzag = (((jnp.arange(H) + 1) % 3).astype(jnp.float32) - 1.0) * 0.1
        time_faaaa = (r01 * (1.0 - h) + zigzag).reshape(H, 1)

        def W(k):
            return jax.random.normal(k, (C, C), dtype=jnp.float32) * 0.02
        return {'x': jax.random.normal(ks[0], (B, T, C), dtype=jnp.float32), 'time_maa_k': time_maa_k, 'time_maa_v': time_maa_v, 'time_maa_r': time_maa_r, 'time_maa_g': time_maa_g, 'time_decay': time_decay, 'time_faaaa': time_faaaa, 'Wr': W(ks[1]), 'Wk': W(ks[2]), 'Wv': W(ks[3]), 'Wg': W(ks[4]), 'Wo': W(ks[5]), 'gamma': jnp.ones((C,), jnp.float32), 'beta': jnp.zeros((C,), jnp.float32)}
    _L1_attn_all = _L1_attn_setup()
    _L1_attn_in = {k: v for k, v in _L1_attn_all.items() if k in ('time_maa_k', 'time_maa_v', 'time_maa_r', 'time_maa_g', 'time_decay', 'time_faaaa', 'Wr', 'Wk', 'Wv', 'Wg', 'Wo', 'gamma', 'beta')}
    del _L1_attn_all

    def _L1_cond2_setup():
        import jax, jax.numpy as jnp
        from jax import lax
        import numpy as np
        B, T, C, TD = (8, 256, 256, 64)

        def _bi_wkv(r, k, v, w, u, time_emb):
            tf = jax.nn.sigmoid(jnp.sum(time_emb, axis=-1))[:, None, None]
            decay = jnp.exp(-jnp.exp(w.astype(jnp.float32)))[None, :] * (0.5 + 0.5 * tf[:, :, 0])
            kf = k.astype(jnp.float32)
            vf = v.astype(jnp.float32)
            ek = jnp.exp(jnp.minimum(kf, 30.0))
            ekv = ek * vf

            def step(carry, x):
                a, b = carry
                ekv_t, ek_t = x
                a = a * decay + ekv_t
                b = b * decay + ek_t
                return ((a, b), (a, b))
            ekv_t = jnp.swapaxes(ekv, 0, 1)
            ek_t = jnp.swapaxes(ek, 0, 1)
            init = (jnp.zeros_like(decay), jnp.zeros_like(decay))
            _, (nf, df) = lax.scan(step, init, (ekv_t, ek_t))
            _, (nb, db) = lax.scan(step, init, (ekv_t, ek_t), reverse=True)
            nf = jnp.swapaxes(nf, 0, 1)
            df = jnp.swapaxes(df, 0, 1)
            nb = jnp.swapaxes(nb, 0, 1)
            db = jnp.swapaxes(db, 0, 1)
            euk = jnp.exp(jnp.minimum(u.astype(jnp.float32)[None, None, :] + kf, 30.0))
            num = nf + nb - ekv + euk * vf
            den = df + db - ek + euk
            base = jax.nn.sigmoid(r.astype(jnp.float32)) * (num / jnp.maximum(den, 1e-08))
            out = base * (0.8 + 0.2 * tf)
            return out.astype(r.dtype)
        key = jax.random.key(seed)
        ks = jax.random.split(key, 6)
        return {'r': jax.random.normal(ks[0], (B, T, C), dtype=jnp.float32), 'k': jax.random.normal(ks[1], (B, T, C), dtype=jnp.float32), 'v': jax.random.normal(ks[2], (B, T, C), dtype=jnp.float32), 'w': jax.random.normal(ks[3], (C,), dtype=jnp.float32), 'u': jax.random.normal(ks[4], (C,), dtype=jnp.float32), 'time_emb': jax.random.normal(ks[5], (B, TD), dtype=jnp.float32)}
    _L1_cond2_all = _L1_cond2_setup()
    _L1_cond2_in = {k: v for k, v in _L1_cond2_all.items() if k in ('w', 'u')}
    del _L1_cond2_all

    def _L1_ffn_setup():
        import jax, jax.numpy as jnp
        import numpy as np
        _FP8_DTYPE = jnp.float8_e4m3fn
        _FP8_MAX = 448.0
        key = jax.random.key(seed)
        k_x, k_w = jax.random.split(key)
        B, S, IN, OUT = (2, 1024, 256, 256)
        x = jax.random.normal(k_x, (B, S, IN), dtype=jnp.float32)
        w_f32 = jax.random.normal(k_w, (OUT, IN), dtype=jnp.float32) * 0.02
        weight = w_f32.astype(_FP8_DTYPE)
        weight_scale = jnp.asarray(1.5, dtype=jnp.float32)
        input_scale = jnp.asarray(0.75, dtype=jnp.bfloat16)
        return {'x': x, 'weight': weight, 'weight_scale': weight_scale, 'input_scale': input_scale}
    _L1_ffn_all = _L1_ffn_setup()
    _L1_ffn_in = {k: v for k, v in _L1_ffn_all.items() if k in ('weight', 'weight_scale', 'input_scale')}
    del _L1_ffn_all
    return {'x': x, 'fside_BxSxS_0': fside_BxSxS_0, 'cond_512': cond_512, 'L0_cond_w': _L0_cond_in['w'], 'L0_cond_u': _L0_cond_in['u'], 'L0_attn_Wq': _L0_attn_in['Wq'], 'L0_attn_Wk': _L0_attn_in['Wk'], 'L0_attn_Wv': _L0_attn_in['Wv'], 'L0_attn_Wo': _L0_attn_in['Wo'], 'L0_cond2_w': _L0_cond2_in['w'], 'L0_cond2_u': _L0_cond2_in['u'], 'L0_ffn_switch_w': _L0_ffn_in['switch_w'], 'L0_ffn_switch_b': _L0_ffn_in['switch_b'], 'L0_ffn_w1': _L0_ffn_in['w1'], 'L0_ffn_b1': _L0_ffn_in['b1'], 'L0_ffn_w2': _L0_ffn_in['w2'], 'L0_ffn_b2': _L0_ffn_in['b2'], 'L0_ffn_w3': _L0_ffn_in['w3'], 'L0_ffn_b3': _L0_ffn_in['b3'], 'L1_cond_w': _L1_cond_in['w'], 'L1_cond_u': _L1_cond_in['u'], 'L1_attn_time_maa_k': _L1_attn_in['time_maa_k'], 'L1_attn_time_maa_v': _L1_attn_in['time_maa_v'], 'L1_attn_time_maa_r': _L1_attn_in['time_maa_r'], 'L1_attn_time_maa_g': _L1_attn_in['time_maa_g'], 'L1_attn_time_decay': _L1_attn_in['time_decay'], 'L1_attn_time_faaaa': _L1_attn_in['time_faaaa'], 'L1_attn_Wr': _L1_attn_in['Wr'], 'L1_attn_Wk': _L1_attn_in['Wk'], 'L1_attn_Wv': _L1_attn_in['Wv'], 'L1_attn_Wg': _L1_attn_in['Wg'], 'L1_attn_Wo': _L1_attn_in['Wo'], 'L1_attn_gamma': _L1_attn_in['gamma'], 'L1_attn_beta': _L1_attn_in['beta'], 'L1_cond2_w': _L1_cond2_in['w'], 'L1_cond2_u': _L1_cond2_in['u'], 'L1_ffn_weight': _L1_ffn_in['weight'], 'L1_ffn_weight_scale': _L1_ffn_in['weight_scale'], 'L1_ffn_input_scale': _L1_ffn_in['input_scale']}

def reference(x, fside_BxSxS_0, cond_512, L0_cond_w, L0_cond_u, L0_attn_Wq, L0_attn_Wk, L0_attn_Wv, L0_attn_Wo, L0_cond2_w, L0_cond2_u, L0_ffn_switch_w, L0_ffn_switch_b, L0_ffn_w1, L0_ffn_b1, L0_ffn_w2, L0_ffn_b2, L0_ffn_w3, L0_ffn_b3, L1_cond_w, L1_cond_u, L1_attn_time_maa_k, L1_attn_time_maa_v, L1_attn_time_maa_r, L1_attn_time_maa_g, L1_attn_time_decay, L1_attn_time_faaaa, L1_attn_Wr, L1_attn_Wk, L1_attn_Wv, L1_attn_Wg, L1_attn_Wo, L1_attn_gamma, L1_attn_beta, L1_cond2_w, L1_cond2_u, L1_ffn_weight, L1_ffn_weight_scale, L1_ffn_input_scale):
    import jax
    import jax.numpy as jnp

    def _L0_cond_ref(r, k, v, w, u, time_emb):
        import jax, jax.numpy as jnp
        from jax import lax
        import numpy as np
        B, T, C, TD = (8, 256, 256, 64)

        def _bi_wkv(r, k, v, w, u, time_emb):
            tf = jax.nn.sigmoid(jnp.sum(time_emb, axis=-1))[:, None, None]
            decay = jnp.exp(-jnp.exp(w.astype(jnp.float32)))[None, :] * (0.5 + 0.5 * tf[:, :, 0])
            kf = k.astype(jnp.float32)
            vf = v.astype(jnp.float32)
            ek = jnp.exp(jnp.minimum(kf, 30.0))
            ekv = ek * vf

            def step(carry, x):
                a, b = carry
                ekv_t, ek_t = x
                a = a * decay + ekv_t
                b = b * decay + ek_t
                return ((a, b), (a, b))
            ekv_t = jnp.swapaxes(ekv, 0, 1)
            ek_t = jnp.swapaxes(ek, 0, 1)
            init = (jnp.zeros_like(decay), jnp.zeros_like(decay))
            _, (nf, df) = lax.scan(step, init, (ekv_t, ek_t))
            _, (nb, db) = lax.scan(step, init, (ekv_t, ek_t), reverse=True)
            nf = jnp.swapaxes(nf, 0, 1)
            df = jnp.swapaxes(df, 0, 1)
            nb = jnp.swapaxes(nb, 0, 1)
            db = jnp.swapaxes(db, 0, 1)
            euk = jnp.exp(jnp.minimum(u.astype(jnp.float32)[None, None, :] + kf, 30.0))
            num = nf + nb - ekv + euk * vf
            den = df + db - ek + euk
            base = jax.nn.sigmoid(r.astype(jnp.float32)) * (num / jnp.maximum(den, 1e-08))
            out = base * (0.8 + 0.2 * tf)
            return out.astype(r.dtype)
        return _bi_wkv(r, k, v, w, u, time_emb)

    def _L0_attn_ref(x, Wq, Wk, Wv, Wo):
        import jax, jax.numpy as jnp
        import numpy as np
        NH = 16
        B, T, D = x.shape
        hd = D // NH
        q = (x @ Wq.T).reshape(B, T, NH, hd).transpose(0, 2, 1, 3)
        k = (x @ Wk.T).reshape(B, T, NH, hd).transpose(0, 2, 1, 3)
        v = (x @ Wv.T).reshape(B, T, NH, hd).transpose(0, 2, 1, 3)
        att = jnp.einsum('bhtd,bhsd->bhts', q, k) / jnp.sqrt(jnp.asarray(hd, x.dtype))
        neg = jnp.finfo(att.dtype).min
        mask = jnp.triu(jnp.full((T, T), neg, dtype=att.dtype), k=1)
        att = att + mask
        w = jax.nn.softmax(att, axis=-1)
        z = jnp.einsum('bhts,bhsd->bhtd', w, v)
        z = z.transpose(0, 2, 1, 3).reshape(B, T, D)
        return z @ Wo.T

    def _L0_cond2_ref(r, k, v, w, u, time_emb):
        import jax, jax.numpy as jnp
        from jax import lax
        import numpy as np
        B, T, C, TD = (8, 256, 256, 64)

        def _bi_wkv(r, k, v, w, u, time_emb):
            tf = jax.nn.sigmoid(jnp.sum(time_emb, axis=-1))[:, None, None]
            decay = jnp.exp(-jnp.exp(w.astype(jnp.float32)))[None, :] * (0.5 + 0.5 * tf[:, :, 0])
            kf = k.astype(jnp.float32)
            vf = v.astype(jnp.float32)
            ek = jnp.exp(jnp.minimum(kf, 30.0))
            ekv = ek * vf

            def step(carry, x):
                a, b = carry
                ekv_t, ek_t = x
                a = a * decay + ekv_t
                b = b * decay + ek_t
                return ((a, b), (a, b))
            ekv_t = jnp.swapaxes(ekv, 0, 1)
            ek_t = jnp.swapaxes(ek, 0, 1)
            init = (jnp.zeros_like(decay), jnp.zeros_like(decay))
            _, (nf, df) = lax.scan(step, init, (ekv_t, ek_t))
            _, (nb, db) = lax.scan(step, init, (ekv_t, ek_t), reverse=True)
            nf = jnp.swapaxes(nf, 0, 1)
            df = jnp.swapaxes(df, 0, 1)
            nb = jnp.swapaxes(nb, 0, 1)
            db = jnp.swapaxes(db, 0, 1)
            euk = jnp.exp(jnp.minimum(u.astype(jnp.float32)[None, None, :] + kf, 30.0))
            num = nf + nb - ekv + euk * vf
            den = df + db - ek + euk
            base = jax.nn.sigmoid(r.astype(jnp.float32)) * (num / jnp.maximum(den, 1e-08))
            out = base * (0.8 + 0.2 * tf)
            return out.astype(r.dtype)
        return _bi_wkv(r, k, v, w, u, time_emb)

    def _L0_ffn_ref(x, switch_w, switch_b, w1, b1, w2, b2, w3, b3):
        import jax, jax.numpy as jnp
        import numpy as np
        B, S, D, E, TOPK, H = (8, 256, 256, 8, 2, 16)
        DH = D // H
        FH = D // H
        ROUTE_LEN = 256
        b, s, d = x.shape
        x0 = x[:, :ROUTE_LEN].reshape(b, -1)
        logits = x0 @ switch_w.T + switch_b
        probs = jax.nn.softmax(logits, axis=-1)
        gate, top_idx = jax.lax.top_k(probs, TOPK)
        xh = x.reshape(b, s, H, DH).transpose(0, 2, 1, 3)
        w1s, b1s = (w1[top_idx], b1[top_idx])
        w2s, b2s = (w2[top_idx], b2[top_idx])
        h = jnp.einsum('bhsd,bkfd->bkhsf', xh, w1s) + b1s[:, :, None, None, :]
        h = jax.nn.gelu(h, approximate=False)
        o = jnp.einsum('bkhsf,bkdf->bkhsd', h, w2s) + b2s[:, :, None, None, :]
        o = (o * gate[:, :, None, None, None]).sum(axis=1)
        o = o.transpose(0, 2, 1, 3).reshape(b, s, d)
        out = x + o
        return out @ w3.T + b3

    def _L1_cond_ref(r, k, v, w, u, time_emb):
        import jax, jax.numpy as jnp
        from jax import lax
        import numpy as np
        B, T, C, TD = (8, 256, 256, 64)

        def _bi_wkv(r, k, v, w, u, time_emb):
            tf = jax.nn.sigmoid(jnp.sum(time_emb, axis=-1))[:, None, None]
            decay = jnp.exp(-jnp.exp(w.astype(jnp.float32)))[None, :] * (0.5 + 0.5 * tf[:, :, 0])
            kf = k.astype(jnp.float32)
            vf = v.astype(jnp.float32)
            ek = jnp.exp(jnp.minimum(kf, 30.0))
            ekv = ek * vf

            def step(carry, x):
                a, b = carry
                ekv_t, ek_t = x
                a = a * decay + ekv_t
                b = b * decay + ek_t
                return ((a, b), (a, b))
            ekv_t = jnp.swapaxes(ekv, 0, 1)
            ek_t = jnp.swapaxes(ek, 0, 1)
            init = (jnp.zeros_like(decay), jnp.zeros_like(decay))
            _, (nf, df) = lax.scan(step, init, (ekv_t, ek_t))
            _, (nb, db) = lax.scan(step, init, (ekv_t, ek_t), reverse=True)
            nf = jnp.swapaxes(nf, 0, 1)
            df = jnp.swapaxes(df, 0, 1)
            nb = jnp.swapaxes(nb, 0, 1)
            db = jnp.swapaxes(db, 0, 1)
            euk = jnp.exp(jnp.minimum(u.astype(jnp.float32)[None, None, :] + kf, 30.0))
            num = nf + nb - ekv + euk * vf
            den = df + db - ek + euk
            base = jax.nn.sigmoid(r.astype(jnp.float32)) * (num / jnp.maximum(den, 1e-08))
            out = base * (0.8 + 0.2 * tf)
            return out.astype(r.dtype)
        return _bi_wkv(r, k, v, w, u, time_emb)

    def _L1_attn_ref(x, time_maa_k, time_maa_v, time_maa_r, time_maa_g, time_decay, time_faaaa, Wr, Wk, Wv, Wg, Wo, gamma, beta):
        import jax, jax.numpy as jnp
        import numpy as np
        B, T, C = (4, 256, 256)
        H = 32
        N = C // H
        N_LAYER = 12
        LAYER_ID = 6
        EPS = 1e-05 * 144
        B, T, C = x.shape
        Hh = time_decay.shape[0]
        Nn = C // Hh
        Q = 32 if T % 32 == 0 else 128 if T % 128 == 0 else T
        nC = T // Q
        xx = jnp.pad(x, ((0, 0), (1, 0), (0, 0)))[:, :T] - x
        xk = x + xx * time_maa_k
        xv = x + xx * time_maa_v
        xr = x + xx * time_maa_r
        xg = x + xx * time_maa_g
        r = (xr @ Wr.T).reshape(B, T, Hh, Nn).transpose(0, 2, 1, 3)
        k = (xk @ Wk.T).reshape(B, T, Hh, Nn).transpose(0, 2, 3, 1)
        v = (xv @ Wv.T).reshape(B, T, Hh, Nn).transpose(0, 2, 1, 3)
        g = jax.nn.silu(xg @ Wg.T)
        w = jnp.exp(-jnp.exp(time_decay))
        u = time_faaaa
        ws = (w ** Q).reshape(1, Hh, 1, 1)
        qa = jnp.arange(Q)
        wk = (w ** (Q - 1 - qa)[None, :]).reshape(1, Hh, 1, Q)
        wb = (w ** qa[None, :]).reshape(1, Hh, Q, 1)
        i = qa[:, None]
        j = qa[None, :]
        pw = w.reshape(Hh, 1, 1) ** jnp.maximum(i - j - 1, 0)[None]
        w_mat = jnp.where(i > j, pw, jnp.where(i == j, u.reshape(Hh, 1, 1), jnp.zeros((), x.dtype))).reshape(1, Hh, Q, Q)
        rr = r.reshape(B, Hh, nC, Q, Nn).transpose(2, 0, 1, 3, 4)
        kk = k.reshape(B, Hh, Nn, nC, Q).transpose(3, 0, 1, 2, 4)
        vv = v.reshape(B, Hh, nC, Q, Nn).transpose(2, 0, 1, 3, 4)

        def step(state, inp):
            rc, kc, vc = inp
            att = rc @ kc * w_mat
            yc = att @ vc + rc @ state * wb
            new_state = ws * state + kc * wk @ vc
            return (new_state, yc)
        state0 = jnp.zeros((B, Hh, Nn, Nn), x.dtype)
        _, ys = jax.lax.scan(step, state0, (rr, kk, vv))
        y = ys.transpose(1, 0, 3, 2, 4).reshape(B, T, Hh, Nn)
        mu = jnp.mean(y, axis=-1, keepdims=True)
        var = jnp.mean(jnp.square(y - mu), axis=-1, keepdims=True)
        yn = ((y - mu) / jnp.sqrt(var + EPS)).reshape(B, T, C) * gamma + beta
        out = yn * g @ Wo.T
        return out

    def _L1_cond2_ref(r, k, v, w, u, time_emb):
        import jax, jax.numpy as jnp
        from jax import lax
        import numpy as np
        B, T, C, TD = (8, 256, 256, 64)

        def _bi_wkv(r, k, v, w, u, time_emb):
            tf = jax.nn.sigmoid(jnp.sum(time_emb, axis=-1))[:, None, None]
            decay = jnp.exp(-jnp.exp(w.astype(jnp.float32)))[None, :] * (0.5 + 0.5 * tf[:, :, 0])
            kf = k.astype(jnp.float32)
            vf = v.astype(jnp.float32)
            ek = jnp.exp(jnp.minimum(kf, 30.0))
            ekv = ek * vf

            def step(carry, x):
                a, b = carry
                ekv_t, ek_t = x
                a = a * decay + ekv_t
                b = b * decay + ek_t
                return ((a, b), (a, b))
            ekv_t = jnp.swapaxes(ekv, 0, 1)
            ek_t = jnp.swapaxes(ek, 0, 1)
            init = (jnp.zeros_like(decay), jnp.zeros_like(decay))
            _, (nf, df) = lax.scan(step, init, (ekv_t, ek_t))
            _, (nb, db) = lax.scan(step, init, (ekv_t, ek_t), reverse=True)
            nf = jnp.swapaxes(nf, 0, 1)
            df = jnp.swapaxes(df, 0, 1)
            nb = jnp.swapaxes(nb, 0, 1)
            db = jnp.swapaxes(db, 0, 1)
            euk = jnp.exp(jnp.minimum(u.astype(jnp.float32)[None, None, :] + kf, 30.0))
            num = nf + nb - ekv + euk * vf
            den = df + db - ek + euk
            base = jax.nn.sigmoid(r.astype(jnp.float32)) * (num / jnp.maximum(den, 1e-08))
            out = base * (0.8 + 0.2 * tf)
            return out.astype(r.dtype)
        return _bi_wkv(r, k, v, w, u, time_emb)

    def _L1_ffn_ref(x, weight, weight_scale, input_scale):
        import jax, jax.numpy as jnp
        import numpy as np
        _FP8_DTYPE = jnp.float8_e4m3fn
        _FP8_MAX = 448.0
        orig_dtype = x.dtype
        w = weight.astype(orig_dtype) * weight_scale.astype(orig_dtype)
        s_f32 = input_scale.astype(jnp.float32)
        x_scaled = x.astype(jnp.float32) / s_f32
        x_fp8 = jnp.clip(x_scaled, -_FP8_MAX, _FP8_MAX).astype(_FP8_DTYPE)
        x_qdq = x_fp8.astype(orig_dtype) * s_f32.astype(orig_dtype)
        return jnp.einsum('bsi,oi->bso', x_qdq, w)
    x = x + _L0_attn_ref(_L0_cond_ref(x, fside_BxSxS_0, fside_BxSxS_0, L0_cond_w, L0_cond_u, cond_512), L0_attn_Wq, L0_attn_Wk, L0_attn_Wv, L0_attn_Wo)
    x = x + _L0_ffn_ref(_L0_cond2_ref(x, fside_BxSxS_0, fside_BxSxS_0, L0_cond2_w, L0_cond2_u, cond_512), L0_ffn_switch_w, L0_ffn_switch_b, L0_ffn_w1, L0_ffn_b1, L0_ffn_w2, L0_ffn_b2, L0_ffn_w3, L0_ffn_b3)
    x = x + _L1_attn_ref(_L1_cond_ref(x, fside_BxSxS_0, fside_BxSxS_0, L1_cond_w, L1_cond_u, cond_512), L1_attn_time_maa_k, L1_attn_time_maa_v, L1_attn_time_maa_r, L1_attn_time_maa_g, L1_attn_time_decay, L1_attn_time_faaaa, L1_attn_Wr, L1_attn_Wk, L1_attn_Wv, L1_attn_Wg, L1_attn_Wo, L1_attn_gamma, L1_attn_beta)
    x = x + _L1_ffn_ref(_L1_cond2_ref(x, fside_BxSxS_0, fside_BxSxS_0, L1_cond2_w, L1_cond2_u, cond_512), L1_ffn_weight, L1_ffn_weight_scale, L1_ffn_input_scale)
    return x

_drawn_inputs = setup_inputs


def setup_inputs(seed=0):
    import zlib

    import numpy as np

    out = dict(_drawn_inputs(seed))
    spreads = {'L0_ffn_switch_b': (0.0, 0.1),
     'L0_ffn_b1': (0.0, 0.8),
     'L0_ffn_b2': (0.0, 0.274),
     'L0_ffn_b3': (0.0, 0.1),
     'L1_attn_gamma': (1.0, 0.6),
     'L1_attn_beta': (0.0, 0.8)}
    factors = {'cond_512': 3.761,
     'L0_cond_w': 11.63,
     'L0_cond_u': 30.752,
     'L0_attn_Wq': 39.833,
     'L0_attn_Wk': 38.816,
     'L0_cond2_u': 2.925,
     'L0_ffn_w1': 8.0,
     'L0_ffn_w2': 8.0,
     'L1_cond_w': 4.016,
     'L1_cond_u': 8.0,
     'L1_attn_time_maa_k': 8.0,
     'L1_attn_time_maa_v': 8.0,
     'L1_attn_time_maa_r': 8.0,
     'L1_attn_time_maa_g': 8.0,
     'L1_attn_time_decay': 31.46,
     'L1_attn_time_faaaa': 8.0,
     'L1_attn_Wr': 3.024,
     'L1_attn_Wk': 3.074,
     'L1_attn_Wv': 2.988,
     'L1_attn_Wg': 3.012,
     'L1_attn_Wo': 3.072,
     'L1_cond2_u': 6.756}
    for name, (base, spread) in spreads.items():
        noise = np.random.default_rng([zlib.crc32(name.encode()), seed]).standard_normal(out[name].shape)
        drawn = base * np.exp(spread * noise) if base else spread * noise
        out[name] = jnp.asarray(drawn.astype(out[name].dtype))
    for name, factor in factors.items():
        out[name] = (out[name] * factor).astype(out[name].dtype)
    return out
```

```python
from contextlib import ExitStack

import numpy as np

import concourse.bass as bass
from concourse import mybir

F32 = mybir.dt.float32
BF16 = mybir.dt.bfloat16
F16 = mybir.dt.float16
FP8 = mybir.dt.float8e4
U8 = mybir.dt.uint8
U16 = mybir.dt.uint16
ALU = mybir.AluOpType
ACT = mybir.ActivationFunctionType
X = mybir.AxisListType.X

P = 128
B, T, C = 4, 256, 256
NB = C // P
TB = T // P
N = NB * T
NEG = -3.0e38

H0, D0 = 16, 16
H1, D1 = 32, 8
EPS1 = 1e-05 * 144
SPLIT_Q = (0, 0, 1, 1, 0, 2)
SPLIT_K = (0, 1, 0, 1, 2, 0)
NPROD = len(SPLIT_Q)
KROWS = 72
SROWS = NPROD * D0
GH = 4
SA = GH * T
SW = SA + GH * P

E, DH = 8, 16
EB = 2 * DH + 2
FP8_MAX, FP8_HALF = 448.0, 224.0

W_COL = {l: 2 * l for l in range(4)}
U_COL = {l: 8 + 2 * l for l in range(4)}
MAA_COL = {"k": 16, "v": 18, "r": 20, "g": 22}
GAMMA_COL, BETA_COL, B3_COL = 24, 26, 28
NVEC = 30
COND_COL, SWB_COL, TD_COL, FA_COL, WS_COL = 0, 256, 264, 296, 328
NROW = 329
CONSTS = {"ident": P, "center": P, "mean8": P, "ones": P, "tri": P, "negd": T, "diagm": 32, "hmask": P,
          "bdm": 8, "rev": E, "eps": 1}
CONST_AT = dict(zip(CONSTS, np.cumsum([0] + list(CONSTS.values())).tolist()))
NCONST = sum(CONSTS.values())
MATS = ["q0", "k0", "v0", "o0", "w3", "r1", "k1", "v1", "g1", "o1"]


def make_steps():
    s = []
    state = {"A": 0, "B": 0, "C": 0}

    def flush():
        if state["C"] < state["B"]:
            s.append(("condC", state["C"]))
            state["C"] += 1

    def cond(n=1):
        for _ in range(n):
            flush()
            if state["A"] < 4 * B:
                s.append(("condA", state["A"]))
                state["A"] += 1
            if state["B"] < state["A"] - 1 or state["A"] == 4 * B > state["B"]:
                s.append(("condB", state["B"]))
                state["B"] += 1

    def add(*steps):
        for step in steps:
            kind, n = step.split()
            s.append((kind, int(n)))

    cond(2)
    flush()
    add("z 0", "qkv 0")
    cond()
    flush()
    add("z 1", "qkv 1")
    cond()
    flush()
    add("z 2", "S 0")
    cond()
    flush()
    add("z 3", "S 1", "mt 0")
    cond()
    add("ST 0", "mt 1", "qkv 2", "post 0")
    cond()
    add("ST 1", "qkv 3")
    cond()
    add("S 2", "post 1", "z 4")
    cond()
    add("S 3", "mt 2", "z 5", "route 0")
    cond()
    add("ST 2", "mt 3", "route 1", "post 2")
    cond()
    add("ST 3")
    cond()
    add("post 3", "z 6", "exp1 0", "route 2", "exp2 0", "exp1 1")
    cond()
    add("z 7", "route 3", "w3 0", "exp2 1", "exp1 2")
    cond()
    add("w3 1", "exp2 2", "exp1 3")
    cond()
    add("w3 2", "exp2 3", "z 8")
    cond()
    add("w3 3")
    cond(3)
    flush()
    add("mix 0", "rk 0", "vg 0", "z 9", "mix 1")
    add(*[f"wmask {g}" for g in range(4)])
    for b in range(B):
        add(f"score {2 * b}")
        if b == 0:
            add(*[f"wmask {g}" for g in range(4, 8)])
        if b < 3:
            add(f"rk {b + 1}")
        add(f"Y {2 * b}", f"score {2 * b + 1}", f"Y {2 * b + 1}")
        add(f"norm {b}")
        if b < 3:
            add(f"vg {b + 1}")
        add(f"out1 {b}")
        if b + 2 < 4:
            add(f"z {8 + b + 2}", f"mix {b + 2}")
        add(f"z {12 + b}", f"fp8 {b}")
    return s


STEPS = make_steps()


def dense_plan():
    uses = {}
    for kind, b in STEPS:
        names = {"qkv": ["q", "k", "v"], "mt": ["t"], "ST": ["av0", "av1", "av2", "av3"], "post": ["t0", "t1", "zT", "o"],
                 "route": ["lg", "lb"], "exp1": ["h0", "h1"], "exp2": ["o"], "w3": ["y"],
                 "rk": ["r", "k"], "vg": ["v", "g"], "Y": ["y"], "norm": ["c", "v"],
                 "out1": ["y"], "fp8": ["y"]}.get(kind, [])
        for n in names:
            uses[(kind, n, b)] = len(uses)
    return uses


def score_plan():
    uses = {}
    for kind, b in STEPS:
        if kind in ("S", "ST", "score"):
            for g in range(4):
                uses[(kind, b, g)] = len(uses)
    return uses


Z_AT = {i: n + 1 for n, i in enumerate(i for kind, i in STEPS if kind == "z")}
DENSE = dense_plan()
SCORE = score_plan()


def build(nc, d):
    with ExitStack() as ctx:
        def sb(name, shape, dt=F32):
            return ctx.enter_context(nc.sbuf_tensor(name, shape, dt))

        def sem(name):
            return ctx.enter_context(nc.semaphore(name))

        x = sb("x", [P, B, NB, T])
        wall = sb("weights", [P, 5, NB * C])
        consts = sb("consts", [P, NCONST])
        cbf = sb("consts_bf16", [P, 3 * P], BF16)
        vecs = sb("vecs", [P, NVEC])
        rows = sb("rows", [P, NROW])
        iscale_bf = sb("iscale_bf", [P, 1], BF16)
        early = sb("early", [P, 2 * 16 * (T + P)])
        mid = sb("mid", [P, H1 * T])

        def part(region, at, pattern, **dims):
            n = dims.pop("n")
            return region[:, at:at + n].rearrange(pattern, **dims)

        fk = part(early, 0, "p (b k t) -> p b k t", n=B * N, b=B, k=NB)
        seq = part(early, 2048, "p (b k m t) -> p b k m t", n=2 * B * N, b=B, k=NB, m=2)
        fwd = [part(early, at, "p (k m t) -> p k m t", n=2 * N, k=NB, m=2) for at in (6144, 11264)]
        bwd = [part(region, at, "p (k m t) -> p k m t", n=2 * N, k=NB, m=2)
               for region, at in ((early, 7168), (mid, 7168))]
        total = part(early, 8192, "p (r k m t) -> p r k m t", n=4 * N, r=2, k=NB, m=2)
        rec = part(early, 10752, "p (k t) -> p k t", n=N, k=NB)
        masked = part(early, 0, "p (r h n) -> p r h n", n=12288, r=2, h=16)
        sw = part(mid, 0, "p (k c e t) -> p k c e t", n=4096, k=NB, c=8, e=E)
        probs = part(mid, 4096, "p (r n) -> p r n", n=2 * SW, r=2)
        gel = part(mid, 4096, "p (w n) -> p w n", n=2 * N, w=2)
        wmask = part(mid, 0, "p (h t) -> p h t", n=H1 * T, h=H1)
        ratio = sb("ratio", [P, 8, NB, T])
        zbuf = sb("zbuf", [P, B, NB, T])
        qst = sb("q_stack", [P, 2, 16, T], BF16)
        kst = sb("k_stack", [P, 2, 16, T], BF16)
        split = sb("split", [P, 2, 3, N], BF16)
        resid = sb("resid", [P, 2, N])
        vbuf = sb("vbuf", [P, 2048])
        vaug = part(vbuf, 0, "p (r s h d) -> p r s h d", n=2048, r=2, s=TB, h=H0)
        vm = part(vbuf, 0, "p (s g e c) -> p s g e c", n=2048, s=TB, g=8, e=GH)
        misc = sb("misc", [P, 3584])
        zaug = part(misc, 0, "p (g t) -> p g t", n=1024, g=4)
        znrm = part(misc, 1024, "p (s c) -> p s c", n=N, s=TB)
        zoT = part(misc, 1536, "p (k t) -> p k t", n=N, k=NB)
        bd = part(misc, 2048, "p (r k w c) -> p r k w c", n=1024, r=2, k=2, w=2)
        mixb = part(misc, 0, "p (m k t) -> p m k t", n=4 * N, m=4, k=NB)
        diff = part(misc, 2048, "p (k t) -> p k t", n=N, k=NB)
        ysb = part(misc, 2560, "p (k t) -> p k t", n=N, k=NB)
        sgate = part(misc, 3072, "p (k t) -> p k t", n=N, k=NB)
        pair = sb("pair", [P, 2 * EB * E])
        esel = part(pair, 0, "p (k c e) -> p k c e", n=2 * EB * E, k=2, e=E)
        lmask = part(pair, 0, "p (e t) -> p e t", n=T, e=E)
        cent = part(pair, 0, "p (k t) -> p k t", n=N, k=NB)
        vsb = sb("vsb", [P, TB, C])
        tmpn = sb("tmpn", [P, 2, N])
        w16 = [tmpn[:, i, 0:N // 2].bitcast(U16) for i in range(2)]
        w8 = tmpn[:, 1, N // 2:N // 2 + N // 4].bitcast(U8)
        expert = sb("expert", [P, E, EB])
        ew = sb("ew", [P, 2, 2, EB])
        small = sb("small", [P, 256])
        mxs = sb("mxs", [P, 2, TB, H0])
        msp = sb("msp", [P, 2, TB, 3, H0], BF16)
        mT = sb("mT", [3 * H0, 2, T], BF16)
        wbf = sb("wbf", [P, NB, C], BF16)
        q8 = sb("q8", [P, 2, N], FP8)
        qbf = sb("qbf", [P, NB, T], BF16)

        dense = [ctx.enter_context(nc.psum_tensor(f"dense{i}", [P, 512], F32)) for i in range(2)]
        score = [ctx.enter_context(nc.psum_tensor(f"score{i}", [P, SW], F32)) for i in range(2)]

        place = {}

        def numbers(name, n):
            at = sum(place.values())
            place[name] = n
            return small[:, at:at + n]

        csum, thc, dfac = (numbers(n, B) for n in ("csum", "thc", "dfac"))
        gain = numbers("gain", B)
        cw = numbers("cw", 2 * 4)
        dw = numbers("dw", 2 * 4)
        dec = numbers("dec", 8 * B).rearrange("p (b w) -> p b w", b=B)
        lam = numbers("lam", H1)
        rscale, rhalf, oscale, iscale = (numbers(n, 1) for n in ("rscale", "rhalf", "oscale", "iscale"))
        gam4, beth = numbers("gam4", NB), numbers("beth", NB)
        lgr, lg, pr, t8, t9 = (numbers(n, E) for n in ("lgr", "lg", "pr", "t8", "t9"))
        s1, s2, s3, nmx = (numbers(n, 1) for n in ("s1", "s2", "s3", "nmx"))
        gt = numbers("gt", 2)
        oh = numbers("oh", 2 * E).rearrange("p (k e) -> p k e", k=2)
        rden = numbers("rden", TB * H0).rearrange("p (s h) -> p s h", s=TB)
        mres = numbers("mres", TB * H0).rearrange("p (s h) -> p s h", s=TB)
        b2s = numbers("b2s", B)

        def mat(name):
            return wall[:, MATS.index(name) % 5, :].rearrange("p (k o) -> p k o", k=NB)

        def const(name):
            return consts[:, CONST_AT[name]:CONST_AT[name] + CONSTS[name]]

        def vec(col, k):
            return vecs[:, col + k:col + k + 1]

        def outer(ap, n):
            return ap.unsqueeze(1).to_broadcast([ap.shape[0], n, ap.shape[1]])

        def inner(ap, n):
            return ap.unsqueeze(2).to_broadcast([ap.shape[0], ap.shape[1], n])

        ident = const("ident")
        identb = cbf[:, 0:P]
        maskb = cbf[:, P:2 * P]
        maskTb = cbf[:, 2 * P:3 * P]

        names = """in_fside in_vecs in_x in_consts in_qkv in_rest in_switch in_later
        clipped csum_done thc_done dw_done ek_raw euk_raw eu_ready scan_done pool_sum tot_ready den_max
        rec_ready ratio_ready tanh_ready z_ready part1 part2 part3 m_split m_in pads_set
        lgr_ready logits_ready exps_done gates_picked bd_ready lam_ready wexp_done wmask_done
        diff_done mix_done vm_ready squared newton_in tanh_g gated scaled8 q8_ready out_in
        vec_step act_step pool_step""".split()
        (in_fside, in_vecs, in_x, in_consts, in_qkv, in_rest, in_switch, in_later,
         clipped, csum_done, thc_done, dw_done, ek_raw, euk_raw, eu_ready, scan_done, pool_sum, tot_ready, den_max,
         rec_ready, ratio_ready, tanh_ready, z_ready, part1, part2, part3, m_split, m_in, pads_set,
         lgr_ready, logits_ready, exps_done, gates_picked, bd_ready, lam_ready, wexp_done, wmask_done,
         diff_done, mix_done, vm_ready, squared, newton_in, tanh_g, gated, scaled8, q8_ready, out_in,
         vec_step, act_step, pool_step) = (sem(n) for n in names)
        stack_in = [sem(f"stack_in{i}") for i in range(2)]
        dense_full = [sem(f"dense_full{i}") for i in range(2)]
        dense_read = [sem(f"dense_read{i}") for i in range(2)]
        score_full = [sem(f"score_full{i}") for i in range(2)]
        score_read = [sem(f"score_read{i}") for i in range(2)]

        def bank(*key):
            return dense[DENSE[key] % 2]

        def bank_free(pe, *key):
            n = DENSE[key]
            if n >= 2:
                pe.wait_ge(dense_read[n % 2], n // 2)

        def bank_full(eng, *key):
            n = DENSE[key]
            eng.wait_ge(dense_full[n % 2], n // 2 + 1)

        def full(*key):
            return dense_full[DENSE[key] % 2]

        def read(*key):
            return dense_read[DENSE[key] % 2]

        def slot_free(pe, *key):
            n = SCORE[key]
            if n >= 2:
                pe.wait_ge(score_read[n % 2], n // 2)

        def slot_full(eng, *key):
            n = SCORE[key]
            eng.wait_ge(score_full[n % 2], n // 2 + 1)

        def bank_done(eng, *key):
            n = DENSE[key]
            eng.wait_ge(dense_read[n % 2], n // 2 + 1)

        def slot_done(eng, *key):
            n = SCORE[key]
            eng.wait_ge(score_read[n % 2], n // 2 + 1)

        def x_ready(eng, i):
            b = i % 4
            if i >= 4:
                bank_done(eng, *[("post", "o", b), ("w3", "y", b), ("out1", "y", b)][i // 4 - 1])

        def stacks_in(eng, kind, b):
            slot = b % 2
            eng.wait_ge(stack_in[slot], 16 * 2 * NPROD * (2 * (b // 2 + 1) if kind == "S" else 4 + b // 2 + 1))

        block = ctx.enter_context(nc.Block())

        @block.sync
        def _(sp):
            sp.dma_start(vecs[:], d["vecs"]).then_inc(in_vecs, 16)
            sp.dma_start(rows[:], d["rows"]).then_inc(in_vecs, 16)
            sp.dma_start(fk[:, 0], d["fside"][:, 0]).then_inc(in_fside, 16)
            sp.dma_start(x[:], d["x"]).then_inc(in_x, 16)
            for b in range(1, B):
                sp.wait_ge(in_fside, 16 * b)
                sp.dma_start(fk[:, b], d["fside"][:, b]).then_inc(in_fside, 16)
            sp.dma_start(wall[:, 0:3], d["weights"][:, 0:3]).then_inc(in_qkv, 16)
            sp.dma_start(cbf[:], d["consts_bf16"]).then_inc(in_consts, 16)
            sp.dma_start(consts[:], d["consts"]).then_inc(in_consts, 16)
            sp.dma_start(wall[:, 3:5], d["weights"][:, 3:5]).then_inc(in_rest, 16)
            sp.dma_start(expert[:], d["expert"]).then_inc(in_rest, 16)
            sp.dma_start(iscale_bf[:], d["iscale"]).then_inc(in_rest, 16)
            sp.dma_start(w8, d["w8"]).then_inc(in_rest, 16)
            sp.dma_start(mid[:, 0:4096], d["switch"]).then_inc(in_switch, 16)

            def stack(which, slot, blk, rows_of, half):
                for r, (dst, parts) in enumerate([(qst, SPLIT_Q), (kst, SPLIT_K)]):
                    sp.wait_ge(part3, which + r + 1)
                    for n, j in enumerate(parts):
                        sp.dma_start(dst[rows_of * n:rows_of * (n + 1), slot, half[0]:half[1], :],
                                     split[:, r, j, blk * T:(blk + 1) * T]).then_inc(stack_in[slot], 16)

            for kind, b in STEPS:
                if kind == "qkv":
                    if b >= 2:
                        slot_full(sp, "ST", b - 2, 3)
                    for blk in range(NB):
                        stack(2 * b, b % 2, blk, D0, (8 * blk, 8 * blk + 8))
                elif kind == "mt":
                    bank_done(sp, "mt", "t", b)
                    sp.dma_start(qst[SROWS:SROWS + 3, b % 2, :, :], mT[:, b % 2, :]).then_inc(m_in, 16)
                elif kind == "rk":
                    for blk in range(NB):
                        if b == 0:
                            slot_full(sp, "ST", 2 + blk, 3)
                            sp.wait_ge(pads_set, 3)
                        else:
                            slot_full(sp, "score", 2 * (b - 1) + blk, 3)
                        stack(8 + 2 * b, blk, blk, D1, (0, 16))
                elif kind == "post" and b == 3:
                    bank_full(sp, "post", "o", 3)
                    sp.dma_start(wall[:, 0:4], d["weights"][:, 5:9]).then_inc(in_later, 16)
                elif kind == "w3" and b == 3:
                    bank_full(sp, "w3", "y", 3)
                    sp.dma_start(wall[:, 4:5], d["weights"][:, 9:10]).then_inc(in_later, 16)
                elif kind == "fp8":
                    bank_done(sp, "fp8", "y", b)
                    sp.dma_start(d["out"][:, b], x[:, b]).then_inc(out_in, 16)
            sp.wait_ge(out_in, 16 * B)

        @block.gpsimd
        def _(pool):
            for kind, i in STEPS:
                b = i
                if kind == "condA":
                    pool.wait_ge(scan_done, i + 1)
                    f = fwd[i % 2]
                    nc.gpsimd.tensor_tensor(f, f, bwd[i % 2], ALU.add).then_inc(pool_sum, 1)
                    pool.wait_ge(pool_sum, i + 1)
                    pool.wait_ge(eu_ready, i + 1)
                    nc.gpsimd.tensor_tensor(total[:, i % 2], total[:, i % 2], f, ALU.add).then_inc(tot_ready, 1)
                elif kind in ("qkv", "rk"):
                    for w in range(2):
                        n = 2 * b + w + (8 if kind == "rk" else 0)
                        pool.wait_ge(part2, n + 1)
                        nc.gpsimd.tensor_tensor(split[:, w, 2], resid[:, w], split[:, w, 1],
                                                ALU.subtract).then_inc(part3, 1)
                elif kind == "route":
                    if b == 0:
                        pool.wait_ge(in_consts, 32)
                    pool.wait_ge(gates_picked, b + 1)
                    if b >= 2:
                        bank_full(pool, "exp2", "o", b - 2)
                    for k in range(2):
                        for w, at in ((0, 0), (1, DH + 1)):
                            last = nc.gpsimd.tensor_tensor(
                                bd[:, b % 2, k, w].rearrange("p (h c) -> p h c", h=8),
                                outer(ew[:, b % 2, k, at:at + DH], 8), inner(const("bdm"), DH), ALU.mult)
                    last.then_inc(bd_ready, 1)
                elif kind == "vg":
                    bank_done(pool, "vg", "v", b)
                    if b >= 1:
                        bank_full(pool, "Y", "y", 2 * b - 1)
                    for s in range(TB):
                        for e in range(GH):
                            last = nc.gpsimd.tensor_tensor(
                                vm[:, s, :, e, :], vsb[:, s].rearrange("p (g c) -> p g c", g=8),
                                outer(const("hmask")[:, 32 * e:32 * e + 32], 8), ALU.mult)
                    last.then_inc(vm_ready, 1)

        @block.scalar
        def _(act):
            steps = [0]

            def link(ins):
                steps[0] += 1
                ins.then_inc(act_step, 1)
                act.wait_ge(act_step, steps[0])

            act.wait_ge(in_x, 16)
            for b in range(B):
                nc.scalar.activation(zbuf[:, b], x[:, b], ACT.Tanh, scale=0.5).then_inc(tanh_ready, 1)
            act.wait_ge(csum_done, 1)
            nc.scalar.activation(thc, csum, ACT.Tanh, scale=0.5).then_inc(thc_done, 1)
            link(nc.scalar.activation(dw, cw, ACT.Exp))
            nc.scalar.activation(dw, dw, ACT.Exp, scale=-1.0).then_inc(dw_done, 1)
            nc.scalar.activation(lam, lam, ACT.Exp).then_inc(dw_done, 1)
            for b in range(B):
                act.wait_ge(clipped, b + 1)
                nc.scalar.activation(seq[:, b, :, 1], seq[:, b, :, 0], ACT.Exp).then_inc(ek_raw, 1)

            def copy_parts(kind, b):
                names = ("q", "k") if kind == "qkv" else ("r", "k")
                for w in range(2):
                    n = 2 * b + w + (8 if kind == "rk" else 0)
                    key = (kind, names[w], b)
                    bank_full(act, *key)
                    before = n // 2
                    if before:
                        for slot in range(2):
                            done = (before + 1 - slot) // 2 * 2 if before <= 4 else 4 + before - 4
                            if done:
                                act.wait_ge(stack_in[slot], 16 * 2 * NPROD * done)
                    nc.scalar.activation(split[:, w, 0], bank(*key)[:, :], ACT.Copy).then_inc(part1, 1)
                for w in range(2):
                    n = 2 * b + w + (8 if kind == "rk" else 0)
                    bank_done(act, kind, names[w], b)
                    nc.scalar.activation(split[:, w, 1], resid[:, w], ACT.Copy).then_inc(part2, 1)

            for kind, i in STEPS:
                b = i
                if kind == "condA":
                    act.wait_ge(clipped, B + i + 1)
                    nc.scalar.activation(total[:, i % 2, :, 1], total[:, i % 2, :, 0], ACT.Exp).then_inc(euk_raw, 1)
                elif kind == "condB":
                    act.wait_ge(den_max, i + 1)
                    if i:
                        act.wait_ge(ratio_ready, i)
                    link(nc.scalar.activation(rec, total[:, i % 2, :, 1], ACT.Ln))
                    nc.scalar.activation(rec, rec, ACT.Exp, scale=-1.0).then_inc(rec_ready, 1)
                elif kind == "z" and i >= B:
                    x_ready(act, i)
                    nc.scalar.activation(zbuf[:, i % B], x[:, i % B], ACT.Tanh, scale=0.5).then_inc(tanh_ready, 1)
                elif kind == "qkv":
                    copy_parts(kind, b)
                    bank_full(act, "qkv", "v", b)
                    if b >= 2:
                        bank_full(act, "ST", "av3", b - 2)
                    nc.scalar.activation(vaug[:, b % 2, :, :, 0:D0],
                                         bank("qkv", "v", b)[:, :].rearrange("p (s h d) -> p s h d", s=TB, h=H0),
                                         ACT.Copy).then_inc(read("qkv", "v", b), 1)
                elif kind == "mt":
                    bank_full(act, "mt", "t", b)
                    if b >= 2:
                        act.wait_ge(m_in, 16 * (b - 1))
                    nc.scalar.activation(mT[:, b % 2, :], bank("mt", "t", b)[0:48, 0:128].bitcast(BF16),
                                         ACT.Copy).then_inc(read("mt", "t", b), 1)
                elif kind == "ST":
                    for g in range(5):
                        if g < 4:
                            n = SCORE["ST", b, g]
                            slot_full(act, "ST", b, g)
                            if 4 * b + g >= 2:
                                q = 4 * b + g - 2
                                bank_full(act, "ST", f"av{q % 4}", q // 4)
                            nc.scalar.activation(probs[:, g % 2], score[n % 2][:, :], ACT.Exp,
                                                 scale=D0 ** -0.5).then_inc(score_read[n % 2], 1)
                        if g >= 1:
                            key = ("ST", f"av{g - 1}", b)
                            bank_full(act, *key)
                            if b >= 1 and g == 1:
                                bank_full(act, "post", "t1", b - 1)
                            nc.scalar.activation(zaug[:, g - 1], bank(*key)[:, 0:T],
                                                 ACT.Copy).then_inc(read(*key), 1)
                elif kind == "post":
                    bank_full(act, "post", "zT", b)
                    if b >= 1:
                        bank_full(act, "post", "o", b - 1)
                    nc.scalar.activation(zoT, bank("post", "zT", b)[:, :].rearrange("p (k t) -> p k t", k=NB),
                                         ACT.Copy).then_inc(read("post", "zT", b), 1)
                elif kind == "route":
                    act.wait_ge(logits_ready, b + 1)
                    nc.scalar.activation(pr, lg, ACT.Exp, bias=nmx).then_inc(exps_done, 1)
                elif kind == "exp1":
                    for k in range(2):
                        key = ("exp1", f"h{k}", b)
                        bank_full(act, *key)
                        if k == 0 and b >= 1:
                            bank_full(act, "exp2", "o", b - 1)
                        if k == 0 and b == 0:
                            bank_full(act, "ST", "av3", 3)
                        nc.scalar.activation(gel[:, k], bank(*key)[:, :], ACT.Gelu,
                                             bias=ew[:, b % 2, k, DH:DH + 1]).then_inc(read(*key), 1)
                elif kind == "wmask":
                    if i == 0:
                        act.wait_ge(lam_ready, 1)
                        act.wait_ge(in_consts, 32)
                        act.wait_ge(tot_ready, 4 * B)
                        bank_full(act, "route", "lg", 3)
                        bank_full(act, "exp2", "o", 3)
                    for h in range(GH * i, GH * i + GH):
                        last = nc.scalar.activation(wmask[:, h], const("negd"), ACT.Exp, scale=lam[:, h:h + 1])
                    last.then_inc(wexp_done, 1)
                elif kind == "rk":
                    copy_parts(kind, b)
                elif kind == "vg":
                    bank_full(act, "vg", "v", b)
                    if b >= 1:
                        act.wait_ge(vm_ready, b)
                    nc.scalar.activation(vsb[:, :, :], bank("vg", "v", b)[:, :].rearrange("p (s c) -> p s c", s=TB),
                                         ACT.Copy).then_inc(read("vg", "v", b), 1)
                    bank_full(act, "vg", "g", b)
                    if b >= 1:
                        act.wait_ge(gated, b)
                    nc.scalar.activation(sgate, bank("vg", "g", b)[:, :].rearrange("p (k t) -> p k t", k=NB),
                                         ACT.Tanh, scale=0.5).then_inc(tanh_g, 1)
                elif kind == "Y":
                    bank_full(act, "Y", "y", i)
                    if i >= 2 and i % 2 == 0:
                        bank_full(act, "norm", "c", i // 2 - 1)
                    nc.scalar.activation(ysb[:, i % 2], bank("Y", "y", i)[:, 0:T], ACT.Copy)\
                        .then_inc(read("Y", "y", i), 1)
                elif kind == "norm":
                    bank_full(act, "norm", "c", b)
                    if b >= 1:
                        act.wait_ge(q8_ready, b)
                        bank_full(act, "out1", "y", b - 1)
                    c = bank("norm", "c", b)
                    nc.scalar.activation(tmpn[:, 0], c[:, :], ACT.Square).then_inc(squared, 1)
                    nc.scalar.activation(cent, c[:, :].rearrange("p (k t) -> p k t", k=NB),
                                         ACT.Copy).then_inc(read("norm", "c", b), 1)
                    bank_full(act, "norm", "v", b)
                    link(nc.scalar.activation(tmpn[:, 1], bank("norm", "v", b)[:, :], ACT.Ln, bias=const("eps")))
                    nc.scalar.activation(tmpn[:, 1], tmpn[:, 1], ACT.Exp, scale=-0.5).then_inc(newton_in, 1)
                elif kind == "fp8":
                    act.wait_ge(z_ready, Z_AT[3 * B + b])
                    z = zbuf[:, b].rearrange("p k t -> p (k t)")
                    nc.scalar.activation(tmpn[:, 0], z, ACT.Copy, scale=rscale)
                    nc.scalar.activation(tmpn[:, 1], z, ACT.Copy, scale=rhalf).then_inc(scaled8, 1)

        @block.tensor
        def _(pe):
            def project(out, w, src, k_outer=False):
                for o in range(NB):
                    for k in range(NB):
                        last = nc.tensor.matmul(out[:, o * T:(o + 1) * T], w[:, k, o * P:(o + 1) * P], src[:, k],
                                                start=(k == 0), stop=(k == NB - 1))
                return last

            def project_t(out, w, src):
                for s in range(TB):
                    for k in range(NB):
                        last = nc.tensor.matmul(out[:, s * C:(s + 1) * C], src[:, k, s * P:(s + 1) * P], w[:, k],
                                                start=(k == 0), stop=(k == NB - 1))
                return last

            def transposed_scores(out, kk, qq, mask):
                last = None
                for (o, w), (ks, qs) in zip(out, (((0, P), (0, T)), ((P, T), (P, T)))):
                    last = nc.tensor.matmul(o, kk[:, ks[0]:ks[1]], qq[:, qs[0]:qs[1]], start=True, stop=not mask)
                    if mask:
                        last = nc.tensor.matmul(w, identb, maskTb, start=False, stop=True)
                return last

            for kind, i in STEPS:
                b = i
                if kind == "qkv":
                    pe.wait_ge(z_ready, Z_AT[b])
                    if b == 0:
                        pe.wait_ge(in_qkv, 16)
                    for n in ("q", "k"):
                        bank_free(pe, "qkv", n, b)
                        project(bank("qkv", n, b), mat(n + "0"), zbuf[:, b]).then_inc(full("qkv", n, b), 1)
                    bank_free(pe, "qkv", "v", b)
                    project_t(bank("qkv", "v", b), mat("v0"), zbuf[:, b]).then_inc(full("qkv", "v", b), 1)
                elif kind == "S":
                    stacks_in(pe, "S", b)
                    if b == 0:
                        pe.wait_ge(in_consts, 32)
                    for g in range(4):
                        slot_free(pe, "S", b, g)
                        n = SCORE["S", b, g]
                        out = score[n % 2]
                        for h in range(GH):
                            q, k = (st[0:SROWS, b % 2, GH * g + h] for st in (qst, kst))
                            for at, t0, w in ((h * T, P, T), (SA + h * P, 0, P)):
                                nc.tensor.matmul(out[:, at:at + w], q[:, t0:t0 + P], k[:, 0:w],
                                                 start=True, stop=False)
                                last = nc.tensor.matmul(out[:, at + w - P:at + w], identb, maskb,
                                                        start=False, stop=True)
                        last.then_inc(score_full[n % 2], 1)
                elif kind == "mt":
                    pe.wait_ge(m_split, b + 1)
                    bank_free(pe, "mt", "t", b)
                    out = bank("mt", "t", b)[0:48, 0:128].bitcast(BF16)
                    for s in range(TB):
                        last = nc.tensor.transpose(out[:, s * P:(s + 1) * P],
                                                   msp[:, b % 2, s].rearrange("p j h -> p (j h)"), identb)
                    last.then_inc(full("mt", "t", b), 1)
                elif kind == "ST":
                    pe.wait_ge(m_in, 16 * (b + 1))
                    pe.wait_ge(pads_set, 2)
                    for g in range(5):
                        if g < 4:
                            slot_free(pe, "ST", b, g)
                            n = SCORE["ST", b, g]
                            out = score[n % 2]
                            for h in range(GH):
                                q, k = (st[0:SROWS + 3, b % 2, GH * g + h] for st in (qst, kst))
                                last = transposed_scores(
                                    [(out[:, h * T:(h + 1) * T], out[:, h * T:h * T + P]),
                                     (out[:, SA + h * P:SA + (h + 1) * P],) * 2], k, q, True)
                            last.then_inc(score_full[n % 2], 1)
                        if g >= 1:
                            gg = g - 1
                            if gg == 0:
                                bank_done(pe, "qkv", "v", b)
                            slot_done(pe, "ST", b, gg)
                            key = ("ST", f"av{gg}", b)
                            bank_free(pe, *key)
                            for s in range(TB):
                                for h in range(GH):
                                    src = (probs[:, gg % 2, h * T:(h + 1) * T] if s == 0 else
                                           probs[:, gg % 2, SA + h * P:SA + (h + 1) * P])
                                    last = nc.tensor.matmul(
                                        bank(*key)[32 * h:32 * h + 32, s * P:T], vaug[:, b % 2, s, GH * gg + h],
                                        src, start=(s == 0), stop=(s == TB - 1), tile_position=(0, 32 * h))
                            last.then_inc(full(*key), 1)
                elif kind == "post":
                    for s in range(TB):
                        if s == 0:
                            bank_done(pe, "ST", "av3", b)
                        key = ("post", f"t{s}", b)
                        bank_free(pe, *key)
                        for g in range(4):
                            last = nc.tensor.transpose(bank(*key)[:, g * P:(g + 1) * P],
                                                       zaug[:, g, s * P:(s + 1) * P], ident)
                        last.then_inc(full(*key), 1)
                    bank_done(pe, "post", "t1", b)
                    bank_done(pe, "post", "t0", b)
                    bank_free(pe, "post", "zT", b)
                    for k in range(NB):
                        for s in range(TB):
                            last = nc.tensor.transpose(
                                bank("post", "zT", b)[:, k * T + s * P:k * T + (s + 1) * P],
                                znrm[:, s, k * P:(k + 1) * P], ident)
                    last.then_inc(full("post", "zT", b), 1)
                    if b == 0:
                        pe.wait_ge(in_rest, 64)
                    bank_done(pe, "post", "zT", b)
                    bank_free(pe, "post", "o", b)
                    project(bank("post", "o", b), mat("o0"), zoT).then_inc(full("post", "o", b), 1)
                elif kind == "route":
                    pe.wait_ge(z_ready, Z_AT[B + b])
                    if b == 0:
                        pe.wait_ge(in_switch, 16)
                    bank_free(pe, "route", "lg", b)
                    out = bank("route", "lg", b)
                    for r in range(2):
                        for k in range(NB):
                            for j in range(4):
                                c = 4 * r + j
                                last = nc.tensor.matmul(
                                    out[32 * j:32 * j + 32, 0:T], zbuf[:, b, k, 32 * c:32 * c + 32],
                                    sw[:, k, c].rearrange("p e t -> p (e t)"),
                                    start=(r == 0 and k == 0), stop=(r == 1 and k == 1),
                                    tile_position=(0, 32 * j))
                    last.then_inc(full("route", "lg", b), 1)
                    pe.wait_ge(lgr_ready, b + 1)
                    bank_free(pe, "route", "lb", b)
                    nc.tensor.matmul(bank("route", "lb", b)[:, 0:E], const("ones"), lgr, start=True, stop=True)\
                        .then_inc(full("route", "lb", b), 1)
                elif kind == "exp1":
                    pe.wait_ge(bd_ready, b + 1)
                    for k in range(2):
                        key = ("exp1", f"h{k}", b)
                        bank_free(pe, *key)
                        nc.tensor.matmul(bank(*key)[:, :], bd[:, b % 2, k, 0], zbuf[:, b].rearrange("p k t -> p (k t)"),
                                         start=True, stop=True).then_inc(full(*key), 1)
                elif kind == "exp2":
                    bank_free(pe, "exp2", "o", b)
                    for k in range(2):
                        bank_done(pe, "exp1", f"h{k}", b)
                        last = nc.tensor.matmul(bank("exp2", "o", b)[:, :], bd[:, b % 2, k, 1], gel[:, k],
                                                start=(k == 0), stop=(k == 1))
                    last.then_inc(full("exp2", "o", b), 1)
                elif kind == "w3":
                    bank_done(pe, "exp2", "o", b)
                    bank_free(pe, "w3", "y", b)
                    project(bank("w3", "y", b), mat("w3"), zbuf[:, b]).then_inc(full("w3", "y", b), 1)
                elif kind == "rk":
                    pe.wait_ge(mix_done, b + 1)
                    if b == 0:
                        pe.wait_ge(in_later, 32)
                    for m, n in enumerate(("r", "k")):
                        bank_free(pe, "rk", n, b)
                        project(bank("rk", n, b), mat(n + "1"), mixb[:, m]).then_inc(full("rk", n, b), 1)
                elif kind == "vg":
                    bank_free(pe, "vg", "v", b)
                    project_t(bank("vg", "v", b), mat("v1"), mixb[:, 2]).then_inc(full("vg", "v", b), 1)
                    bank_free(pe, "vg", "g", b)
                    project(bank("vg", "g", b), mat("g1"), mixb[:, 3]).then_inc(full("vg", "g", b), 1)
                elif kind == "score":
                    stacks_in(pe, "score", i)
                    for g in range(4):
                        slot_free(pe, "score", i, g)
                        n = SCORE["score", i, g]
                        out = score[n % 2]
                        for h in range(GH):
                            q, k = (st[0:KROWS, i % 2, GH * g + h] for st in (qst, kst))
                            last = transposed_scores(
                                [(out[:, h * T:(h + 1) * T], None),
                                 (out[:, SA + h * P:SA + (h + 1) * P], None)], k, q, False)
                        last.then_inc(score_full[n % 2], 1)
                elif kind == "Y":
                    slot_done(pe, "score", i, 3)
                    slot_done(pe, "score", i, 2)
                    if i % 2 == 0:
                        pe.wait_ge(vm_ready, i // 2 + 1)
                    bank_free(pe, "Y", "y", i)
                    out = bank("Y", "y", i)
                    for e in range(GH):
                        for s in range(TB):
                            for g in range(4):
                                last = nc.tensor.matmul(
                                    out[32 * g:32 * g + 32, s * P:T], vm[:, s, 4 * (i % 2) + g, e],
                                    masked[:, i % 2, GH * g + e, s * T:s * T + (T if s == 0 else P)],
                                    start=(e == 0 and s == 0), stop=(e == GH - 1 and s == TB - 1),
                                    tile_position=(0, 32 * g))
                    last.then_inc(full("Y", "y", i), 1)
                elif kind == "norm":
                    for u in (2 * b, 2 * b + 1):
                        bank_done(pe, "Y", "y", u)
                    bank_free(pe, "norm", "c", b)
                    nc.tensor.matmul(bank("norm", "c", b)[:, :], const("center"), ysb.rearrange("p k t -> p (k t)"),
                                     start=True, stop=True).then_inc(full("norm", "c", b), 1)
                    pe.wait_ge(squared, b + 1)
                    bank_free(pe, "norm", "v", b)
                    nc.tensor.matmul(bank("norm", "v", b)[:, :], const("mean8"), tmpn[:, 0],
                                     start=True, stop=True).then_inc(full("norm", "v", b), 1)
                elif kind == "out1":
                    pe.wait_ge(gated, b + 1)
                    bank_free(pe, "out1", "y", b)
                    project(bank("out1", "y", b), mat("o1"), cent).then_inc(full("out1", "y", b), 1)
                elif kind == "fp8":
                    pe.wait_ge(q8_ready, b + 1)
                    bank_free(pe, "fp8", "y", b)
                    project(bank("fp8", "y", b), wbf, qbf).then_inc(full("fp8", "y", b), 1)

        @block.vector
        def _(dve):
            steps = [0]

            def link(ins):
                steps[0] += 1
                ins.then_inc(vec_step, 1)
                dve.wait_ge(vec_step, steps[0])

            V = nc.vector
            V.memset(kst[SROWS:SROWS + 3, :, :, :], 1.0).then_inc(pads_set, 1)
            V.memset(vaug[:, :, :, :, D0:2 * D0], 1.0).then_inc(pads_set, 1)
            for r in range(2):
                V.memset(bwd[r][:, :, :, T - 1:T], 0.0)
            dve.wait_ge(in_vecs, 32)
            V.tensor_scalar(cw, vecs[:, 0:8], 80.0, None, ALU.min)
            V.tensor_scalar(lam, rows[:, TD_COL:TD_COL + H1], 80.0, None, ALU.min)
            for b in range(B):
                dve.wait_ge(in_fside, 16 * (b + 1))
                V.tensor_scalar(seq[:, b, :, 0], fk[:, b], 30.0, None, ALU.min).then_inc(clipped, 1)
            V.reduce_sum(csum, rows[:, 0:256].rearrange("p (b c) -> p b c", b=B), axis=X).then_inc(csum_done, 1)
            dve.wait_ge(thc_done, 1)
            V.tensor_scalar(gain, thc, -0.05, -0.45, ALU.mult, ALU.add)
            link(V.tensor_scalar(dfac, thc, 0.25, 0.75, ALU.mult, ALU.add))
            dve.wait_ge(dw_done, 2)
            for b in range(B):
                V.tensor_scalar(dec[:, b], dw, dfac[:, b:b + 1], None, ALU.mult)
            link(V.tensor_scalar(lam, lam, 1e30, None, ALU.min))
            for b in range(B):
                dve.wait_ge(ek_raw, b + 1)
                link(V.tensor_tensor(seq[:, b, :, 0], seq[:, b, :, 1], fk[:, b], ALU.mult))

            def setup_rest():
                dve.wait_ge(in_rest, 64)
                link(V.tensor_copy(w16[0], w8))
                link(V.tensor_scalar(w16[1], w16[0], 0x80, 8, ALU.bitwise_and, ALU.logical_shift_left))
                link(V.tensor_scalar(w16[0], w16[0], 0x7F, 7, ALU.bitwise_and, ALU.logical_shift_left))
                link(V.tensor_tensor(w16[0], w16[0], w16[1], ALU.bitwise_or))
                V.tensor_scalar(wbf[:, :, :].rearrange("p k o -> p (k o)"), w16[0].bitcast(F16), 256.0, None, ALU.mult)
                link(V.tensor_copy(iscale, iscale_bf[:, 0:1]))
                V.tensor_scalar(oscale, iscale, rows[:, WS_COL:WS_COL + 1], None, ALU.mult)
                V.tensor_scalar(gam4, vecs[:, GAMMA_COL:GAMMA_COL + 2], -0.25, None, ALU.mult)
                V.tensor_scalar(beth, vecs[:, BETA_COL:BETA_COL + 2], 0.5, None, ALU.mult)
                link(V.reciprocal(rscale, iscale))
                V.tensor_scalar(rhalf, rscale, 0.5, None, ALU.mult).then_inc(lam_ready, 1)

            def rest(kind, b):
                names = ("q", "k") if kind == "qkv" else ("r", "k")
                for w in range(2):
                    n = 2 * b + w + (8 if kind == "rk" else 0)
                    dve.wait_ge(part1, n + 1)
                    if n >= 2:
                        dve.wait_ge(part3, n - 1)
                    key = (kind, names[w], b)
                    V.tensor_tensor(resid[:, w], bank(*key)[:, :], split[:, w, 0],
                                    ALU.subtract).then_inc(read(*key), 1)

            for kind, i in STEPS:
                b = i
                if kind == "condA":
                    l, b = divmod(i, B)
                    if i == 5:
                        setup_rest()
                    if i >= 2:
                        dve.wait_ge(tot_ready, i - 1)
                        dve.wait_ge(ratio_ready, i - 1)
                    for k in range(NB):
                        last = V.tensor_scalar(total[:, i % 2, k, 0], fk[:, b, k], vec(U_COL[l], k), 30.0,
                                               ALU.add, ALU.min)
                    last.then_inc(clipped, 1)
                    f, w = fwd[i % 2], bwd[i % 2]
                    for k in range(NB):
                        decay = dec[:, b, 2 * l + k:2 * l + k + 1]
                        for m in range(2):
                            V.tensor_tensor_scan(f[:, k, m], decay.to_broadcast([P, T]), seq[:, b, k, m],
                                                 0.0, ALU.mult, ALU.add)
                            last = V.tensor_tensor_scan(w[:, k, m, 0:T - 1][:, ::-1], seq[:, b, k, m, 1:T][:, ::-1],
                                                        decay.to_broadcast([P, T - 1]), 0.0, ALU.add, ALU.mult)
                    last.then_inc(scan_done, 1)
                    dve.wait_ge(euk_raw, i + 1)
                    V.tensor_tensor(total[:, i % 2, :, 0], total[:, i % 2, :, 1], fk[:, b], ALU.mult).then_inc(eu_ready, 1)
                elif kind == "condB":
                    dve.wait_ge(tot_ready, i + 1)
                    V.tensor_scalar(total[:, i % 2, :, 1], total[:, i % 2, :, 1], 1e-8, None,
                                    ALU.max).then_inc(den_max, 1)
                elif kind == "condC":
                    dve.wait_ge(rec_ready, i + 1)
                    num, den = total[:, i % 2, :, 0], total[:, i % 2, :, 1]
                    V.scalar_tensor_tensor(num, num, gain[:, i % B:i % B + 1], rec, ALU.mult, ALU.mult)
                    link(V.tensor_tensor(den, den, rec, ALU.mult))
                    V.scalar_tensor_tensor(ratio[:, i % 8], den, 2.0, num, ALU.subtract,
                                           ALU.mult).then_inc(ratio_ready, 1)
                elif kind == "z":
                    dve.wait_ge(tanh_ready, Z_AT[i])
                    dve.wait_ge(ratio_ready, i + 1)
                    z = zbuf[:, i % B]
                    V.scalar_tensor_tensor(z, z, 1.0, ratio[:, i % 8], ALU.add, ALU.mult).then_inc(z_ready, 1)
                elif kind == "qkv":
                    rest(kind, b)
                elif kind == "S":
                    r = b % 2
                    for g in range(4):
                        n = SCORE["S", b, g]
                        slot_full(dve, "S", b, g)
                        src = score[n % 2]
                        V.reduce_max(mxs[:, r, 1, GH * g:GH * g + GH],
                                     src[:, 0:SA].rearrange("p (h t) -> p h t", h=GH), axis=X)
                        V.reduce_max(mxs[:, r, 0, GH * g:GH * g + GH],
                                     src[:, SA:SW].rearrange("p (h t) -> p h t", h=GH),
                                     axis=X).then_inc(score_read[n % 2], 1)
                    slot_done(dve, "S", b, 3)
                    slot_done(dve, "S", b, 2)
                    if b >= 2:
                        bank_full(dve, "mt", "t", b - 2)
                    m = [msp[:, r, :, j] for j in range(3)]
                    link(V.tensor_scalar(m[0], mxs[:, r], -1.0, None, ALU.mult))
                    link(V.scalar_tensor_tensor(mres, mxs[:, r], -1.0, m[0], ALU.mult, ALU.subtract))
                    link(V.tensor_copy(m[1], mres))
                    V.tensor_tensor(m[2], mres, m[1], ALU.subtract).then_inc(m_split, 1)
                elif kind == "post":
                    for s in range(TB):
                        key = ("post", f"t{s}", b)
                        bank_full(dve, *key)
                        if s == 0 and b >= 1:
                            bank_full(dve, "post", "zT", b - 1)
                        src = bank(*key)[:, :].rearrange("p (h d) -> p h d", h=H0)
                        link(V.reciprocal(rden[:, s], src[:, :, D0]))
                        V.tensor_tensor(znrm[:, s].rearrange("p (h d) -> p h d", h=H0), src[:, :, 0:D0],
                                        inner(rden[:, s], D0), ALU.mult).then_inc(read(*key), 1)
                    key = ("post", "o", b)
                    bank_full(dve, *key)
                    V.tensor_tensor(x[:, b], x[:, b], bank(*key)[:, :].rearrange("p (k t) -> p k t", k=NB),
                                    ALU.add).then_inc(read(*key), 1)
                elif kind == "route":
                    key = ("route", "lg", b)
                    if b == 0:
                        dve.wait_ge(in_consts, 32)
                    bank_full(dve, *key)
                    V.tensor_tensor(lmask, bank(*key)[:, 0:T].rearrange("p (e t) -> p e t", e=E),
                                    outer(const("diagm"), E), ALU.mult).then_inc(read(*key), 1)
                    bank_done(dve, *key)
                    V.reduce_sum(lgr, lmask, axis=X).then_inc(lgr_ready, 1)
                    key = ("route", "lb", b)
                    bank_full(dve, *key)
                    V.tensor_tensor(lg, bank(*key)[:, 0:E], rows[:, SWB_COL:SWB_COL + E],
                                    ALU.add).then_inc(read(*key), 1)
                    bank_done(dve, *key)
                    link(V.reduce_max(s1, lg, axis=X))
                    V.tensor_scalar(nmx, s1, -1.0, None, ALU.mult).then_inc(logits_ready, 1)
                    dve.wait_ge(exps_done, b + 1)
                    link(V.reduce_sum(s2, pr, axis=X))
                    link(V.reciprocal(s3, s2))
                    link(V.tensor_scalar(pr, pr, s3, None, ALU.mult))
                    p = pr
                    for k in range(2):
                        link(V.reduce_max(gt[:, k:k + 1], p, axis=X))
                        link(V.scalar_tensor_tensor(t8, p, gt[:, k:k + 1], const("rev"), ALU.is_equal, ALU.mult))
                        link(V.reduce_max(s1, t8, axis=X))
                        link(V.tensor_scalar(oh[:, k], t8, s1, None, ALU.is_equal))
                        if k == 0:
                            link(V.scalar_tensor_tensor(t9, oh[:, 0], -2.0, pr, ALU.mult, ALU.add))
                            p = t9
                    for k in range(2):
                        last = V.tensor_tensor(esel[:, k], expert[:, :, :].rearrange("p e c -> p c e"),
                                               outer(oh[:, k], EB), ALU.mult)
                    link(last)
                    if b >= 2:
                        bank_done(dve, "exp1", "h1", b - 2)
                        dve.wait_ge(bd_ready, b - 1)
                    link(V.reduce_sum(ew[:, b % 2].rearrange("p k c -> p (k c)"),
                                      esel.rearrange("p k c e -> p (k c) e"), axis=X))
                    for k in range(2):
                        half = ew[:, b % 2, k, DH + 1:EB]
                        last = V.tensor_scalar(half, half, gt[:, k:k + 1], None, ALU.mult)
                    last.then_inc(gates_picked, 1)
                    dve.wait_ge(gates_picked, b + 1)
                    link(V.tensor_tensor(b2s[:, b:b + 1], ew[:, b % 2, 0, EB - 1:EB], ew[:, b % 2, 1, EB - 1:EB],
                                         ALU.add))
                elif kind == "exp2":
                    key = ("exp2", "o", b)
                    bank_full(dve, *key)
                    z = zbuf[:, b]
                    V.scalar_tensor_tensor(z, bank(*key)[:, :].rearrange("p (k t) -> p k t", k=NB), b2s[:, b:b + 1], z,
                                           ALU.add, ALU.add).then_inc(read(*key), 1)
                elif kind == "w3":
                    key = ("w3", "y", b)
                    bank_full(dve, *key)
                    for k in range(NB):
                        last = V.scalar_tensor_tensor(x[:, b, k], bank(*key)[:, k * T:(k + 1) * T], vec(B3_COL, k),
                                                      x[:, b, k], ALU.add, ALU.add)
                    last.then_inc(read(*key), 1)
                    if b == 3:
                        for u in range(2):
                            slot_full(dve, "ST", 2 + u, 3)
                        for p in (32, 64):
                            last = V.memset(kst[p:p + 32, :, :, :].rearrange("p r h t -> p (r h t)").bitcast(F32), 0.0)
                        last.then_inc(pads_set, 1)
                elif kind == "mix":
                    z = zbuf[:, b]
                    dve.wait_ge(z_ready, Z_AT[2 * B + b])
                    V.tensor_tensor(diff[:, :, 1:T], z[:, :, 0:T - 1], z[:, :, 1:T], ALU.subtract)
                    if b:
                        bank_full(dve, "vg", "g", b - 1)
                    link(V.tensor_scalar(diff[:, :, 0:1], z[:, :, 0:1], -1.0, None, ALU.mult))
                    for m, name in enumerate(("r", "k", "v", "g")):
                        for k in range(NB):
                            last = V.scalar_tensor_tensor(mixb[:, m, k], diff[:, k], vec(MAA_COL[name], k), z[:, k],
                                                          ALU.mult, ALU.add)
                    last.then_inc(mix_done, 1)
                elif kind == "rk":
                    rest(kind, b)
                elif kind == "vg":
                    key = ("vg", "g", b)
                    dve.wait_ge(tanh_g, b + 1)
                    V.scalar_tensor_tensor(sgate, sgate, 1.0, bank(*key)[:, :].rearrange("p (k t) -> p k t", k=NB),
                                           ALU.add, ALU.mult).then_inc(read(*key), 1)
                elif kind == "wmask":
                    dve.wait_ge(wexp_done, i + 1)
                    w = wmask[:, GH * i:GH * i + GH, 0:P]
                    link(V.tensor_tensor(w, w, outer(const("tri"), GH), ALU.mult))
                    for h in range(GH):
                        last = V.scalar_tensor_tensor(w[:, h], ident, rows[:, FA_COL + GH * i + h:FA_COL + GH * i + h + 1],
                                                      w[:, h], ALU.mult, ALU.add)
                    last.then_inc(wmask_done, 1)
                elif kind == "score":
                    for g in range(4):
                        slot_full(dve, "score", i, g)
                        n = SCORE["score", i, g]
                        if i < 2:
                            dve.wait_ge(wmask_done, 4 * i + g + 1)
                        if i >= 2 and g == 0:
                            bank_full(dve, "Y", "y", i - 2)
                        src, dst = score[n % 2], masked[:, i % 2, GH * g:GH * g + GH]
                        w = wmask[:, 16 * (i % 2) + GH * g:16 * (i % 2) + GH * g + GH]
                        V.tensor_tensor(dst[:, :, 0:T], src[:, 0:SA].rearrange("p (h t) -> p h t", h=GH), w, ALU.mult)
                        V.tensor_tensor(dst[:, :, T:T + P], src[:, SA:SW].rearrange("p (h t) -> p h t", h=GH),
                                        w[:, :, 0:P], ALU.mult).then_inc(score_read[n % 2], 1)
                elif kind == "norm":
                    dve.wait_ge(newton_in, b + 1)
                    sq, r = tmpn[:, 0], tmpn[:, 1]
                    link(V.tensor_tensor(sq, r, r, ALU.mult))
                    key = ("norm", "v", b)
                    V.scalar_tensor_tensor(sq, bank(*key)[:, :], EPS1, sq, ALU.add, ALU.mult).then_inc(read(*key), 1)
                    bank_done(dve, *key)
                    link(V.scalar_tensor_tensor(r, sq, 3.0, r, ALU.subtract, ALU.mult))
                    for k in range(NB):
                        last = V.scalar_tensor_tensor(cent[:, k], cent[:, k], gam4[:, k:k + 1],
                                                      tmpn[:, 1, k * T:(k + 1) * T], ALU.mult, ALU.mult)
                    link(last)
                    for k in range(NB):
                        last = V.scalar_tensor_tensor(cent[:, k], cent[:, k], beth[:, k:k + 1], sgate[:, k],
                                                      ALU.add, ALU.mult)
                    last.then_inc(gated, 1)
                elif kind == "out1":
                    key = ("out1", "y", b)
                    bank_full(dve, *key)
                    V.tensor_tensor(x[:, b], x[:, b], bank(*key)[:, :].rearrange("p (k t) -> p k t", k=NB),
                                    ALU.add).then_inc(read(*key), 1)
                elif kind == "fp8":
                    dve.wait_ge(scaled8, b + 1)
                    whole, half = tmpn[:, 0], tmpn[:, 1]
                    V.tensor_scalar(q8[:, 0], whole, 128.0, -128.0, ALU.min, ALU.max, saturate=False)
                    link(V.tensor_scalar(q8[:, 1], half, FP8_HALF, -FP8_HALF, ALU.min, ALU.max, saturate=False))
                    link(V.tensor_scalar(whole, q8[:, 1], 64.0, -64.0, ALU.min, ALU.max))
                    link(V.tensor_tensor(half, q8[:, 1], whole, ALU.subtract))
                    if b:
                        bank_full(dve, "fp8", "y", b - 1)
                    V.scalar_tensor_tensor(qbf[:, :, :].rearrange("p k t -> p (k t)"), half, 2.0, q8[:, 0],
                                           ALU.mult, ALU.add).then_inc(q8_ready, 1)
                    key = ("fp8", "y", b)
                    bank_full(dve, *key)
                    V.scalar_tensor_tensor(x[:, b], bank(*key)[:, :].rearrange("p (k t) -> p k t", k=NB), oscale,
                                           x[:, b], ALU.mult, ALU.add).then_inc(read(*key), 1)


def by_partition(a):
    return a.reshape(NB, P, -1).transpose(1, 0, 2)


def host_arrays(i):
    h = {k: np.asarray(v) for k, v in i.items()}

    def activations(a):
        return a.transpose(2, 0, 1).reshape(NB, P, B, T).transpose(1, 2, 0, 3)

    def order(heads, width):
        return np.concatenate([k * P + np.arange(P).reshape(heads, width).T.ravel() for k in range(NB)])

    q0, r1 = order(8, D0), order(16, D1)
    mats = [h["L0_attn_Wq"][q0], h["L0_attn_Wk"][q0], h["L0_attn_Wv"], h["L0_attn_Wo"], h["L0_ffn_w3"],
            h["L1_attn_Wr"][r1], h["L1_attn_Wk"][r1], h["L1_attn_Wv"], h["L1_attn_Wg"], h["L1_attn_Wo"]]
    weights = np.stack([by_partition(m.T).reshape(P, NB * C) for m in mats], axis=1)
    cols = [h[f"{n}_{w}"] for w in "wu" for n in ("L0_cond", "L0_cond2", "L1_cond", "L1_cond2")]
    cols += [h[f"L1_attn_time_maa_{n}"].reshape(C) for n in "kvrg"]
    cols += [h["L1_attn_gamma"], h["L1_attn_beta"], h["L0_ffn_b3"]]
    vecs = np.concatenate([c.reshape(NB, P).T for c in cols], axis=1)
    row = np.concatenate([h["cond_512"].ravel(), h["L0_ffn_switch_b"], h["L1_attn_time_decay"].ravel(),
                          h["L1_attn_time_faaaa"].ravel(), h["L1_ffn_weight_scale"].reshape(1)])
    sw = h["L0_ffn_switch_w"].reshape(E, 8, 32, NB, P)
    bank = np.concatenate([h["L0_ffn_w1"].transpose(2, 0, 1), h["L0_ffn_b1"].T[:, :, None],
                           h["L0_ffn_w2"].transpose(2, 0, 1), h["L0_ffn_b2"].T[:, :, None]], axis=2)
    t = np.arange(P)
    same = t[:, None] // D1 == t[None, :] // D1
    negd = -np.maximum(np.arange(T)[None, :] - t[:, None] - 1, 0)
    hmask = np.arange(32)[None, :] // D1 == np.arange(GH)[:, None]
    made = {"ident": np.eye(P), "center": np.eye(P) - same / D1, "mean8": same / D1, "ones": np.ones((P, P)),
            "tri": t[None, :] > t[:, None], "negd": negd, "diagm": t[:, None] % 32 == np.arange(32)[None, :],
            "hmask": np.broadcast_to(hmask.reshape(1, P), (P, P)),
            "bdm": t[:, None] // DH == np.arange(8)[None, :],
            "rev": np.broadcast_to(E - np.arange(E), (P, E)), "eps": np.full((P, 1), EPS1)}
    bf16 = mybir.dt.np(BF16)
    later = np.where(t[None, :] > t[:, None], NEG, 0.0)
    out = {
        "x": activations(h["x"]), "fside": activations(h["fside_BxSxS_0"]), "weights": weights, "vecs": vecs,
        "rows": np.tile(row[None, :], (P, 1)), "switch": sw.transpose(4, 3, 1, 0, 2).reshape(P, -1),
        "expert": np.tile(bank, (8, 1, 1)), "w8": by_partition(h["L1_ffn_weight"].view(np.uint8).T).reshape(P, -1),
        "iscale": np.tile(h["L1_ffn_input_scale"].reshape(1, 1), (P, 1)),
        "consts": np.concatenate([made[n] for n in CONSTS], axis=1).astype(np.float32),
        "consts_bf16": np.concatenate([np.eye(P), later, later.T], axis=1).astype(bf16),
    }
    return {k: np.ascontiguousarray(v) for k, v in out.items()}


def kernel(**inputs):
    import concourse.bacc as bacc
    from concourse.bass_utils import run_bass_kernel_spmd

    arrays = host_arrays(inputs)
    nc = bacc.Bacc("TRN2", target_bir_lowering=False, num_devices=1)
    d = {k: nc.dram_tensor(f"in_{k}", a.shape, mybir.dt.from_np(a.dtype), kind="ExternalInput").ap()
         for k, a in arrays.items()}
    d["out"] = nc.dram_tensor("out", (P, B, NB, T), F32, kind="ExternalOutput").ap()
    build(nc, d)
    result = run_bass_kernel_spmd(nc, [{f"in_{k}": a for k, a in arrays.items()}], core_ids=[0])
    out = result.results[0]["out"]
    return out.transpose(1, 3, 2, 0).reshape(B, T, C)
```

```python
from contextlib import ExitStack

import numpy as np

import concourse.bass as bass
from concourse import mybir

F32 = mybir.dt.float32
BF16 = mybir.dt.bfloat16
F16 = mybir.dt.float16
FP8 = mybir.dt.float8e4
U8 = mybir.dt.uint8
U16 = mybir.dt.uint16
ALU = mybir.AluOpType
ACT = mybir.ActivationFunctionType
X = mybir.AxisListType.X

P = 128
B, T, C = 4, 256, 256
NB = C // P
TB = T // P
N = NB * T
NEG = -3.0e38

H0, D0 = 16, 16
H1, D1 = 32, 8
EPS1 = 1e-05 * 144
SPLIT_Q = (0, 0, 1, 1, 0, 2)
SPLIT_K = (0, 1, 0, 1, 2, 0)
NPROD = len(SPLIT_Q)
KROWS = 72
SROWS = NPROD * D0
GH = 4
SA = GH * T
SW = SA + GH * P

E, DH = 8, 16
EB = 2 * DH + 2
LOWEST = -40.0
EXP_LN_SET, GELU_SET = 6, 10
TWO_ONES = float(np.array([0x3F803F80], np.uint32).view(np.float32)[0])
FP8_MAX, FP8_HALF = 448.0, 224.0

W_COL = {l: 2 * l for l in range(4)}
U_COL = {l: 8 + 2 * l for l in range(4)}
MAA_COL = {"k": 16, "v": 18, "r": 20, "g": 22}
GAMMA_COL, BETA_COL, B3_COL = 24, 26, 28
NVEC = 30
COND_COL, SWB_COL, TD_COL, FA_COL, WS_COL = 0, 256, 264, 296, 328
NROW = 329
CONSTS = {"ident": P, "center": P, "mean8": P, "ones": P, "tri": P, "negd": T, "diagm": 32, "hmask": P,
          "bdm": 8, "rev": E, "eps": 1, "zero": 1}
CONST_AT = dict(zip(CONSTS, np.cumsum([0] + list(CONSTS.values())).tolist()))
NCONST = sum(CONSTS.values())
MATS = ["q0", "k0", "v0", "o0", "w3", "r1", "k1", "v1", "g1", "o1"]


ORDER = """
seq:1 condA:0 clamp:0 clamp:1 clamp:2 condA:1 seq:2 clamp:3 condB:0 condC:0 z:0 condB:1 seq:3 qk:0 condA:2
condC:1 z:1 condA:3 condB:2 condC:2 qk:1 S:0 S:1 S:2 S:3 z:2 v:0 mt:0 mx:0 condB:3 condA:4 qk:2 ST:0 condC:3
S:4 ST:1 av:0 condA:5 ST:2 av:1 condB:4 S:5 condC:4 ST:3 S:6 condB:5 av:2 S:7 condA:6 mx:1 z:3 v:1 condC:5 S:8
mt:1 qk:3 ST:4 condB:6 ST:5 av:3 condA:7 condC:6 post:0 S:9 S:10 S:11 av:4 condA:8 mx:2 av:5 ST:6 ST:7 av:6
condB:7 mt:2 scales:0 v:2 av:7 condC:7 v:3 condB:8 condA:9 condC:8 ST:8 condA:10 condB:9 S:12 S:13 condC:9
post:1 z:4 S:14 condB:10 S:15 condC:10 ST:9 condA:11 mx:3 route:0 z:5 ST:10 condB:11 mt:3 condA:12 av:8
condC:11 av:9 route:1 ST:11 condA:13 av:10 av:11 ST:12 ST:13 condB:12 post:2 condC:12 av:12 ST:14 condB:13
ST:15 av:13 av:14 condA:14 av:15 condC:13 post:3 z:6 exp1:0 condB:14 condA:15 exp2:0 route:2 exp1:1 w3:0 z:7
exp2:1 condC:14 route:3 exp1:2 exp2:2 z:8 condB:15 w3:1 w3:2 exp1:3 exp2:3 mix:0 pads:0 w3:3 wmask:0 wmask:1
wmask:2 wmask:3 rk:0 v1:0 z:10 z:9 condC:15 g1:0 mix:1 score:0 score:1 gate:0 wmask:4 wmask:5 rk:1 score:2
score:3 score:4 wmask:6 score:5 wmask:7 Y:0 score:6 score:7 v1:1 score:8 score:9 z:11 Y:1 score:10 norm:0
score:11 var:0 g1:1 mix:2 gate:1 score:12 score:13 rk:2 score:14 out1:0 score:15 z:12 fp8:0 Y:2 Y:3 v1:2
norm:1 last:0 score:16 score:17 var:1 g1:2 mix:3 gate:2 score:18 score:19 rk:3 score:20 out1:1 score:21 v1:3
score:22 score:23 z:13 fp8:1 Y:4 Y:5 score:24 score:25 score:26 norm:2 score:27 score:28 var:2 Y:6 score:29
g1:3 out1:2 score:30 gate:3 score:31 z:14 fp8:2 Y:7 last:1 norm:3 var:3 out1:3 z:15 last:2 fp8:3 last:3
"""
STEPS = [(kind, int(i)) for kind, i in (step.split(":") for step in ORDER.split())]


def dense_plan():
    uses = {}
    for kind, b in STEPS:
        names = {"qk": ["q", "k"], "v": ["v"], "mt": ["t"], "av": ["o"], "post": ["t0", "t1", "zT", "o"],
                 "route": ["lg", "lb"], "exp1": ["h0", "h1"], "exp2": ["o"], "w3": ["y"],
                 "rk": ["r", "k"], "v1": ["v"], "g1": ["g"], "Y": ["y"], "norm": ["c"], "var": ["v"],
                 "out1": ["y"], "last": ["y"]}.get(kind, [])
        for n in names:
            uses[(kind, n, b)] = len(uses)
    return uses


def score_plan():
    uses = {}
    for kind, b in STEPS:
        if kind in ("S", "ST", "score"):
            uses[(kind, b)] = len(uses)
    return uses


Z_AT = {i: n + 1 for n, i in enumerate(i for kind, i in STEPS if kind == "z")}
CLIP_AT = {s: n + 2 for n, s in enumerate(s for s in STEPS if s[0] in ("seq", "condA"))}
DENSE = dense_plan()
SCORE = score_plan()


def build(nc, d):
    with ExitStack() as ctx:
        def sb(name, shape, dt=F32):
            return ctx.enter_context(nc.sbuf_tensor(name, shape, dt))

        def sem(name):
            return ctx.enter_context(nc.semaphore(name))

        x = sb("x", [P, B, NB, T])
        wall = sb("weights", [P, 5, NB * C])
        consts = sb("consts", [P, NCONST])
        cbf = sb("consts_bf16", [P, 3 * P], BF16)
        vecs = sb("vecs", [P, NVEC])
        rows = sb("rows", [P, NROW])
        iscale_bf = sb("iscale_bf", [P, 1], BF16)
        early = sb("early", [P, 2 * 16 * (T + P)])
        mid = sb("mid", [P, H1 * T])

        def part(region, at, pattern, **dims):
            n = dims.pop("n")
            return region[:, at:at + n].rearrange(pattern, **dims)

        fk = part(early, 0, "p (b k t) -> p b k t", n=B * N, b=B, k=NB)
        seq = part(early, 2048, "p (b k m t) -> p b k m t", n=2 * B * N, b=B, k=NB, m=2)
        fwd = [part(early, at, "p (k m t) -> p k m t", n=2 * N, k=NB, m=2) for at in (6144, 11264)]
        bwd = [part(region, at, "p (k m t) -> p k m t", n=2 * N, k=NB, m=2)
               for region, at in ((early, 7168), (mid, 7168))]
        total = part(early, 8192, "p (r k m t) -> p r k m t", n=4 * N, r=2, k=NB, m=2)
        rec = part(early, 10752, "p (k t) -> p k t", n=N, k=NB)
        masked = part(early, 0, "p (r h n) -> p r h n", n=12288, r=2, h=16)
        sw = part(mid, 0, "p (k c e t) -> p k c e t", n=4096, k=NB, c=8, e=E)
        probs = part(mid, 4096, "p (r n) -> p r n", n=2 * SW, r=2)
        gel = part(mid, 4096, "p (w n) -> p w n", n=2 * N, w=2)
        wmask = part(mid, 0, "p (h t) -> p h t", n=H1 * T, h=H1)
        ratio = sb("ratio", [P, 8, NB, T])
        zbuf = sb("zbuf", [P, B, NB, T])
        qst = sb("q_stack", [P, 2, 16, T], BF16)
        kst = sb("k_stack", [P, 2, 16, T], BF16)
        split = sb("split", [P, 2, 3, N], BF16)
        resid = sb("resid", [P, 2, N])
        vbuf = sb("vbuf", [P, 2048])
        vaug = part(vbuf, 0, "p (r s h d) -> p r s h d", n=2048, r=2, s=TB, h=H0)
        vm = [a.rearrange("p (s g e c) -> p s g e c", s=TB, g=8, e=GH)
              for a in (vbuf[:, 0:2048], ratio[:, 0:4].rearrange("p r k t -> p (r k t)"))]
        misc = sb("misc", [P, 3584])
        zaug = part(misc, 0, "p (g t) -> p g t", n=1024, g=4)
        znrm = part(misc, 1024, "p (s c) -> p s c", n=N, s=TB)
        zoT = part(misc, 1536, "p (k t) -> p k t", n=N, k=NB)
        bd = part(misc, 2048, "p (r k w c) -> p r k w c", n=1024, r=2, k=2, w=2)
        mixb = part(misc, 0, "p (m k t) -> p m k t", n=4 * N, m=4, k=NB)
        diff = part(misc, 2048, "p (k t) -> p k t", n=N, k=NB)
        ysb = part(misc, 2560, "p (k t) -> p k t", n=N, k=NB)
        sgate = part(misc, 3072, "p (k t) -> p k t", n=N, k=NB)
        pair = sb("pair", [P, 2 * EB * E])
        esel = part(pair, 0, "p (k c e) -> p k c e", n=2 * EB * E, k=2, e=E)
        lmask = part(pair, 0, "p (e t) -> p e t", n=T, e=E)
        cent = part(pair, 0, "p (k t) -> p k t", n=N, k=NB)
        vsb = sb("vsb", [P, TB, C])
        tmpn = sb("tmpn", [P, 2, N])
        w16 = [tmpn[:, i, 0:N // 2].bitcast(U16) for i in range(2)]
        w8 = tmpn[:, 1, N // 2:N // 2 + N // 4].bitcast(U8)
        expert = sb("expert", [P, E, EB])
        ew = sb("ew", [P, 2, 2, EB])
        small = sb("small", [P, 256])
        mxs = sb("mxs", [P, 2, TB, H0])
        msp = sb("msp", [P, 2, TB, 3, H0], BF16)
        mT = sb("mT", [3 * H0, 2, T], BF16)
        wbf = sb("wbf", [P, NB, C], BF16)
        q8 = sb("q8", [P, 2, N], FP8)
        qbf = sb("qbf", [P, NB, T], BF16)

        dense = [ctx.enter_context(nc.psum_tensor(f"dense{i}", [P, 512], F32)) for i in range(2)]
        score = [ctx.enter_context(nc.psum_tensor(f"score{i}", [P, SW], F32)) for i in range(2)]

        place = {}

        def numbers(name, n):
            at = sum(place.values())
            place[name] = n
            return small[:, at:at + n]

        csum, dfac = (numbers(n, B) for n in ("csum", "dfac"))
        gain = numbers("gain", B)
        cw = numbers("cw", 2 * 4)
        dw = numbers("dw", 2 * 4)
        dec = numbers("dec", 8 * B).rearrange("p (b w) -> p b w", b=B)
        lam = numbers("lam", H1)
        rscale, rhalf, oscale, iscale = (numbers(n, 1) for n in ("rscale", "rhalf", "oscale", "iscale"))
        gam2, bet = numbers("gam2", NB), numbers("bet", NB)
        lgr, lg, pr, t8, t9 = (numbers(n, E) for n in ("lgr", "lg", "pr", "t8", "t9"))
        s1, s2, s3, nmx = (numbers(n, 1) for n in ("s1", "s2", "s3", "nmx"))
        gt = numbers("gt", 2)
        oh = numbers("oh", 2 * E).rearrange("p (k e) -> p k e", k=2)
        rden = numbers("rden", TB * H0).rearrange("p (s h) -> p s h", s=TB)
        mres = numbers("mres", TB * H0).rearrange("p (s h) -> p s h", s=TB)
        b2s = numbers("b2s", B)

        def mat(name):
            return wall[:, MATS.index(name) % 5, :].rearrange("p (k o) -> p k o", k=NB)

        def const(name):
            return consts[:, CONST_AT[name]:CONST_AT[name] + CONSTS[name]]

        def vec(col, k):
            return vecs[:, col + k:col + k + 1]

        def outer(ap, n):
            return ap.unsqueeze(1).to_broadcast([ap.shape[0], n, ap.shape[1]])

        def inner(ap, n):
            return ap.unsqueeze(2).to_broadcast([ap.shape[0], ap.shape[1], n])

        ident = const("ident")
        identb = cbf[:, 0:P]
        maskb = cbf[:, P:2 * P]
        maskTb = cbf[:, 2 * P:3 * P]

        names = """in_vecs in_consts in_qkv in_rest in_switch in_later
        clipped seq_ready csum_done thc_done clamped clamped_g dw_done ek_raw euk_raw eu_ready scan_done pool_sum tot_ready den_max
        rec_ready ratio_ready sig_ready z_ready part1 part2 part3 m_split pads_set
        lgr_ready logits_ready exps_done gates_picked bd_ready lam_ready wexp_done wtri_done wmask_done
        diff_done mix_done vm_ready squared newton_in sig_g gated scaled8 q8_ready out_in
        vec_step act_step pool_step""".split()
        (in_vecs, in_consts, in_qkv, in_rest, in_switch, in_later,
         clipped, seq_ready, csum_done, thc_done, clamped, clamped_g, dw_done, ek_raw, euk_raw, eu_ready, scan_done, pool_sum, tot_ready, den_max,
         rec_ready, ratio_ready, sig_ready, z_ready, part1, part2, part3, m_split, pads_set,
         lgr_ready, logits_ready, exps_done, gates_picked, bd_ready, lam_ready, wexp_done, wtri_done, wmask_done,
         diff_done, mix_done, vm_ready, squared, newton_in, sig_g, gated, scaled8, q8_ready, out_in,
         vec_step, act_step, pool_step) = (sem(n) for n in names)
        in_fside = [sem(f"in_fside{b}") for b in range(B)]
        in_x = [sem(f"in_x{b}") for b in range(B)]
        m_in = [sem(f"m_in{i}") for i in range(2)]
        stack_in = [sem(f"stack_in{i}") for i in range(2)]
        dense_full = [sem(f"dense_full{i}") for i in range(2)]
        dense_read = [sem(f"dense_read{i}") for i in range(2)]
        score_full = [sem(f"score_full{i}") for i in range(2)]
        score_read = [sem(f"score_read{i}") for i in range(2)]

        def bank(*key):
            return dense[DENSE[key] % 2]

        def bank_free(pe, *key):
            n = DENSE[key]
            if n >= 2:
                pe.wait_ge(dense_read[n % 2], n // 2)

        def bank_full(eng, *key):
            n = DENSE[key]
            eng.wait_ge(dense_full[n % 2], n // 2 + 1)

        def full(*key):
            return dense_full[DENSE[key] % 2]

        def read(*key):
            return dense_read[DENSE[key] % 2]

        def slot(*key):
            return score[SCORE[key] % 2]

        def slot_filled(*key):
            return score_full[SCORE[key] % 2]

        def slot_read(*key):
            return score_read[SCORE[key] % 2]

        def slot_free(pe, *key):
            n = SCORE[key]
            if n >= 2:
                pe.wait_ge(score_read[n % 2], n // 2)

        def slot_full(eng, *key):
            n = SCORE[key]
            eng.wait_ge(score_full[n % 2], n // 2 + 1)

        def bank_done(eng, *key):
            n = DENSE[key]
            eng.wait_ge(dense_read[n % 2], n // 2 + 1)

        def slot_done(eng, *key):
            n = SCORE[key]
            eng.wait_ge(score_read[n % 2], n // 2 + 1)

        def x_ready(eng, i):
            b = i % 4
            if i >= 4:
                bank_done(eng, *[("post", "o", b), ("w3", "y", b), ("out1", "y", b)][i // 4 - 1])

        def stacks_in(eng, kind, b):
            slot = b % 2
            eng.wait_ge(stack_in[slot], 16 * 2 * NPROD * ((0 if kind == "S" else 2) + b // 2 + 1))

        block = ctx.enter_context(nc.Block())

        @block.sync
        def _(sp):
            sp.dma_start(fk[:, 0], d["fside"][:, 0]).then_inc(in_fside[0], 16)
            sp.dma_start(rows[:], d["rows"]).then_inc(in_vecs, 16)
            sp.dma_start(vecs[:], d["vecs"]).then_inc(in_vecs, 16)
            for b in range(B):
                if b:
                    sp.dma_start(fk[:, b], d["fside"][:, b]).then_inc(in_fside[b], 16)
                sp.dma_start(x[:, b], d["x"][:, b]).then_inc(in_x[b], 16)
            sp.dma_start(wall[:, 0:3], d["weights"][:, 0:3]).then_inc(in_qkv, 16)
            sp.dma_start(cbf[:], d["consts_bf16"]).then_inc(in_consts, 16)
            sp.dma_start(consts[:], d["consts"]).then_inc(in_consts, 16)
            sp.dma_start(wall[:, 3:5], d["weights"][:, 3:5]).then_inc(in_rest, 16)
            sp.dma_start(expert[:], d["expert"]).then_inc(in_rest, 16)
            sp.dma_start(iscale_bf[:], d["iscale"]).then_inc(in_rest, 16)
            sp.dma_start(w8, d["w8"]).then_inc(in_rest, 16)
            sp.dma_start(mid[:, 0:4096], d["switch"]).then_inc(in_switch, 16)

            def stack(which, slot, width, cols):
                for r, (dst, parts) in enumerate([(qst, SPLIT_Q), (kst, SPLIT_K)]):
                    sp.wait_ge(part3, which + r + 1)
                    for n, j in enumerate(parts):
                        sp.dma_start(dst[width * n:width * (n + 1), slot, :, :],
                                     split[:, r, j, cols]).then_inc(stack_in[slot], 16)

            for kind, b in STEPS:
                if kind == "qk":
                    if b >= 2:
                        slot_full(sp, "ST", 4 * (b - 2) + 3)
                    stack(2 * b, b % 2, D0, slice(0, N))
                elif kind == "mt":
                    bank_done(sp, "mt", "t", b)
                    sp.dma_start(qst[SROWS:SROWS + 3, b % 2, :, :], mT[:, b % 2, :]).then_inc(m_in[b % 2], 16)
                elif kind == "rk":
                    for blk in range(NB):
                        if b == 0:
                            slot_full(sp, "ST", 4 * (2 + blk) + 3)
                            sp.wait_ge(pads_set, 4)
                        else:
                            slot_full(sp, "score", 4 * (2 * (b - 1) + blk) + 3)
                        stack(8 + 2 * b, blk, D1, slice(blk * T, (blk + 1) * T))
                elif kind == "post" and b == 3:
                    bank_full(sp, "post", "o", 3)
                    sp.dma_start(wall[:, 0:4], d["weights"][:, 5:9]).then_inc(in_later, 16)
                elif kind == "w3" and b == 3:
                    bank_full(sp, "w3", "y", 3)
                    sp.dma_start(wall[:, 4:5], d["weights"][:, 9:10]).then_inc(in_later, 16)
                elif kind == "last":
                    bank_done(sp, "last", "y", b)
                    sp.dma_start(d["out"][:, b], x[:, b]).then_inc(out_in, 16)
            sp.wait_ge(out_in, 16 * B)

        @block.gpsimd
        def _(pool):
            nc.gpsimd.memset(bwd[0][:, :, :, T - 1:T], 0.0)
            nc.gpsimd.memset(bwd[1][:, :, :, T - 1:T], 0.0)
            nc.gpsimd.memset(vaug[:, :, :, :, D0:2 * D0], 1.0).then_inc(pads_set, 1)
            pool.wait_ge(pads_set, 1)
            nc.gpsimd.memset(kst[SROWS:SROWS + 3, :, :, :].rearrange("p r h t -> p (r h t)").bitcast(F32),
                             TWO_ONES).then_inc(pads_set, 1)
            pool.wait_ge(pads_set, 2)
            def values(b):
                pool.wait_ge(ek_raw, b + 1)
                nc.gpsimd.tensor_tensor(seq[:, b, :, 0], seq[:, b, :, 1], fk[:, b], ALU.mult).then_inc(seq_ready, 1)

            values(0)
            for kind, i in STEPS:
                b = i
                if kind == "seq":
                    values(b)
                elif kind == "condA":
                    n = i % 2
                    pool.wait_ge(euk_raw, i + 1)
                    nc.gpsimd.tensor_tensor(total[:, n, :, 0], total[:, n, :, 1], fk[:, i % B],
                                            ALU.mult).then_inc(eu_ready, 1)
                    pool.wait_ge(scan_done, i + 1)
                    f = fwd[i % 2]
                    nc.gpsimd.tensor_tensor(f, f, bwd[i % 2], ALU.add).then_inc(pool_sum, 1)
                    pool.wait_ge(pool_sum, i + 1)
                    pool.wait_ge(eu_ready, i + 1)
                    nc.gpsimd.tensor_tensor(total[:, i % 2], total[:, i % 2], f, ALU.add).then_inc(tot_ready, 1)
                elif kind in ("qk", "rk"):
                    for w in range(2):
                        n = 2 * b + w + (8 if kind == "rk" else 0)
                        pool.wait_ge(part2, n + 1)
                        nc.gpsimd.tensor_tensor(split[:, w, 2], resid[:, w], split[:, w, 1],
                                                ALU.subtract).then_inc(part3, 1)
                elif kind == "route":
                    if b == 0:
                        pool.wait_ge(in_consts, 32)
                    pool.wait_ge(gates_picked, b + 1)
                    if b >= 2:
                        bank_full(pool, "exp2", "o", b - 2)
                    for k in range(2):
                        for w, at in ((0, 0), (1, DH + 1)):
                            last = nc.gpsimd.tensor_tensor(
                                bd[:, b % 2, k, w].rearrange("p (h c) -> p h c", h=8),
                                outer(ew[:, b % 2, k, at:at + DH], 8), inner(const("bdm"), DH), ALU.mult)
                    last.then_inc(bd_ready, 1)
                elif kind == "mix":
                    z = zbuf[:, b]
                    pool.wait_ge(z_ready, Z_AT[2 * B + b])
                    if b:
                        pool.wait_ge(mix_done, b)
                    else:
                        bank_done(pool, "exp2", "o", 2)
                    nc.gpsimd.tensor_tensor(diff[:, :, 1:T], z[:, :, 0:T - 1], z[:, :, 1:T], ALU.subtract)
                    nc.gpsimd.tensor_tensor(diff[:, :, 0:1], outer(const("zero"), NB), z[:, :, 0:1],
                                            ALU.subtract).then_inc(diff_done, 1)
                elif kind == "wmask":
                    pool.wait_ge(wexp_done, i + 1)
                    w = wmask[:, GH * i:GH * i + GH, 0:P]
                    nc.gpsimd.tensor_tensor(w, w, outer(const("tri"), GH), ALU.mult).then_inc(wtri_done, 1)
                elif kind == "pads":
                    pool.wait_ge(tot_ready, 4 * B)
                    pool.wait_ge(bd_ready, B)
                    pool.wait_ge(diff_done, 1)
                    for u in (2, 3):
                        slot_full(pool, "ST", 4 * u + 3)
                    for p in (32, 64):
                        nc.gpsimd.memset(kst[p:p + 32, :, :, :].rearrange("p r h t -> p (r h t)").bitcast(F32),
                                         0.0).then_inc(pads_set, 1)
                        pool.wait_ge(pads_set, 2 + p // 32)
                elif kind == "v1":
                    bank_done(pool, "v1", "v", b)
                    if b == 1:
                        pool.wait_ge(z_ready, max(Z_AT[2 * B + n] for n in range(B)))
                    if b >= 2:
                        bank_full(pool, "Y", "y", 2 * b - 3)
                    for s in range(TB):
                        for e in range(GH):
                            last = nc.gpsimd.tensor_tensor(
                                vm[b % 2][:, s, :, e, :], vsb[:, s].rearrange("p (g c) -> p g c", g=8),
                                outer(const("hmask")[:, 32 * e:32 * e + 32], 8), ALU.mult)
                    last.then_inc(vm_ready, 1)

        @block.scalar
        def _(act):
            steps = [0]

            def link(ins):
                steps[0] += 1
                ins.then_inc(act_step, 1)
                act.wait_ge(act_step, steps[0])

            def load_exp_ln():
                nc.scalar.add_instruction(mybir.InstLoadActFuncSet(name=nc.get_next_instruction_name(),
                                                                   act_func_set_id=EXP_LN_SET))

            def sigmoid(v):
                link(nc.scalar.activation(v, v, ACT.Exp, scale=-1.0))
                link(nc.scalar.activation(v, v, ACT.Ln, bias=1.0))
                return nc.scalar.activation(v, v, ACT.Exp, scale=-1.0)

            load_exp_ln()
            act.wait_ge(clipped, 1)
            nc.scalar.activation(seq[:, 0, :, 1], seq[:, 0, :, 0], ACT.Exp).then_inc(ek_raw, 1)
            act.wait_ge(csum_done, 1)
            sigmoid(csum).then_inc(thc_done, 1)
            link(nc.scalar.activation(dw, cw, ACT.Exp))
            nc.scalar.activation(dw, dw, ACT.Exp, scale=-1.0).then_inc(dw_done, 1)
            nc.scalar.activation(lam, lam, ACT.Exp).then_inc(dw_done, 1)
            def copy_parts(kind, b):
                names = ("q", "k") if kind == "qk" else ("r", "k")
                for w in range(2):
                    n = 2 * b + w + (8 if kind == "rk" else 0)
                    key = (kind, names[w], b)
                    bank_full(act, *key)
                    before = n // 2
                    if before:
                        for slot in range(2):
                            done = (before + 1 - slot) // 2 if before <= 4 else before - 2
                            if done:
                                act.wait_ge(stack_in[slot], 16 * 2 * NPROD * done)
                    nc.scalar.activation(split[:, w, 0], bank(*key)[:, :], ACT.Copy).then_inc(part1, 1)
                for w in range(2):
                    n = 2 * b + w + (8 if kind == "rk" else 0)
                    bank_done(act, kind, names[w], b)
                    nc.scalar.activation(split[:, w, 1], resid[:, w], ACT.Copy).then_inc(part2, 1)

            for kind, i in STEPS:
                b = i
                if kind == "seq":
                    act.wait_ge(clipped, CLIP_AT["seq", b])
                    nc.scalar.activation(seq[:, b, :, 1], seq[:, b, :, 0], ACT.Exp).then_inc(ek_raw, 1)
                elif kind == "condA":
                    act.wait_ge(clipped, CLIP_AT["condA", i])
                    nc.scalar.activation(total[:, i % 2, :, 1], total[:, i % 2, :, 0], ACT.Exp).then_inc(euk_raw, 1)
                elif kind == "condB":
                    act.wait_ge(den_max, i + 1)
                    if i:
                        act.wait_ge(ratio_ready, i)
                    link(nc.scalar.activation(rec, total[:, i % 2, :, 1], ACT.Ln))
                    nc.scalar.activation(rec, rec, ACT.Exp, scale=-1.0).then_inc(rec_ready, 1)
                elif kind == "z":
                    act.wait_ge(clamped, i + 1)
                    sigmoid(zbuf[:, i % B]).then_inc(sig_ready, 1)
                elif kind == "qk":
                    copy_parts(kind, b)
                elif kind == "v":
                    bank_full(act, "v", "v", b)
                    if b >= 2:
                        bank_full(act, "av", "o", 4 * (b - 2) + 3)
                    nc.scalar.activation(vaug[:, b % 2, :, :, 0:D0],
                                         bank("v", "v", b)[:, :].rearrange("p (s h d) -> p s h d", s=TB, h=H0),
                                         ACT.Copy).then_inc(read("v", "v", b), 1)
                elif kind == "mt":
                    bank_full(act, "mt", "t", b)
                    if b >= 2:
                        act.wait_ge(m_in[b % 2], 16 * (b // 2))
                    nc.scalar.activation(mT[:, b % 2, :], bank("mt", "t", b)[0:48, 0:128].bitcast(BF16),
                                         ACT.Copy).then_inc(read("mt", "t", b), 1)
                elif kind == "ST":
                    slot_full(act, "ST", i)
                    if i >= 2:
                        bank_full(act, "av", "o", i - 2)
                    nc.scalar.activation(probs[:, i % 2], slot("ST", i)[:, :], ACT.Exp,
                                         scale=D0 ** -0.5).then_inc(slot_read("ST", i), 1)
                elif kind == "av":
                    key = ("av", "o", i)
                    bank_full(act, *key)
                    if i >= 4 and i % 4 == 0:
                        bank_full(act, "post", "t1", i // 4 - 1)
                    nc.scalar.activation(zaug[:, i % 4], bank(*key)[:, 0:T], ACT.Copy).then_inc(read(*key), 1)
                elif kind == "post":
                    bank_full(act, "post", "zT", b)
                    if b >= 1:
                        bank_full(act, "post", "o", b - 1)
                    nc.scalar.activation(zoT, bank("post", "zT", b)[:, :].rearrange("p (k t) -> p k t", k=NB),
                                         ACT.Copy).then_inc(read("post", "zT", b), 1)
                elif kind == "route":
                    act.wait_ge(logits_ready, b + 1)
                    nc.scalar.activation(pr, lg, ACT.Exp, bias=nmx).then_inc(exps_done, 1)
                elif kind == "exp1":
                    nc.scalar.add_instruction(mybir.InstLoadActFuncSet(name=nc.get_next_instruction_name(),
                                                                       act_func_set_id=GELU_SET))
                    for k in range(2):
                        key = ("exp1", f"h{k}", b)
                        bank_full(act, *key)
                        if k == 0 and b >= 1:
                            bank_full(act, "exp2", "o", b - 1)
                        if k == 0 and b == 0:
                            bank_full(act, "av", "o", 4 * B - 1)
                        nc.scalar.activation(gel[:, k], bank(*key)[:, :], ACT.Gelu,
                                             bias=ew[:, b % 2, k, DH:DH + 1]).then_inc(read(*key), 1)
                    load_exp_ln()
                elif kind == "wmask":
                    if i == 0:
                        act.wait_ge(lam_ready, 1)
                        act.wait_ge(in_consts, 32)
                        act.wait_ge(tot_ready, 4 * B)
                        bank_full(act, "route", "lg", 3)
                        bank_full(act, "exp2", "o", 3)
                    for h in range(GH * i, GH * i + GH):
                        last = nc.scalar.activation(wmask[:, h], const("negd"), ACT.Exp, scale=lam[:, h:h + 1])
                    last.then_inc(wexp_done, 1)
                elif kind == "rk":
                    copy_parts(kind, b)
                elif kind == "v1":
                    bank_full(act, "v1", "v", b)
                    if b >= 1:
                        act.wait_ge(vm_ready, b)
                    nc.scalar.activation(vsb[:, :, :], bank("v1", "v", b)[:, :].rearrange("p (s c) -> p s c", s=TB),
                                         ACT.Copy).then_inc(read("v1", "v", b), 1)
                elif kind == "g1":
                    act.wait_ge(clamped_g, b + 1)
                    sigmoid(sgate).then_inc(sig_g, 1)
                elif kind == "Y":
                    bank_full(act, "Y", "y", i)
                    if i >= 2 and i % 2 == 0:
                        bank_full(act, "norm", "c", i // 2 - 1)
                    nc.scalar.activation(ysb[:, i % 2], bank("Y", "y", i)[:, 0:T], ACT.Copy)\
                        .then_inc(read("Y", "y", i), 1)
                elif kind == "norm":
                    bank_full(act, "norm", "c", b)
                    if b >= 1:
                        act.wait_ge(q8_ready, b)
                        bank_full(act, "out1", "y", b - 1)
                    c = bank("norm", "c", b)
                    nc.scalar.activation(tmpn[:, 0], c[:, :], ACT.Square).then_inc(squared, 1)
                    nc.scalar.activation(cent, c[:, :].rearrange("p (k t) -> p k t", k=NB),
                                         ACT.Copy).then_inc(read("norm", "c", b), 1)
                elif kind == "var":
                    bank_full(act, "var", "v", b)
                    link(nc.scalar.activation(tmpn[:, 1], bank("var", "v", b)[:, :], ACT.Ln, bias=const("eps")))
                    link(nc.scalar.activation(tmpn[:, 1], tmpn[:, 1], ACT.Exp, scale=-0.5))
                    nc.scalar.activation(tmpn[:, 0], tmpn[:, 1], ACT.Square).then_inc(newton_in, 1)
                elif kind == "fp8":
                    act.wait_ge(z_ready, Z_AT[3 * B + b])
                    z = zbuf[:, b].rearrange("p k t -> p (k t)")
                    nc.scalar.activation(tmpn[:, 0], z, ACT.Copy, scale=rscale)
                    nc.scalar.activation(tmpn[:, 1], z, ACT.Copy, scale=rhalf).then_inc(scaled8, 1)

        @block.tensor
        def _(pe):
            def project(out, w, src, k_outer=False):
                for o in range(NB):
                    for k in range(NB):
                        last = nc.tensor.matmul(out[:, o * T:(o + 1) * T], w[:, k, o * P:(o + 1) * P], src[:, k],
                                                start=(k == 0), stop=(k == NB - 1))
                return last

            def project_t(out, w, src):
                for s in range(TB):
                    for k in range(NB):
                        last = nc.tensor.matmul(out[:, s * C:(s + 1) * C], src[:, k, s * P:(s + 1) * P], w[:, k],
                                                start=(k == 0), stop=(k == NB - 1))
                return last

            def transposed_scores(out, kk, qq, mask):
                last = None
                for (o, w), (ks, qs) in zip(out, (((0, P), (0, T)), ((P, T), (P, T)))):
                    last = nc.tensor.matmul(o, kk[:, ks[0]:ks[1]], qq[:, qs[0]:qs[1]], start=True, stop=not mask)
                    if mask:
                        last = nc.tensor.matmul(w, identb, maskTb, start=False, stop=True)
                return last

            for kind, i in STEPS:
                b = i
                if kind == "qk":
                    pe.wait_ge(z_ready, Z_AT[b])
                    if b == 0:
                        pe.wait_ge(in_qkv, 16)
                    for n in ("q", "k"):
                        bank_free(pe, "qk", n, b)
                        project(bank("qk", n, b), mat(n + "0"), zbuf[:, b]).then_inc(full("qk", n, b), 1)
                elif kind == "v":
                    bank_free(pe, "v", "v", b)
                    project_t(bank("v", "v", b), mat("v0"), zbuf[:, b]).then_inc(full("v", "v", b), 1)
                elif kind == "S":
                    b, g = divmod(i, 4)
                    if g == 0:
                        stacks_in(pe, "S", b)
                    if i == 0:
                        pe.wait_ge(in_consts, 32)
                    slot_free(pe, "S", i)
                    out = slot("S", i)
                    for h in range(GH):
                        q, k = (st[0:SROWS, b % 2, GH * g + h] for st in (qst, kst))
                        for at, t0, w in ((h * T, P, T), (SA + h * P, 0, P)):
                            nc.tensor.matmul(out[:, at:at + w], q[:, t0:t0 + P], k[:, 0:w],
                                             start=True, stop=False)
                            last = nc.tensor.matmul(out[:, at + w - P:at + w], identb, maskb,
                                                    start=False, stop=True)
                    last.then_inc(slot_filled("S", i), 1)
                elif kind == "mt":
                    pe.wait_ge(m_split, b + 1)
                    bank_free(pe, "mt", "t", b)
                    out = bank("mt", "t", b)[0:48, 0:128].bitcast(BF16)
                    for s in range(TB):
                        last = nc.tensor.transpose(out[:, s * P:(s + 1) * P],
                                                   msp[:, b % 2, s].rearrange("p j h -> p (j h)"), identb)
                    last.then_inc(full("mt", "t", b), 1)
                elif kind == "ST":
                    b, g = divmod(i, 4)
                    if g == 0:
                        pe.wait_ge(m_in[b % 2], 16 * (b // 2 + 1))
                        pe.wait_ge(pads_set, 2)
                    slot_free(pe, "ST", i)
                    out = slot("ST", i)
                    for h in range(GH):
                        q, k = (st[0:SROWS + 3, b % 2, GH * g + h] for st in (qst, kst))
                        last = transposed_scores(
                            [(out[:, h * T:(h + 1) * T], out[:, h * T:h * T + P]),
                             (out[:, SA + h * P:SA + (h + 1) * P],) * 2], k, q, True)
                    last.then_inc(slot_filled("ST", i), 1)
                elif kind == "av":
                    b, g = divmod(i, 4)
                    if g == 0:
                        bank_done(pe, "v", "v", b)
                    slot_done(pe, "ST", i)
                    key = ("av", "o", i)
                    bank_free(pe, *key)
                    for s in range(TB):
                        for h in range(GH):
                            src = (probs[:, g % 2, h * T:(h + 1) * T] if s == 0 else
                                   probs[:, g % 2, SA + h * P:SA + (h + 1) * P])
                            last = nc.tensor.matmul(
                                bank(*key)[32 * h:32 * h + 32, s * P:T], vaug[:, b % 2, s, GH * g + h],
                                src, start=(s == 0), stop=(s == TB - 1), tile_position=(0, 32 * h))
                    last.then_inc(full(*key), 1)
                elif kind == "post":
                    for s in range(TB):
                        if s == 0:
                            for g in (2, 3):
                                bank_done(pe, "av", "o", 4 * b + g)
                        key = ("post", f"t{s}", b)
                        bank_free(pe, *key)
                        for g in range(4):
                            last = nc.tensor.transpose(bank(*key)[:, g * P:(g + 1) * P],
                                                       zaug[:, g, s * P:(s + 1) * P], ident)
                        last.then_inc(full(*key), 1)
                    bank_done(pe, "post", "t1", b)
                    bank_done(pe, "post", "t0", b)
                    bank_free(pe, "post", "zT", b)
                    for k in range(NB):
                        for s in range(TB):
                            last = nc.tensor.transpose(
                                bank("post", "zT", b)[:, k * T + s * P:k * T + (s + 1) * P],
                                znrm[:, s, k * P:(k + 1) * P], ident)
                    last.then_inc(full("post", "zT", b), 1)
                    if b == 0:
                        pe.wait_ge(in_rest, 64)
                    bank_done(pe, "post", "zT", b)
                    bank_free(pe, "post", "o", b)
                    project(bank("post", "o", b), mat("o0"), zoT).then_inc(full("post", "o", b), 1)
                elif kind == "route":
                    pe.wait_ge(z_ready, Z_AT[B + b])
                    if b == 0:
                        pe.wait_ge(in_switch, 16)
                    bank_free(pe, "route", "lg", b)
                    out = bank("route", "lg", b)
                    for r in range(2):
                        for k in range(NB):
                            for j in range(4):
                                c = 4 * r + j
                                last = nc.tensor.matmul(
                                    out[32 * j:32 * j + 32, 0:T], zbuf[:, b, k, 32 * c:32 * c + 32],
                                    sw[:, k, c].rearrange("p e t -> p (e t)"),
                                    start=(r == 0 and k == 0), stop=(r == 1 and k == 1),
                                    tile_position=(0, 32 * j))
                    last.then_inc(full("route", "lg", b), 1)
                    pe.wait_ge(lgr_ready, b + 1)
                    bank_free(pe, "route", "lb", b)
                    nc.tensor.matmul(bank("route", "lb", b)[:, 0:E], const("ones"), lgr, start=True, stop=True)\
                        .then_inc(full("route", "lb", b), 1)
                elif kind == "exp1":
                    pe.wait_ge(bd_ready, b + 1)
                    for k in range(2):
                        key = ("exp1", f"h{k}", b)
                        bank_free(pe, *key)
                        nc.tensor.matmul(bank(*key)[:, :], bd[:, b % 2, k, 0], zbuf[:, b].rearrange("p k t -> p (k t)"),
                                         start=True, stop=True).then_inc(full(*key), 1)
                elif kind == "exp2":
                    bank_free(pe, "exp2", "o", b)
                    for k in range(2):
                        bank_done(pe, "exp1", f"h{k}", b)
                        last = nc.tensor.matmul(bank("exp2", "o", b)[:, :], bd[:, b % 2, k, 1], gel[:, k],
                                                start=(k == 0), stop=(k == 1))
                    last.then_inc(full("exp2", "o", b), 1)
                elif kind == "w3":
                    bank_done(pe, "exp2", "o", b)
                    bank_free(pe, "w3", "y", b)
                    project(bank("w3", "y", b), mat("w3"), zbuf[:, b]).then_inc(full("w3", "y", b), 1)
                elif kind == "rk":
                    pe.wait_ge(mix_done, b + 1)
                    if b == 0:
                        pe.wait_ge(in_later, 32)
                    for m, n in enumerate(("r", "k")):
                        bank_free(pe, "rk", n, b)
                        project(bank("rk", n, b), mat(n + "1"), mixb[:, m]).then_inc(full("rk", n, b), 1)
                elif kind == "v1":
                    bank_free(pe, "v1", "v", b)
                    project_t(bank("v1", "v", b), mat("v1"), mixb[:, 2]).then_inc(full("v1", "v", b), 1)
                elif kind == "g1":
                    bank_free(pe, "g1", "g", b)
                    project(bank("g1", "g", b), mat("g1"), mixb[:, 3]).then_inc(full("g1", "g", b), 1)
                elif kind == "score":
                    u, g = divmod(i, 4)
                    if g == 0:
                        stacks_in(pe, "score", u)
                    slot_free(pe, "score", i)
                    out = slot("score", i)
                    for h in range(GH):
                        q, k = (st[0:KROWS, u % 2, GH * g + h] for st in (qst, kst))
                        last = transposed_scores(
                            [(out[:, h * T:(h + 1) * T], None),
                             (out[:, SA + h * P:SA + (h + 1) * P], None)], k, q, False)
                    last.then_inc(slot_filled("score", i), 1)
                elif kind == "Y":
                    slot_done(pe, "score", 4 * i + 3)
                    slot_done(pe, "score", 4 * i + 2)
                    if i % 2 == 0:
                        pe.wait_ge(vm_ready, i // 2 + 1)
                    bank_free(pe, "Y", "y", i)
                    out = bank("Y", "y", i)
                    for e in range(GH):
                        for s in range(TB):
                            for g in range(4):
                                last = nc.tensor.matmul(
                                    out[32 * g:32 * g + 32, s * P:T], vm[i // 2 % 2][:, s, 4 * (i % 2) + g, e],
                                    masked[:, i % 2, GH * g + e, s * T:s * T + (T if s == 0 else P)],
                                    start=(e == 0 and s == 0), stop=(e == GH - 1 and s == TB - 1),
                                    tile_position=(0, 32 * g))
                    last.then_inc(full("Y", "y", i), 1)
                elif kind == "norm":
                    for u in (2 * b, 2 * b + 1):
                        bank_done(pe, "Y", "y", u)
                    bank_free(pe, "norm", "c", b)
                    nc.tensor.matmul(bank("norm", "c", b)[:, :], const("center"), ysb.rearrange("p k t -> p (k t)"),
                                     start=True, stop=True).then_inc(full("norm", "c", b), 1)
                elif kind == "var":
                    pe.wait_ge(squared, b + 1)
                    bank_free(pe, "var", "v", b)
                    nc.tensor.matmul(bank("var", "v", b)[:, :], const("mean8"), tmpn[:, 0],
                                     start=True, stop=True).then_inc(full("var", "v", b), 1)
                elif kind == "out1":
                    pe.wait_ge(gated, b + 1)
                    bank_free(pe, "out1", "y", b)
                    project(bank("out1", "y", b), mat("o1"), cent).then_inc(full("out1", "y", b), 1)
                elif kind == "last":
                    pe.wait_ge(q8_ready, b + 1)
                    bank_free(pe, "last", "y", b)
                    project(bank("last", "y", b), wbf, qbf).then_inc(full("last", "y", b), 1)

        @block.vector
        def _(dve):
            steps = [0]

            def link(ins):
                steps[0] += 1
                ins.then_inc(vec_step, 1)
                dve.wait_ge(vec_step, steps[0])

            V = nc.vector
            dve.wait_ge(in_fside[0], 16)
            V.tensor_scalar(seq[:, 0, :, 0], fk[:, 0], 30.0, None, ALU.min).then_inc(clipped, 1)
            dve.wait_ge(in_vecs, 32)
            V.reduce_sum(csum, rows[:, 0:256].rearrange("p (b c) -> p b c", b=B), axis=X)
            V.tensor_scalar(cw, vecs[:, 0:8], 80.0, None, ALU.min)
            link(V.tensor_scalar(lam, rows[:, TD_COL:TD_COL + H1], 80.0, None, ALU.min))
            V.tensor_scalar(csum, csum, LOWEST, None, ALU.max).then_inc(csum_done, 1)
            dve.wait_ge(thc_done, 1)
            V.tensor_scalar(gain, csum, -0.2, -0.8, ALU.mult, ALU.add)
            link(V.tensor_scalar(dfac, csum, 0.5, 0.5, ALU.mult, ALU.add))
            dve.wait_ge(dw_done, 2)
            for b in range(B):
                V.tensor_scalar(dec[:, b], dw, dfac[:, b:b + 1], None, ALU.mult)
            link(V.tensor_scalar(lam, lam, 1e30, None, ALU.min))
            def clamp(i):
                V.tensor_scalar(zbuf[:, i % B], x[:, i % B], LOWEST, None, ALU.max).then_inc(clamped, 1)

            def setup_rest():
                dve.wait_ge(in_rest, 64)
                link(V.tensor_copy(w16[0], w8))
                link(V.tensor_scalar(w16[1], w16[0], 0x80, 8, ALU.bitwise_and, ALU.logical_shift_left))
                link(V.tensor_scalar(w16[0], w16[0], 0x7F, 7, ALU.bitwise_and, ALU.logical_shift_left))
                link(V.tensor_tensor(w16[0], w16[0], w16[1], ALU.bitwise_or))
                V.tensor_scalar(wbf[:, :, :].rearrange("p k o -> p (k o)"), w16[0].bitcast(F16), 256.0, None, ALU.mult)
                link(V.tensor_copy(iscale, iscale_bf[:, 0:1]))
                V.tensor_scalar(oscale, iscale, rows[:, WS_COL:WS_COL + 1], None, ALU.mult)
                V.tensor_scalar(gam2, vecs[:, GAMMA_COL:GAMMA_COL + 2], -0.5, None, ALU.mult)
                V.tensor_scalar(bet, vecs[:, BETA_COL:BETA_COL + 2], 1.0, None, ALU.mult)
                link(V.reciprocal(rscale, iscale))
                V.tensor_scalar(rhalf, rscale, 0.5, None, ALU.mult).then_inc(lam_ready, 1)

            def rest(kind, b):
                names = ("q", "k") if kind == "qk" else ("r", "k")
                for w in range(2):
                    n = 2 * b + w + (8 if kind == "rk" else 0)
                    dve.wait_ge(part1, n + 1)
                    if n >= 2:
                        dve.wait_ge(part3, n - 1)
                    key = (kind, names[w], b)
                    V.tensor_tensor(resid[:, w], bank(*key)[:, :], split[:, w, 0],
                                    ALU.subtract).then_inc(read(*key), 1)

            for kind, i in STEPS:
                b = i
                if kind == "seq":
                    dve.wait_ge(in_fside[b], 16)
                    V.tensor_scalar(seq[:, b, :, 0], fk[:, b], 30.0, None, ALU.min).then_inc(clipped, 1)
                elif kind == "clamp":
                    dve.wait_ge(in_x[b], 16)
                    clamp(b)
                elif kind == "scales":
                    setup_rest()
                elif kind == "condA":
                    l, b = divmod(i, B)
                    if i >= 2:
                        dve.wait_ge(tot_ready, i - 1)
                        dve.wait_ge(ratio_ready, i - 1)
                    for k in range(NB):
                        last = V.tensor_scalar(total[:, i % 2, k, 0], fk[:, b, k], vec(U_COL[l], k), 30.0,
                                               ALU.add, ALU.min)
                    last.then_inc(clipped, 1)
                    f, w = fwd[i % 2], bwd[i % 2]
                    if i < B:
                        dve.wait_ge(seq_ready, b + 1)
                    for k in range(NB):
                        decay = dec[:, b, 2 * l + k:2 * l + k + 1]
                        for m in range(2):
                            V.tensor_tensor_scan(f[:, k, m], decay.to_broadcast([P, T]), seq[:, b, k, m],
                                                 0.0, ALU.mult, ALU.add)
                            last = V.tensor_tensor_scan(w[:, k, m, 0:T - 1][:, ::-1], seq[:, b, k, m, 1:T][:, ::-1],
                                                        decay.to_broadcast([P, T - 1]), 0.0, ALU.add, ALU.mult)
                    last.then_inc(scan_done, 1)
                elif kind == "condB":
                    dve.wait_ge(tot_ready, i + 1)
                    V.tensor_scalar(total[:, i % 2, :, 1], total[:, i % 2, :, 1], 1e-8, None,
                                    ALU.max).then_inc(den_max, 1)
                elif kind == "condC":
                    dve.wait_ge(rec_ready, i + 1)
                    num, den = total[:, i % 2, :, 0], total[:, i % 2, :, 1]
                    V.scalar_tensor_tensor(num, num, gain[:, i % B:i % B + 1], rec, ALU.mult, ALU.mult)
                    link(V.tensor_tensor(den, den, rec, ALU.mult))
                    V.scalar_tensor_tensor(ratio[:, i % 8], den, 2.0, num, ALU.subtract,
                                           ALU.mult).then_inc(ratio_ready, 1)
                elif kind == "z":
                    dve.wait_ge(sig_ready, Z_AT[i])
                    dve.wait_ge(ratio_ready, i + 1)
                    z = zbuf[:, i % B]
                    V.tensor_tensor(z, z, ratio[:, i % 8], ALU.mult).then_inc(z_ready, 1)
                elif kind == "qk":
                    rest(kind, b)
                elif kind == "S":
                    b, g = divmod(i, 4)
                    slot_full(dve, "S", i)
                    src = slot("S", i)
                    V.reduce_max(mxs[:, b % 2, 1, GH * g:GH * g + GH],
                                 src[:, 0:SA].rearrange("p (h t) -> p h t", h=GH), axis=X)
                    V.reduce_max(mxs[:, b % 2, 0, GH * g:GH * g + GH],
                                 src[:, SA:SW].rearrange("p (h t) -> p h t", h=GH),
                                 axis=X).then_inc(slot_read("S", i), 1)
                elif kind == "mx":
                    r = b % 2
                    for g in range(4):
                        slot_done(dve, "S", 4 * b + g)
                    if b >= 2:
                        bank_full(dve, "mt", "t", b - 2)
                    m = [msp[:, r, :, j] for j in range(3)]
                    link(V.tensor_scalar(m[0], mxs[:, r], -1.0, None, ALU.mult))
                    link(V.scalar_tensor_tensor(mres, mxs[:, r], -1.0, m[0], ALU.mult, ALU.subtract))
                    link(V.tensor_copy(m[1], mres))
                    V.tensor_tensor(m[2], mres, m[1], ALU.subtract).then_inc(m_split, 1)
                elif kind == "post":
                    for s in range(TB):
                        key = ("post", f"t{s}", b)
                        bank_full(dve, *key)
                        if s == 0 and b >= 1:
                            bank_full(dve, "post", "zT", b - 1)
                        src = bank(*key)[:, :].rearrange("p (h d) -> p h d", h=H0)
                        link(V.reciprocal(rden[:, s], src[:, :, D0]))
                        V.tensor_tensor(znrm[:, s].rearrange("p (h d) -> p h d", h=H0), src[:, :, 0:D0],
                                        inner(rden[:, s], D0), ALU.mult).then_inc(read(*key), 1)
                    key = ("post", "o", b)
                    bank_full(dve, *key)
                    V.tensor_tensor(x[:, b], x[:, b], bank(*key)[:, :].rearrange("p (k t) -> p k t", k=NB),
                                    ALU.add).then_inc(read(*key), 1)
                    bank_done(dve, *key)
                    clamp(B + b)
                elif kind == "route":
                    key = ("route", "lg", b)
                    if b == 0:
                        dve.wait_ge(in_consts, 32)
                    bank_full(dve, *key)
                    V.tensor_tensor(lmask, bank(*key)[:, 0:T].rearrange("p (e t) -> p e t", e=E),
                                    outer(const("diagm"), E), ALU.mult).then_inc(read(*key), 1)
                    bank_done(dve, *key)
                    V.reduce_sum(lgr, lmask, axis=X).then_inc(lgr_ready, 1)
                    key = ("route", "lb", b)
                    bank_full(dve, *key)
                    V.tensor_tensor(lg, bank(*key)[:, 0:E], rows[:, SWB_COL:SWB_COL + E],
                                    ALU.add).then_inc(read(*key), 1)
                    bank_done(dve, *key)
                    link(V.reduce_max(s1, lg, axis=X))
                    V.tensor_scalar(nmx, s1, -1.0, None, ALU.mult).then_inc(logits_ready, 1)
                    dve.wait_ge(exps_done, b + 1)
                    link(V.reduce_sum(s2, pr, axis=X))
                    link(V.reciprocal(s3, s2))
                    link(V.tensor_scalar(pr, pr, s3, None, ALU.mult))
                    p = pr
                    for k in range(2):
                        link(V.reduce_max(gt[:, k:k + 1], p, axis=X))
                        link(V.scalar_tensor_tensor(t8, p, gt[:, k:k + 1], const("rev"), ALU.is_equal, ALU.mult))
                        link(V.reduce_max(s1, t8, axis=X))
                        link(V.tensor_scalar(oh[:, k], t8, s1, None, ALU.is_equal))
                        if k == 0:
                            link(V.scalar_tensor_tensor(t9, oh[:, 0], -2.0, pr, ALU.mult, ALU.add))
                            p = t9
                    for k in range(2):
                        last = V.tensor_tensor(esel[:, k], expert[:, :, :].rearrange("p e c -> p c e"),
                                               outer(oh[:, k], EB), ALU.mult)
                    link(last)
                    if b >= 2:
                        bank_done(dve, "exp1", "h1", b - 2)
                        dve.wait_ge(bd_ready, b - 1)
                    link(V.reduce_sum(ew[:, b % 2].rearrange("p k c -> p (k c)"),
                                      esel.rearrange("p k c e -> p (k c) e"), axis=X))
                    for k in range(2):
                        half = ew[:, b % 2, k, DH + 1:EB]
                        last = V.tensor_scalar(half, half, gt[:, k:k + 1], None, ALU.mult)
                    last.then_inc(gates_picked, 1)
                    dve.wait_ge(gates_picked, b + 1)
                    link(V.tensor_tensor(b2s[:, b:b + 1], ew[:, b % 2, 0, EB - 1:EB], ew[:, b % 2, 1, EB - 1:EB],
                                         ALU.add))
                elif kind == "exp2":
                    key = ("exp2", "o", b)
                    bank_full(dve, *key)
                    z = zbuf[:, b]
                    V.scalar_tensor_tensor(z, bank(*key)[:, :].rearrange("p (k t) -> p k t", k=NB), b2s[:, b:b + 1], z,
                                           ALU.add, ALU.add).then_inc(read(*key), 1)
                elif kind == "w3":
                    key = ("w3", "y", b)
                    bank_full(dve, *key)
                    for k in range(NB):
                        last = V.scalar_tensor_tensor(x[:, b, k], bank(*key)[:, k * T:(k + 1) * T], vec(B3_COL, k),
                                                      x[:, b, k], ALU.add, ALU.add)
                    last.then_inc(read(*key), 1)
                    bank_done(dve, *key)
                    clamp(2 * B + b)
                elif kind == "mix":
                    z = zbuf[:, b]
                    if b:
                        bank_full(dve, "g1", "g", b - 1)
                    dve.wait_ge(diff_done, b + 1)
                    for m, name in enumerate(("r", "k", "v", "g")):
                        for k in range(NB):
                            last = V.scalar_tensor_tensor(mixb[:, m, k], diff[:, k], vec(MAA_COL[name], k), z[:, k],
                                                          ALU.mult, ALU.add)
                    last.then_inc(mix_done, 1)
                elif kind == "rk":
                    rest(kind, b)
                elif kind == "g1":
                    key = ("g1", "g", b)
                    g = bank(*key)[:, :].rearrange("p (k t) -> p k t", k=NB)
                    bank_full(dve, *key)
                    if b >= 1:
                        dve.wait_ge(gated, b)
                    V.tensor_scalar(sgate, g, LOWEST, None, ALU.max).then_inc(clamped_g, 1)
                elif kind == "gate":
                    key = ("g1", "g", b)
                    g = bank(*key)[:, :].rearrange("p (k t) -> p k t", k=NB)
                    dve.wait_ge(sig_g, b + 1)
                    V.tensor_tensor(sgate, sgate, g, ALU.mult).then_inc(read(*key), 1)
                elif kind == "wmask":
                    dve.wait_ge(wtri_done, i + 1)
                    w = wmask[:, GH * i:GH * i + GH, 0:P]
                    for h in range(GH):
                        last = V.scalar_tensor_tensor(w[:, h], ident, rows[:, FA_COL + GH * i + h:FA_COL + GH * i + h + 1],
                                                      w[:, h], ALU.mult, ALU.add)
                    last.then_inc(wmask_done, 1)
                elif kind == "score":
                    u, g = divmod(i, 4)
                    slot_full(dve, "score", i)
                    if u < 2:
                        dve.wait_ge(wmask_done, i + 1)
                    if u >= 2 and g == 0:
                        bank_full(dve, "Y", "y", u - 2)
                    src, dst = slot("score", i), masked[:, u % 2, GH * g:GH * g + GH]
                    w = wmask[:, 16 * (u % 2) + GH * g:16 * (u % 2) + GH * g + GH]
                    V.tensor_tensor(dst[:, :, 0:T], src[:, 0:SA].rearrange("p (h t) -> p h t", h=GH), w, ALU.mult)
                    V.tensor_tensor(dst[:, :, T:T + P], src[:, SA:SW].rearrange("p (h t) -> p h t", h=GH),
                                    w[:, :, 0:P], ALU.mult).then_inc(slot_read("score", i), 1)
                elif kind == "var":
                    dve.wait_ge(newton_in, b + 1)
                    sq, r = tmpn[:, 0], tmpn[:, 1]
                    key = ("var", "v", b)
                    V.scalar_tensor_tensor(sq, bank(*key)[:, :], EPS1, sq, ALU.add, ALU.mult).then_inc(read(*key), 1)
                    bank_done(dve, *key)
                    link(V.scalar_tensor_tensor(r, sq, 3.0, r, ALU.subtract, ALU.mult))
                    for k in range(NB):
                        last = V.scalar_tensor_tensor(cent[:, k], cent[:, k], gam2[:, k:k + 1],
                                                      tmpn[:, 1, k * T:(k + 1) * T], ALU.mult, ALU.mult)
                    link(last)
                    for k in range(NB):
                        last = V.scalar_tensor_tensor(cent[:, k], cent[:, k], bet[:, k:k + 1], sgate[:, k],
                                                      ALU.add, ALU.mult)
                    last.then_inc(gated, 1)
                elif kind == "out1":
                    key = ("out1", "y", b)
                    bank_full(dve, *key)
                    V.tensor_tensor(x[:, b], x[:, b], bank(*key)[:, :].rearrange("p (k t) -> p k t", k=NB),
                                    ALU.add).then_inc(read(*key), 1)
                    bank_done(dve, *key)
                    clamp(3 * B + b)
                elif kind == "fp8":
                    dve.wait_ge(scaled8, b + 1)
                    whole, half = tmpn[:, 0], tmpn[:, 1]
                    V.tensor_scalar(q8[:, 0], whole, 128.0, -128.0, ALU.min, ALU.max, saturate=False)
                    link(V.tensor_scalar(q8[:, 1], half, FP8_HALF, -FP8_HALF, ALU.min, ALU.max, saturate=False))
                    link(V.tensor_scalar(whole, q8[:, 1], 64.0, -64.0, ALU.min, ALU.max))
                    link(V.tensor_tensor(half, q8[:, 1], whole, ALU.subtract))
                    if b:
                        bank_full(dve, "last", "y", b - 1)
                    V.scalar_tensor_tensor(qbf[:, :, :].rearrange("p k t -> p (k t)"), half, 2.0, q8[:, 0],
                                           ALU.mult, ALU.add).then_inc(q8_ready, 1)
                elif kind == "last":
                    key = ("last", "y", b)
                    bank_full(dve, *key)
                    V.scalar_tensor_tensor(x[:, b], bank(*key)[:, :].rearrange("p (k t) -> p k t", k=NB), oscale,
                                           x[:, b], ALU.mult, ALU.add).then_inc(read(*key), 1)


def by_partition(a):
    return a.reshape(NB, P, -1).transpose(1, 0, 2)


def host_arrays(i):
    h = {k: np.asarray(v) for k, v in i.items()}

    def activations(a):
        return a.transpose(2, 0, 1).reshape(NB, P, B, T).transpose(1, 2, 0, 3)

    def order(heads, width):
        return np.concatenate([k * P + np.arange(P).reshape(heads, width).T.ravel() for k in range(NB)])

    q0 = np.arange(C).reshape(8, NB, D0).transpose(1, 2, 0).ravel()
    r1 = order(16, D1)
    mats = [h["L0_attn_Wq"][q0], h["L0_attn_Wk"][q0], h["L0_attn_Wv"], h["L0_attn_Wo"], h["L0_ffn_w3"],
            h["L1_attn_Wr"][r1], h["L1_attn_Wk"][r1], h["L1_attn_Wv"], h["L1_attn_Wg"], h["L1_attn_Wo"]]
    weights = np.stack([by_partition(m.T).reshape(P, NB * C) for m in mats], axis=1)
    cols = [h[f"{n}_{w}"] for w in "wu" for n in ("L0_cond", "L0_cond2", "L1_cond", "L1_cond2")]
    cols += [h[f"L1_attn_time_maa_{n}"].reshape(C) for n in "kvrg"]
    cols += [h["L1_attn_gamma"], h["L1_attn_beta"], h["L0_ffn_b3"]]
    vecs = np.concatenate([c.reshape(NB, P).T for c in cols], axis=1)
    row = np.concatenate([h["cond_512"].ravel(), h["L0_ffn_switch_b"], h["L1_attn_time_decay"].ravel(),
                          h["L1_attn_time_faaaa"].ravel(), h["L1_ffn_weight_scale"].reshape(1)])
    sw = h["L0_ffn_switch_w"].reshape(E, 8, 32, NB, P)
    bank = np.concatenate([h["L0_ffn_w1"].transpose(2, 0, 1), h["L0_ffn_b1"].T[:, :, None],
                           h["L0_ffn_w2"].transpose(2, 0, 1), h["L0_ffn_b2"].T[:, :, None]], axis=2)
    t = np.arange(P)
    same = t[:, None] // D1 == t[None, :] // D1
    negd = -np.maximum(np.arange(T)[None, :] - t[:, None] - 1, 0)
    hmask = np.arange(32)[None, :] // D1 == np.arange(GH)[:, None]
    made = {"ident": np.eye(P), "center": np.eye(P) - same / D1, "mean8": same / D1, "ones": np.ones((P, P)),
            "tri": t[None, :] > t[:, None], "negd": negd, "diagm": t[:, None] % 32 == np.arange(32)[None, :],
            "hmask": np.broadcast_to(hmask.reshape(1, P), (P, P)),
            "bdm": t[:, None] // DH == np.arange(8)[None, :],
            "rev": np.broadcast_to(E - np.arange(E), (P, E)), "eps": np.full((P, 1), EPS1),
            "zero": np.zeros((P, 1))}
    bf16 = mybir.dt.np(BF16)
    later = np.where(t[None, :] > t[:, None], NEG, 0.0)
    out = {
        "x": activations(h["x"]), "fside": activations(h["fside_BxSxS_0"]), "weights": weights, "vecs": vecs,
        "rows": np.tile(row[None, :], (P, 1)), "switch": sw.transpose(4, 3, 1, 0, 2).reshape(P, -1),
        "expert": np.tile(bank, (8, 1, 1)), "w8": by_partition(h["L1_ffn_weight"].view(np.uint8).T).reshape(P, -1),
        "iscale": np.tile(h["L1_ffn_input_scale"].reshape(1, 1), (P, 1)),
        "consts": np.concatenate([made[n] for n in CONSTS], axis=1).astype(np.float32),
        "consts_bf16": np.concatenate([np.eye(P), later, later.T], axis=1).astype(bf16),
    }
    return {k: np.ascontiguousarray(v) for k, v in out.items()}


def kernel(**inputs):
    import concourse.bacc as bacc
    from concourse.bass_utils import run_bass_kernel_spmd

    arrays = host_arrays(inputs)
    nc = bacc.Bacc("TRN2", target_bir_lowering=False, num_devices=1)
    d = {k: nc.dram_tensor(f"in_{k}", a.shape, mybir.dt.from_np(a.dtype), kind="ExternalInput").ap()
         for k, a in arrays.items()}
    d["out"] = nc.dram_tensor("out", (P, B, NB, T), F32, kind="ExternalOutput").ap()
    build(nc, d)
    result = run_bass_kernel_spmd(nc, [{f"in_{k}": a for k, a in arrays.items()}], core_ids=[0])
    out = result.results[0]["out"]
    return out.transpose(1, 3, 2, 0).reshape(B, T, C)
```

```python
from contextlib import ExitStack

import numpy as np

import concourse.bass as bass
from concourse import mybir

F32 = mybir.dt.float32
BF16 = mybir.dt.bfloat16
F16 = mybir.dt.float16
FP8 = mybir.dt.float8e4
U8 = mybir.dt.uint8
U16 = mybir.dt.uint16
ALU = mybir.AluOpType
ACT = mybir.ActivationFunctionType
X = mybir.AxisListType.X

P = 128
B, T, C = 4, 256, 256
NB = C // P
TB = T // P
N = NB * T
NEG = -3.0e38

H0, D0 = 16, 16
H1, D1 = 32, 8
EPS1 = 1e-05 * 144
SPLIT_Q = (0, 0, 1, 1, 0, 2)
SPLIT_K = (0, 1, 0, 1, 2, 0)
NPROD = len(SPLIT_Q)
KROWS = 72
SROWS = NPROD * D0
GH = 4
SA = GH * T
SW = SA + GH * P

E, DH = 8, 16
EB = 2 * DH + 2
ON_VECTOR = 1
LOWEST = -40.0
EXP_LN_SET, GELU_SET = 6, 10
TWO_ONES = float(np.array([0x3F803F80], np.uint32).view(np.float32)[0])
FP8_HALF = 448.0 / 2

W_COL = {l: 2 * l for l in range(4)}
U_COL = {l: 8 + 2 * l for l in range(4)}
MAA_COL = {"k": 16, "v": 18, "r": 20, "g": 22}
GAMMA_COL, BETA_COL, B3_COL, DECAY_COL = 24, 26, 28, 30
NVEC = 32
COND_COL, SWB_COL, TD_COL, FA_COL, WS_COL = 0, 256, 264, 296, 328
NROW = 329
CONSTS = {"ident": P, "center": P, "mean8": P, "ones": P, "tri": P, "negd": P, "negi": P, "smask": P, "negj": 1,
          "diagm": 32, "hmask": P, "bdm": 8, "rev": E, "eps": 1, "zero": 1}
CONST_AT = dict(zip(CONSTS, np.cumsum([0] + list(CONSTS.values())).tolist()))
NCONST = sum(CONSTS.values())
MATS = ["q0", "k0", "v0", "o0", "w3", "r1", "k1", "v1", "g1", "o1"]


AFTER_SCORES = ("exp1", "exp2", "w3", "rk", "kt", "state", "v1", "g1", "Y", "norm", "var", "out1", "last")


ORDER = """
condA:0 clamp:0 seq:1 condB:0 clamp:1 seq:2 condN:0 condC:0 z:0 seq:3 condA:1 qk:0 condB:1 condN:1 condA:2
condC:1 z:1 condA:3 qk:1 S:0 condB:2 S:1 v:0 clamp:2 S:2 clamp:3 condN:2 S:3 condC:2 z:2 v:1 condB:3 mx:0
condN:3 mt:0 condA:4 condC:3 z:3 qk:2 S:4 S:5 condB:4 S:6 ST:0 condN:4 condA:5 ST:1 av:0 condC:4 ST:2 S:7 av:1
av:2 ST:3 mx:1 condA:6 mt:1 av:3 condB:5 condN:5 post:0 condB:6 condC:5 ST:4 condN:6 condA:7 qk:3 S:8 S:9 z:4
v:2 ST:5 av:4 condC:6 condB:7 S:10 condN:7 av:5 condA:8 ST:6 S:11 ST:7 condC:7 av:6 mx:2 condA:9 av:7 mt:2
condB:8 post:1 condB:9 condN:8 condN:9 condC:8 condA:10 ST:8 S:12 z:5 lg:0 S:13 ST:9 condC:9 condA:11 lg:1
av:8 ST:10 condB:10 S:14 av:9 ST:11 S:15 condN:10 av:10 av:11 condB:11 condN:11 mx:3 condC:10 condA:12 mt:3
v:3 post:2 condB:12 condC:11 ST:12 condN:12 condA:13 ST:13 ST:14 av:12 av:13 scales:0 condC:12 ST:15 av:14
condA:14 av:15 condB:13 post:3 condN:13 z:6 condC:13 condA:15 z:7 lg:2 lg:3 condB:14 route:0 condN:14 pick:0
pick:1 exp1:0 condC:14 pick:2 exp2:0 pick:3 condB:15 w3:0 exp2:1 z:8 condN:15 exp1:1 condC:15 exp2:2 mix:0
w3:1 pads:0 exp2:3 w3:2 decay:0 rk:0 wmask:0 kt:0 wmask:1 wmask:2 v1:0 z:9 g1:0 w3:3 score:0 gate:0 state:0
mix:1 score:1 wmask:3 wmask:4 z:10 score:2 wmask:5 wmask:6 rk:1 score:3 score:4 wmask:7 score:5 score:6 v1:1
score:7 kt:1 Y:0 score:8 score:9 z:11 state:1 Y:1 score:10 norm:0 score:11 score:12 var:0 g1:1 mix:2 Y:2
out1:0 score:13 gate:1 score:14 z:12 rk:2 score:15 fp8:0 v1:2 Y:3 kt:2 norm:1 var:1 last:0 g1:2 mix:3 score:16
out1:1 gate:2 score:17 rk:3 score:18 score:19 state:2 v1:3 score:20 score:21 kt:3 score:22 z:13 score:23 fp8:1
Y:4 Y:5 score:24 score:25 norm:2 state:3 score:26 score:27 var:2 score:28 g1:3 score:29 out1:2 score:30
score:31 z:14 gate:3 fp8:2 Y:6 Y:7 last:1 norm:3 last:2 var:3 out1:3 z:15 fp8:3 last:3
"""
STEPS = [(kind, int(i)) for kind, i in (step.split(":") for step in ORDER.split())]


def dense_plan():
    uses, used, last = {}, [0] * 4, [-4, -3, -2, -1]
    for kind, b in STEPS:
        names = {"qk": ["q", "k"], "v": ["v"], "mt": ["t"], "av": ["o"], "post": ["t0", "t1", "zT", "o"],
                 "lg": ["g"], "route": ["b"], "exp1": ["h00", "h01", "h10", "h11"], "exp2": ["o"], "w3": ["y"],
                 "rk": ["r", "k"], "kt": ["k"], "state": ["s"], "v1": ["v"], "g1": ["g"],
                 "Y": ["y"], "norm": ["c"], "var": ["v"],
                 "out1": ["y"], "last": ["y"]}.get(kind, [])
        for n in names:
            i = min(range(4 if kind in AFTER_SCORES else 2), key=lambda i: last[i])
            uses[(kind, n, b)] = (i, used[i])
            used[i], last[i] = used[i] + 1, len(uses)
    return uses


def score_plan():
    uses = {}
    for kind, b in STEPS:
        if kind in ("S", "ST", "score"):
            uses[(kind, b)] = len(uses)
    return uses


Z_AT = {i: n + 1 for n, i in enumerate(i for kind, i in STEPS if kind == "z")}
CLIP_AT = {s: n + 2 for n, s in enumerate(s for s in STEPS if s[0] in ("seq", "condA"))}
DENSE = dense_plan()
SCORE = score_plan()


def build(nc, d):
    with ExitStack() as ctx:
        def sb(name, shape, dt=F32):
            return ctx.enter_context(nc.sbuf_tensor(name, shape, dt))

        def sem(name):
            return ctx.enter_context(nc.semaphore(name))

        x = sb("x", [P, B, NB, T])
        wall = sb("weights", [P, 5, NB * C])
        consts = sb("consts", [P, NCONST])
        cbf = sb("consts_bf16", [P, 3 * P], BF16)
        vecs = sb("vecs", [P, NVEC])
        rows = sb("rows", [P, NROW])
        iscale_bf = sb("iscale_bf", [P, 1], BF16)
        early = sb("early", [P, 2 * 16 * (T + P)])
        mid = sb("mid", [P, 8192])

        def part(region, at, pattern, **dims):
            n = dims.pop("n")
            return region[:, at:at + n].rearrange(pattern, **dims)

        fk = part(early, 0, "p (b k t) -> p b k t", n=B * N, b=B, k=NB)
        seq = part(early, 2048, "p (b k m t) -> p b k m t", n=2 * B * N, b=B, k=NB, m=2)
        fwd = [part(early, at, "p (k m t) -> p k m t", n=2 * N, k=NB, m=2) for at in (6144, 11264)]
        bwd = [part(region, at, "p (k m t) -> p k m t", n=2 * N, k=NB, m=2)
               for region, at in ((early, 7168), (mid, 7168))]
        total = part(early, 8192, "p (r k m t) -> p r k m t", n=4 * N, r=2, k=NB, m=2)
        rec = part(early, 10752, "p (k t) -> p k t", n=N, k=NB)
        masked = part(early, 0, "p (r h s n) -> p r h s n", n=8192, r=2, h=16, s=TB)
        rdec = part(early, 8192, "p (r k n) -> p r k n", n=2 * NB * P, r=2, k=NB)
        kdec = early[:, 8704:8960]
        state = part(early, 8960, "p (r k n) -> p r k n", n=2 * NB * P, r=2, k=NB)
        wp = part(early, 9472, "p (k n) -> p k n", n=NB * P, k=NB)
        vsb = part(early, 9728, "p (s c) -> p s c", n=N, s=TB)
        sw = part(mid, 0, "p (k c e t) -> p k c e t", n=4096, k=NB, c=8, e=E)
        probs = part(mid, 4096, "p (r n) -> p r n", n=2 * SW, r=2)
        gel = part(mid, 4096, "p (r w n) -> p r w n", n=4 * N, r=2, w=2)
        wmask = part(mid, 0, "p (h t) -> p h t", n=H1 * P, h=H1)
        lgr, pr, t8, t9 = (part(early, 10240 + 32 * n, "p (b e) -> p b e", n=B * E, b=B) for n in range(4))
        oh = part(early, 10240 + 32 * 4, "p (k b e) -> p k b e", n=2 * B * E, k=2, b=B)
        s1, s2, s3 = (early[:, 10432 + B * n:10432 + B * (n + 1)] for n in range(3))
        gt = part(early, 10448, "p (k b) -> p k b", n=2 * B, k=2)
        ratio = sb("ratio", [P, 8, NB, T])
        zbuf = sb("zbuf", [P, B, NB, T])
        qst = sb("q_stack", [P, 2, 16, T], BF16)
        kst = sb("k_stack", [P, 2, 16, T], BF16)
        split = sb("split", [P, 2, 3, N], BF16)
        resid = sb("resid", [P, 2, N])
        vbuf = sb("vbuf", [P, 2048])
        vaug = part(vbuf, 0, "p (r s h d) -> p r s h d", n=2048, r=2, s=TB, h=H0)
        vm = [a.rearrange("p (s g e c) -> p s g e c", s=TB, g=8, e=GH)
              for a in (vbuf[:, 0:2048], ratio[:, 0:4].rearrange("p r k t -> p (r k t)"))]
        misc = sb("misc", [P, 3584])
        zaug = part(misc, 0, "p (g t) -> p g t", n=1024, g=4)
        znrm = part(misc, 1024, "p (s c) -> p s c", n=N, s=TB)
        zoT = part(misc, 1536, "p (k t) -> p k t", n=N, k=NB)
        bd = part(misc, 2048, "p (r k w c) -> p r k w c", n=1024, r=2, k=2, w=2)
        mixb = part(misc, 0, "p (m k t) -> p m k t", n=4 * N, m=4, k=NB)
        diff = part(misc, 2048, "p (k t) -> p k t", n=N, k=NB)
        ysb = part(misc, 2560, "p (k t) -> p k t", n=N, k=NB)
        sgate = part(misc, 3072, "p (k t) -> p k t", n=N, k=NB)
        pair = sb("pair", [P, 2 * EB * E])
        esel = part(pair, 0, "p (k c e) -> p k c e", n=2 * EB * E, k=2, e=E)
        lmask = part(pair, 0, "p (e t) -> p e t", n=T, e=E)
        cent = part(pair, 0, "p (k t) -> p k t", n=N, k=NB)
        tmpn = sb("tmpn", [P, 2, N])
        w16 = [tmpn[:, i, 0:N // 2].bitcast(U16) for i in range(2)]
        w8 = tmpn[:, 1, N // 2:N // 2 + N // 4].bitcast(U8)
        expert = sb("expert", [P, E, EB])
        ew = sb("ew", [P, 2, 2, EB])
        small = sb("small", [P, 256])
        mxs = sb("mxs", [P, 2, TB, H0])
        msp = sb("msp", [P, 2, TB, 3, H0], BF16)
        mT = sb("mT", [3 * H0, 2, T], BF16)
        wbf = sb("wbf", [P, NB, C], BF16)
        q8 = sb("q8", [P, 2, N], FP8)
        qbf = sb("qbf", [P, NB, T], BF16)

        dense = [ctx.enter_context(nc.psum_tensor(f"dense{i}", [P, 512], F32)) for i in range(2)]
        score = [ctx.enter_context(nc.psum_tensor(f"score{i}", [P, SW], F32)) for i in range(2)]
        dense += [s[:, SA:SW] for s in score]

        place = {}

        def numbers(name, n):
            at = sum(place.values())
            place[name] = n
            return small[:, at:at + n]

        csum, dfac = (numbers(n, B) for n in ("csum", "dfac"))
        gain = numbers("gain", B)
        cw = numbers("cw", 2 * 4)
        dw = numbers("dw", 2 * 4)
        dec = numbers("dec", 8 * B).rearrange("p (b w) -> p b w", b=B)
        lam = numbers("lam", H1)
        lamc = numbers("lamc", NB)
        dk = numbers("dk", H1)
        rscale, rhalf, oscale, iscale = (numbers(n, 1) for n in ("rscale", "rhalf", "oscale", "iscale"))
        gam2, bet = numbers("gam2", NB), numbers("bet", NB)
        rden = numbers("rden", TB * H0).rearrange("p (s h) -> p s h", s=TB)
        mres = numbers("mres", TB * H0).rearrange("p (s h) -> p s h", s=TB)
        b2s = numbers("b2s", B)

        def mat(name):
            return wall[:, MATS.index(name) % 5, :].rearrange("p (k o) -> p k o", k=NB)

        def const(name):
            return consts[:, CONST_AT[name]:CONST_AT[name] + CONSTS[name]]

        def vec(col, k):
            return vecs[:, col + k:col + k + 1]

        def outer(ap, n):
            return ap.unsqueeze(1).to_broadcast([ap.shape[0], n, ap.shape[1]])

        def inner(ap, n):
            return ap.unsqueeze(2).to_broadcast([ap.shape[0], ap.shape[1], n])

        ident = const("ident")
        identb = cbf[:, 0:P]
        maskb = cbf[:, P:2 * P]
        maskTb = cbf[:, 2 * P:3 * P]

        names = """in_vecs in_consts in_qkv in_rest in_switch in_later in_out1
        clipped seq_ready csum_done thc_done clamped clamped_g dw_done ek_raw euk_raw eu_ready scan_done
        pool_sum tot_ready den_max
        rec_ready rec_used ratio_ready sig_ready z_ready part1 part2 part3 m_split pads_set
        lgr_ready logits_ready exps_done gates_picked bd_ready lam_ready decay_ready wexp_done wtri_done wmask_done
        diff_done mix_done vm_ready squared newton_in sig_g gated scaled8 q8_ready out_in
        vec_step act_step""".split()
        (in_vecs, in_consts, in_qkv, in_rest, in_switch, in_later, in_out1,
         clipped, seq_ready, csum_done, thc_done, clamped, clamped_g, dw_done, ek_raw, euk_raw, eu_ready, scan_done,
         pool_sum, tot_ready, den_max,
         rec_ready, rec_used, ratio_ready, sig_ready, z_ready, part1, part2, part3, m_split, pads_set,
         lgr_ready, logits_ready, exps_done, gates_picked, bd_ready, lam_ready, decay_ready, wexp_done, wtri_done,
         wmask_done,
         diff_done, mix_done, vm_ready, squared, newton_in, sig_g, gated, scaled8, q8_ready, out_in,
         vec_step, act_step) = (sem(n) for n in names)
        in_fside = [sem(f"in_fside{b}") for b in range(B)]
        in_x = [sem(f"in_x{b}") for b in range(B)]
        m_in = [sem(f"m_in{i}") for i in range(2)]
        stack_in = [sem(f"stack_in{i}") for i in range(2)]
        dense_full = [sem(f"dense_full{i}") for i in range(4)]
        dense_read = [sem(f"dense_read{i}") for i in range(4)]
        score_full = [sem(f"score_full{i}") for i in range(2)]
        score_read = [sem(f"score_read{i}") for i in range(2)]

        def bank(*key):
            return dense[DENSE[key][0]]

        def bank_free(pe, *key):
            i, n = DENSE[key]
            if n:
                pe.wait_ge(dense_read[i], n)
            elif i >= 2:
                slot_done(pe, *max((k for k in SCORE if k[0] != "score" and SCORE[k] % 2 == i - 2), key=SCORE.get))

        def bank_full(eng, *key):
            i, n = DENSE[key]
            eng.wait_ge(dense_full[i], n + 1)

        def full(*key):
            return dense_full[DENSE[key][0]]

        def read(*key):
            return dense_read[DENSE[key][0]]

        def slot(*key):
            return score[SCORE[key] % 2]

        def slot_filled(*key):
            return score_full[SCORE[key] % 2]

        def slot_read(*key):
            return score_read[SCORE[key] % 2]

        def slot_free(pe, *key):
            n = SCORE[key]
            if n >= 2:
                pe.wait_ge(score_read[n % 2], n // 2)

        def slot_full(eng, *key):
            n = SCORE[key]
            eng.wait_ge(score_full[n % 2], n // 2 + 1)

        def bank_done(eng, *key):
            i, n = DENSE[key]
            eng.wait_ge(dense_read[i], n + 1)

        def slot_done(eng, *key):
            n = SCORE[key]
            eng.wait_ge(score_read[n % 2], n // 2 + 1)

        def stacks_in(eng, kind, b):
            slot = b % 2
            eng.wait_ge(stack_in[slot], 16 * 2 * NPROD * ((0 if kind == "S" else 2) + b // 2 + 1))

        block = ctx.enter_context(nc.Block())

        @block.sync
        def _(sp):
            sp.dma_start(fk[:, 0], d["fside"][:, 0]).then_inc(in_fside[0], 16)
            sp.dma_start(rows[:], d["rows"]).then_inc(in_vecs, 16)
            sp.dma_start(vecs[:], d["vecs"]).then_inc(in_vecs, 16)
            for b in range(B):
                if b:
                    sp.dma_start(fk[:, b], d["fside"][:, b]).then_inc(in_fside[b], 16)
                sp.dma_start(x[:, b], d["x"][:, b]).then_inc(in_x[b], 16)
            sp.dma_start(wall[:, 0:3], d["weights"][:, 0:3]).then_inc(in_qkv, 16)
            sp.dma_start(cbf[:], d["consts_bf16"]).then_inc(in_consts, 16)
            sp.dma_start(consts[:], d["consts"]).then_inc(in_consts, 16)
            sp.dma_start(wall[:, 3:5], d["weights"][:, 3:5]).then_inc(in_rest, 16)
            sp.dma_start(expert[:], d["expert"]).then_inc(in_rest, 16)
            sp.dma_start(iscale_bf[:], d["iscale"]).then_inc(in_rest, 16)
            sp.dma_start(w8, d["w8"]).then_inc(in_rest, 16)
            sp.dma_start(mid[:, 0:4096], d["switch"]).then_inc(in_switch, 16)

            def stack(which, slot, width, cols):
                for r, (dst, parts) in enumerate([(qst, SPLIT_Q), (kst, SPLIT_K)]):
                    sp.wait_ge(part3, which + r + 1)
                    for n, j in enumerate(parts):
                        sp.dma_start(dst[width * n:width * (n + 1), slot, :, :],
                                     split[:, r, j, cols]).then_inc(stack_in[slot], 16)

            for kind, b in STEPS:
                if kind == "qk":
                    if b >= 2:
                        slot_full(sp, "ST", 4 * (b - 2) + 3)
                    stack(2 * b, b % 2, D0, slice(0, N))
                elif kind == "mt":
                    bank_done(sp, "mt", "t", b)
                    sp.dma_start(qst[SROWS:SROWS + 3, b % 2, :, :], mT[:, b % 2, :]).then_inc(m_in[b % 2], 16)
                elif kind == "rk":
                    for blk in range(NB):
                        if b == 0:
                            slot_full(sp, "ST", 4 * (2 + blk) + 3)
                            sp.wait_ge(pads_set, 4)
                        else:
                            slot_full(sp, "score", 4 * (2 * (b - 1) + blk) + 3)
                        stack(8 + 2 * b, blk, D1, slice(blk * T, (blk + 1) * T))
                elif kind == "post" and b == 3:
                    bank_full(sp, "post", "o", 3)
                    sp.dma_start(wall[:, 0:4], d["weights"][:, 5:9]).then_inc(in_later, 16)
                elif kind == "w3" and b == 3:
                    bank_full(sp, "w3", "y", 3)
                    sp.dma_start(wall[:, 4:5], d["weights"][:, 9:10]).then_inc(in_out1, 16)
                elif kind == "last":
                    bank_done(sp, "last", "y", b)
                    sp.dma_start(d["out"][:, b], x[:, b]).then_inc(out_in, 16)
            sp.wait_ge(out_in, 16 * B)

        @block.gpsimd
        def _(pool):
            nc.gpsimd.memset(bwd[0][:, :, :, T - 1:T], 0.0)
            nc.gpsimd.memset(bwd[1][:, :, :, T - 1:T], 0.0)
            nc.gpsimd.memset(vaug[:, :, :, :, D0:2 * D0], 1.0).then_inc(pads_set, 1)
            pool.wait_ge(pads_set, 1)
            nc.gpsimd.memset(kst[SROWS:SROWS + 3, :, :, :].rearrange("p r h t -> p (r h t)").bitcast(F32),
                             TWO_ONES).then_inc(pads_set, 1)
            pool.wait_ge(pads_set, 2)

            def values(b):
                pool.wait_ge(ek_raw, b + 1)
                nc.gpsimd.tensor_tensor(seq[:, b, :, 0], seq[:, b, :, 1], fk[:, b], ALU.mult).then_inc(seq_ready, 1)

            values(0)
            for kind, i in STEPS:
                b = i
                if kind == "seq":
                    values(b)
                elif kind == "condA":
                    n = i % 2
                    pool.wait_ge(euk_raw, i + 1)
                    nc.gpsimd.tensor_tensor(total[:, n, :, 0], total[:, n, :, 1], fk[:, i % B],
                                            ALU.mult).then_inc(eu_ready, 1)
                    if i < ON_VECTOR:
                        continue
                    pool.wait_ge(scan_done, i + 1)
                    f = fwd[i % 2]
                    nc.gpsimd.tensor_tensor(f, f, bwd[i % 2], ALU.add).then_inc(pool_sum, 1)
                    pool.wait_ge(pool_sum, i + 1 - ON_VECTOR)
                    pool.wait_ge(eu_ready, i + 1)
                    nc.gpsimd.tensor_tensor(total[:, i % 2], total[:, i % 2], f, ALU.add).then_inc(tot_ready, 1)
                elif kind == "condN" and i >= ON_VECTOR:
                    pool.wait_ge(rec_ready, i + 1)
                    num, den = total[:, i % 2, :, 0], total[:, i % 2, :, 1]
                    nc.gpsimd.tensor_tensor(num, num, rec, ALU.mult)
                    nc.gpsimd.tensor_tensor(den, den, rec, ALU.mult).then_inc(rec_used, 1)
                elif kind in ("qk", "rk"):
                    for w in range(2):
                        n = 2 * b + w + (8 if kind == "rk" else 0)
                        pool.wait_ge(part2, n + 1)
                        nc.gpsimd.tensor_tensor(split[:, w, 2], resid[:, w], split[:, w, 1],
                                                ALU.subtract).then_inc(part3, 1)
                elif kind == "pick":
                    if b == 0:
                        pool.wait_ge(in_consts, 32)
                    pool.wait_ge(gates_picked, b + 1)
                    if b >= 2:
                        bank_full(pool, "exp2", "o", b - 2)
                    for k in range(2):
                        for w, at in ((0, 0), (1, DH + 1)):
                            last = nc.gpsimd.tensor_tensor(
                                bd[:, b % 2, k, w].rearrange("p (h c) -> p h c", h=8),
                                outer(ew[:, b % 2, k, at:at + DH], 8), inner(const("bdm"), DH), ALU.mult)
                    last.then_inc(bd_ready, 1)
                elif kind == "mix":
                    z = zbuf[:, b]
                    pool.wait_ge(z_ready, Z_AT[2 * B + b])
                    if b:
                        pool.wait_ge(mix_done, b)
                    else:
                        bank_done(pool, "exp2", "o", 2)
                    nc.gpsimd.tensor_tensor(diff[:, :, 1:T], z[:, :, 0:T - 1], z[:, :, 1:T], ALU.subtract)
                    nc.gpsimd.tensor_tensor(diff[:, :, 0:1], outer(const("zero"), NB), z[:, :, 0:1],
                                            ALU.subtract).then_inc(diff_done, 1)
                elif kind == "wmask":
                    pool.wait_ge(wexp_done, i + 1)
                    w = wmask[:, GH * i:GH * i + GH, 0:P]
                    nc.gpsimd.tensor_tensor(w, w, outer(const("tri"), GH), ALU.mult).then_inc(wtri_done, 1)
                elif kind == "pads":
                    pool.wait_ge(tot_ready, 4 * B - ON_VECTOR)
                    pool.wait_ge(bd_ready, B)
                    pool.wait_ge(rec_used, 4 * B)
                    pool.wait_ge(diff_done, 1)
                    for u in (2, 3):
                        slot_full(pool, "ST", 4 * u + 3)
                    for p in (32, 64):
                        nc.gpsimd.memset(kst[p:p + 32, :, :, :].rearrange("p r h t -> p (r h t)").bitcast(F32),
                                         0.0).then_inc(pads_set, 1)
                        pool.wait_ge(pads_set, 2 + p // 32)
                elif kind == "v1":
                    bank_done(pool, "v1", "v", b)
                    if b == 1:
                        pool.wait_ge(z_ready, max(Z_AT[2 * B + n] for n in range(B)))
                    if b >= 2:
                        bank_full(pool, "Y", "y", 2 * b - 3)
                    for s in range(TB):
                        for e in range(GH):
                            last = nc.gpsimd.tensor_tensor(
                                vm[b % 2][:, s, :, e, :], vsb[:, s].rearrange("p (g c) -> p g c", g=8),
                                outer(const("hmask")[:, 32 * e:32 * e + 32], 8), ALU.mult)
                    last.then_inc(vm_ready, 1)

        @block.scalar
        def _(act):
            steps = [0]

            def link(ins):
                steps[0] += 1
                ins.then_inc(act_step, 1)
                act.wait_ge(act_step, steps[0])

            def load_exp_ln():
                nc.scalar.add_instruction(mybir.InstLoadActFuncSet(name=nc.get_next_instruction_name(),
                                                                   act_func_set_id=EXP_LN_SET))

            def sigmoid(v):
                link(nc.scalar.activation(v, v, ACT.Exp, scale=-1.0))
                link(nc.scalar.activation(v, v, ACT.Ln, bias=1.0))
                return nc.scalar.activation(v, v, ACT.Exp, scale=-1.0)

            load_exp_ln()
            act.wait_ge(clipped, 1)
            nc.scalar.activation(seq[:, 0, :, 1], seq[:, 0, :, 0], ACT.Exp).then_inc(ek_raw, 1)
            act.wait_ge(csum_done, 1)
            sigmoid(csum).then_inc(thc_done, 1)
            link(nc.scalar.activation(dw, cw, ACT.Exp))
            nc.scalar.activation(dw, dw, ACT.Exp, scale=-1.0).then_inc(dw_done, 1)
            nc.scalar.activation(lamc, lamc, ACT.Exp)
            nc.scalar.activation(lam, lam, ACT.Exp).then_inc(dw_done, 1)
            def copy_parts(kind, b):
                names = ("q", "k") if kind == "qk" else ("r", "k")
                for w in range(2):
                    n = 2 * b + w + (8 if kind == "rk" else 0)
                    key = (kind, names[w], b)
                    bank_full(act, *key)
                    before = n // 2
                    if before:
                        for slot in range(2):
                            done = (before + 1 - slot) // 2 if before <= 4 else before - 2
                            if done:
                                act.wait_ge(stack_in[slot], 16 * 2 * NPROD * done)
                    nc.scalar.activation(split[:, w, 0], bank(*key)[:, :], ACT.Copy).then_inc(part1, 1)
                for w in range(2):
                    n = 2 * b + w + (8 if kind == "rk" else 0)
                    bank_done(act, kind, names[w], b)
                    nc.scalar.activation(split[:, w, 1], resid[:, w], ACT.Copy).then_inc(part2, 1)

            for kind, i in STEPS:
                b = i
                if kind == "seq":
                    act.wait_ge(clipped, CLIP_AT["seq", b])
                    nc.scalar.activation(seq[:, b, :, 1], seq[:, b, :, 0], ACT.Exp).then_inc(ek_raw, 1)
                elif kind == "condA":
                    act.wait_ge(clipped, CLIP_AT["condA", i])
                    nc.scalar.activation(total[:, i % 2, :, 1], total[:, i % 2, :, 0], ACT.Exp).then_inc(euk_raw, 1)
                elif kind == "condB":
                    act.wait_ge(den_max, i + 1)
                    if i:
                        act.wait_ge(rec_used, i)
                    link(nc.scalar.activation(rec, total[:, i % 2, :, 1], ACT.Ln))
                    nc.scalar.activation(rec, rec, ACT.Exp, scale=-1.0).then_inc(rec_ready, 1)
                elif kind == "z":
                    act.wait_ge(clamped, i + 1)
                    sigmoid(zbuf[:, i % B]).then_inc(sig_ready, 1)
                elif kind == "qk":
                    copy_parts(kind, b)
                elif kind == "v":
                    bank_full(act, "v", "v", b)
                    if b >= 2:
                        bank_full(act, "av", "o", 4 * (b - 2) + 3)
                    nc.scalar.activation(vaug[:, b % 2, :, :, 0:D0],
                                         bank("v", "v", b)[:, :].rearrange("p (s h d) -> p s h d", s=TB, h=H0),
                                         ACT.Copy).then_inc(read("v", "v", b), 1)
                elif kind == "mt":
                    bank_full(act, "mt", "t", b)
                    if b >= 2:
                        act.wait_ge(m_in[b % 2], 16 * (b // 2))
                    nc.scalar.activation(mT[:, b % 2, :], bank("mt", "t", b)[0:48, 0:128].bitcast(BF16),
                                         ACT.Copy).then_inc(read("mt", "t", b), 1)
                elif kind == "ST":
                    slot_full(act, "ST", i)
                    if i >= 2:
                        bank_full(act, "av", "o", i - 2)
                    nc.scalar.activation(probs[:, i % 2], slot("ST", i)[:, :], ACT.Exp,
                                         scale=D0 ** -0.5).then_inc(slot_read("ST", i), 1)
                elif kind == "av":
                    key = ("av", "o", i)
                    bank_full(act, *key)
                    if i >= 4 and i % 4 == 0:
                        bank_full(act, "post", "t1", i // 4 - 1)
                    nc.scalar.activation(zaug[:, i % 4], bank(*key)[:, 0:T], ACT.Copy).then_inc(read(*key), 1)
                elif kind == "post":
                    bank_full(act, "post", "zT", b)
                    if b >= 1:
                        bank_full(act, "post", "o", b - 1)
                    nc.scalar.activation(zoT, bank("post", "zT", b)[:, :].rearrange("p (k t) -> p k t", k=NB),
                                         ACT.Copy).then_inc(read("post", "zT", b), 1)
                elif kind == "route":
                    act.wait_ge(logits_ready, 1)
                    nc.scalar.activation(pr, pr, ACT.Exp).then_inc(exps_done, 1)
                elif kind == "exp1":
                    nc.scalar.add_instruction(mybir.InstLoadActFuncSet(name=nc.get_next_instruction_name(),
                                                                       act_func_set_id=GELU_SET))
                    for b in (2 * i, 2 * i + 1):
                        if i:
                            bank_full(act, "exp2", "o", b - 2)
                        else:
                            bank_full(act, "av", "o", 4 * B - 1)
                        for k in range(2):
                            key = ("exp1", f"h{b % 2}{k}", i)
                            bank_full(act, *key)
                            nc.scalar.activation(gel[:, b % 2, k], bank(*key)[:, :], ACT.Gelu,
                                                 bias=ew[:, b % 2, k, DH:DH + 1]).then_inc(read(*key), 1)
                    load_exp_ln()
                elif kind == "wmask":
                    if i == 0:
                        act.wait_ge(lam_ready, 1)
                        act.wait_ge(in_consts, 32)
                        bank_full(act, "lg", "g", 3)
                    for h in range(GH * i, GH * i + GH):
                        last = nc.scalar.activation(wmask[:, h], const("negd"), ACT.Exp, scale=lam[:, h:h + 1])
                    last.then_inc(wexp_done, 1)
                elif kind == "rk":
                    copy_parts(kind, b)
                elif kind == "decay":
                    act.wait_ge(lam_ready, 1)
                    act.wait_ge(in_consts, 32)
                    act.wait_ge(ratio_ready, 4 * B)
                    for k in range(NB):
                        nc.scalar.activation(wp[:, k], const("negi"), ACT.Exp, scale=lamc[:, k:k + 1])
                    nc.scalar.activation(dk, lam, ACT.Exp, scale=const("negj")).then_inc(decay_ready, 1)
                elif kind == "v1":
                    bank_full(act, "v1", "v", b)
                    if b == 0:
                        act.wait_ge(ratio_ready, 4 * B)
                    else:
                        bank_full(act, "state", "s", b - 1)
                        act.wait_ge(vm_ready, b)
                    nc.scalar.activation(vsb[:, :, :], bank("v1", "v", b)[:, :].rearrange("p (s c) -> p s c", s=TB),
                                         ACT.Copy).then_inc(read("v1", "v", b), 1)
                elif kind == "g1":
                    act.wait_ge(clamped_g, b + 1)
                    sigmoid(sgate).then_inc(sig_g, 1)
                elif kind == "Y":
                    bank_full(act, "Y", "y", i)
                    if i >= 2 and i % 2 == 0:
                        bank_full(act, "norm", "c", i // 2 - 1)
                    nc.scalar.activation(ysb[:, i % 2], bank("Y", "y", i)[:, 0:T], ACT.Copy)\
                        .then_inc(read("Y", "y", i), 1)
                elif kind == "norm":
                    bank_full(act, "norm", "c", b)
                    if b >= 1:
                        act.wait_ge(q8_ready, b)
                        bank_full(act, "out1", "y", b - 1)
                    c = bank("norm", "c", b)
                    nc.scalar.activation(tmpn[:, 0], c[:, :], ACT.Square).then_inc(squared, 1)
                    nc.scalar.activation(cent, c[:, :].rearrange("p (k t) -> p k t", k=NB),
                                         ACT.Copy).then_inc(read("norm", "c", b), 1)
                elif kind == "var":
                    bank_full(act, "var", "v", b)
                    link(nc.scalar.activation(tmpn[:, 1], bank("var", "v", b)[:, :], ACT.Ln, bias=const("eps")))
                    link(nc.scalar.activation(tmpn[:, 1], tmpn[:, 1], ACT.Exp, scale=-0.5))
                    nc.scalar.activation(tmpn[:, 0], tmpn[:, 1], ACT.Square).then_inc(newton_in, 1)
                elif kind == "fp8":
                    act.wait_ge(z_ready, Z_AT[3 * B + b])
                    z = zbuf[:, b].rearrange("p k t -> p (k t)")
                    nc.scalar.activation(tmpn[:, 0], z, ACT.Copy, scale=rscale)
                    nc.scalar.activation(tmpn[:, 1], z, ACT.Copy, scale=rhalf).then_inc(scaled8, 1)

        @block.tensor
        def _(pe):
            def project(out, w, src):
                for o in range(NB):
                    for k in range(NB):
                        last = nc.tensor.matmul(out[:, o * T:(o + 1) * T], w[:, k, o * P:(o + 1) * P], src[:, k],
                                                start=(k == 0), stop=(k == NB - 1))
                return last

            def project_t(out, w, src):
                for s in range(TB):
                    for k in range(NB):
                        last = nc.tensor.matmul(out[:, s * C:(s + 1) * C], src[:, k, s * P:(s + 1) * P], w[:, k],
                                                start=(k == 0), stop=(k == NB - 1))
                return last

            def transposed_scores(out, kk, qq, mask):
                last = None
                for (o, w), (ks, qs) in zip(out, (((0, P), (0, T)), ((P, T), (P, T)))):
                    last = nc.tensor.matmul(o, kk[:, ks[0]:ks[1]], qq[:, qs[0]:qs[1]], start=True, stop=not mask)
                    if mask:
                        last = nc.tensor.matmul(w, identb, maskTb, start=False, stop=True)
                return last

            for kind, i in STEPS:
                b = i
                if kind == "qk":
                    pe.wait_ge(z_ready, Z_AT[b])
                    if b == 0:
                        pe.wait_ge(in_qkv, 16)
                    for n in ("q", "k"):
                        bank_free(pe, "qk", n, b)
                        project(bank("qk", n, b), mat(n + "0"), zbuf[:, b]).then_inc(full("qk", n, b), 1)
                elif kind == "v":
                    bank_free(pe, "v", "v", b)
                    project_t(bank("v", "v", b), mat("v0"), zbuf[:, b]).then_inc(full("v", "v", b), 1)
                elif kind == "S":
                    b, g = divmod(i, 4)
                    if g == 0:
                        stacks_in(pe, "S", b)
                    if i == 0:
                        pe.wait_ge(in_consts, 32)
                    slot_free(pe, "S", i)
                    out = slot("S", i)
                    for h in range(GH):
                        q, k = (st[0:SROWS, b % 2, GH * g + h] for st in (qst, kst))
                        for at, t0, w in ((h * T, P, T), (SA + h * P, 0, P)):
                            nc.tensor.matmul(out[:, at:at + w], q[:, t0:t0 + P], k[:, 0:w],
                                             start=True, stop=False)
                            last = nc.tensor.matmul(out[:, at + w - P:at + w], identb, maskb,
                                                    start=False, stop=True)
                    last.then_inc(slot_filled("S", i), 1)
                elif kind == "mt":
                    pe.wait_ge(m_split, b + 1)
                    bank_free(pe, "mt", "t", b)
                    out = bank("mt", "t", b)[0:48, 0:128].bitcast(BF16)
                    for s in range(TB):
                        last = nc.tensor.transpose(out[:, s * P:(s + 1) * P],
                                                   msp[:, b % 2, s].rearrange("p j h -> p (j h)"), identb)
                    last.then_inc(full("mt", "t", b), 1)
                elif kind == "ST":
                    b, g = divmod(i, 4)
                    if g == 0:
                        pe.wait_ge(m_in[b % 2], 16 * (b // 2 + 1))
                        pe.wait_ge(pads_set, 2)
                    slot_free(pe, "ST", i)
                    out = slot("ST", i)
                    for h in range(GH):
                        q, k = (st[0:SROWS + 3, b % 2, GH * g + h] for st in (qst, kst))
                        last = transposed_scores(
                            [(out[:, h * T:(h + 1) * T], out[:, h * T:h * T + P]),
                             (out[:, SA + h * P:SA + (h + 1) * P],) * 2], k, q, True)
                    last.then_inc(slot_filled("ST", i), 1)
                elif kind == "av":
                    b, g = divmod(i, 4)
                    if g == 0:
                        bank_done(pe, "v", "v", b)
                    slot_done(pe, "ST", i)
                    key = ("av", "o", i)
                    bank_free(pe, *key)
                    for s in range(TB):
                        for h in range(GH):
                            src = (probs[:, g % 2, h * T:(h + 1) * T] if s == 0 else
                                   probs[:, g % 2, SA + h * P:SA + (h + 1) * P])
                            last = nc.tensor.matmul(
                                bank(*key)[32 * h:32 * h + 32, s * P:T], vaug[:, b % 2, s, GH * g + h],
                                src, start=(s == 0), stop=(s == TB - 1), tile_position=(0, 32 * h))
                    last.then_inc(full(*key), 1)
                elif kind == "post":
                    for s in range(TB):
                        if s == 0:
                            for g in (2, 3):
                                bank_done(pe, "av", "o", 4 * b + g)
                        key = ("post", f"t{s}", b)
                        bank_free(pe, *key)
                        for g in range(4):
                            last = nc.tensor.transpose(bank(*key)[:, g * P:(g + 1) * P],
                                                       zaug[:, g, s * P:(s + 1) * P], ident)
                        last.then_inc(full(*key), 1)
                    bank_done(pe, "post", "t1", b)
                    bank_done(pe, "post", "t0", b)
                    bank_free(pe, "post", "zT", b)
                    for k in range(NB):
                        for s in range(TB):
                            last = nc.tensor.transpose(
                                bank("post", "zT", b)[:, k * T + s * P:k * T + (s + 1) * P],
                                znrm[:, s, k * P:(k + 1) * P], ident)
                    last.then_inc(full("post", "zT", b), 1)
                    if b == 0:
                        pe.wait_ge(in_rest, 64)
                    bank_done(pe, "post", "zT", b)
                    bank_free(pe, "post", "o", b)
                    project(bank("post", "o", b), mat("o0"), zoT).then_inc(full("post", "o", b), 1)
                elif kind == "lg":
                    pe.wait_ge(z_ready, Z_AT[B + b])
                    if b == 0:
                        pe.wait_ge(in_switch, 16)
                    bank_free(pe, "lg", "g", b)
                    out = bank("lg", "g", b)
                    for r in range(2):
                        for k in range(NB):
                            for j in range(4):
                                c = 4 * r + j
                                last = nc.tensor.matmul(
                                    out[32 * j:32 * j + 32, 0:T], zbuf[:, b, k, 32 * c:32 * c + 32],
                                    sw[:, k, c].rearrange("p e t -> p (e t)"),
                                    start=(r == 0 and k == 0), stop=(r == 1 and k == 1),
                                    tile_position=(0, 32 * j))
                    last.then_inc(full("lg", "g", b), 1)
                elif kind == "route":
                    pe.wait_ge(lgr_ready, B)
                    bank_free(pe, "route", "b", 0)
                    nc.tensor.matmul(bank("route", "b", 0)[:, 0:B * E], const("ones"),
                                     lgr.rearrange("p b e -> p (b e)"), start=True,
                                     stop=True).then_inc(full("route", "b", 0), 1)
                elif kind == "exp1":
                    for b in (2 * i, 2 * i + 1):
                        pe.wait_ge(bd_ready, b + 1)
                        for k in range(2):
                            key = ("exp1", f"h{b % 2}{k}", i)
                            bank_free(pe, *key)
                            nc.tensor.matmul(bank(*key)[:, :], bd[:, b % 2, k, 0],
                                             zbuf[:, b].rearrange("p k t -> p (k t)"),
                                             start=True, stop=True).then_inc(full(*key), 1)
                elif kind == "exp2":
                    bank_free(pe, "exp2", "o", b)
                    for k in range(2):
                        bank_done(pe, "exp1", f"h{b % 2}{k}", b // 2)
                        last = nc.tensor.matmul(bank("exp2", "o", b)[:, :], bd[:, b % 2, k, 1], gel[:, b % 2, k],
                                                start=(k == 0), stop=(k == 1))
                    last.then_inc(full("exp2", "o", b), 1)
                elif kind == "w3":
                    bank_done(pe, "exp2", "o", b)
                    bank_free(pe, "w3", "y", b)
                    project(bank("w3", "y", b), mat("w3"), zbuf[:, b]).then_inc(full("w3", "y", b), 1)
                elif kind == "rk":
                    pe.wait_ge(mix_done, b + 1)
                    if b == 0:
                        pe.wait_ge(in_later, 16)
                    for m, n in enumerate(("r", "k")):
                        bank_free(pe, "rk", n, b)
                        project(bank("rk", n, b), mat(n + "1"), mixb[:, m]).then_inc(full("rk", n, b), 1)
                elif kind == "kt":
                    bank_free(pe, "kt", "k", b)
                    for k in range(NB):
                        last = nc.tensor.matmul(bank("kt", "k", b)[:, 0:C], mixb[:, 1, k, 0:P], mat("k1")[:, k],
                                                start=(k == 0), stop=(k == NB - 1))
                    last.then_inc(full("kt", "k", b), 1)
                elif kind == "state":
                    bank_done(pe, "kt", "k", b)
                    bank_done(pe, "v1", "v", b)
                    bank_free(pe, "state", "s", b)
                    for k in range(NB):
                        last = nc.tensor.matmul(bank("state", "s", b)[:, k * P:(k + 1) * P], kdec[:, k * P:(k + 1) * P],
                                                vsb[:, 0, k * P:(k + 1) * P], start=True, stop=True)
                    last.then_inc(full("state", "s", b), 1)
                elif kind == "v1":
                    bank_free(pe, "v1", "v", b)
                    project_t(bank("v1", "v", b), mat("v1"), mixb[:, 2]).then_inc(full("v1", "v", b), 1)
                elif kind == "g1":
                    bank_free(pe, "g1", "g", b)
                    project(bank("g1", "g", b), mat("g1"), mixb[:, 3]).then_inc(full("g1", "g", b), 1)
                elif kind == "score":
                    u, g = divmod(i, 4)
                    if g == 0:
                        stacks_in(pe, "score", u)
                    slot_free(pe, "score", i)
                    out = slot("score", i)
                    for h in range(GH):
                        q, k = (st[0:KROWS, u % 2, GH * g + h] for st in (qst, kst))
                        for s in range(TB):
                            at = (TB * h + s) * P
                            last = nc.tensor.matmul(out[:, at:at + P], k[:, s * P:(s + 1) * P],
                                                    q[:, s * P:(s + 1) * P], start=True, stop=True)
                    last.then_inc(slot_filled("score", i), 1)
                elif kind == "Y":
                    slot_done(pe, "score", 4 * i + 3)
                    slot_done(pe, "score", 4 * i + 2)
                    if i % 2 == 0:
                        pe.wait_ge(vm_ready, i // 2 + 1)
                    bank_free(pe, "Y", "y", i)
                    out = bank("Y", "y", i)
                    bank_done(pe, "state", "s", i // 2)
                    bank_done(pe, "rk", "r", i // 2)
                    slot_b = i // 2 % 2
                    for s in range(TB):
                        if s == 1:
                            nc.tensor.matmul(out[:, P:T], state[:, slot_b, i % 2], rdec[:, slot_b, i % 2],
                                             start=True, stop=False)
                        for e in range(GH):
                            for g in range(4):
                                last = nc.tensor.matmul(
                                    out[32 * g:32 * g + 32, s * P:(s + 1) * P], vm[slot_b][:, s, 4 * (i % 2) + g, e],
                                    masked[:, i % 2, GH * g + e, s],
                                    start=(e == 0 and s == 0), stop=(e == GH - 1), tile_position=(0, 32 * g))
                    last.then_inc(full("Y", "y", i), 1)
                elif kind == "norm":
                    for u in (2 * b, 2 * b + 1):
                        bank_done(pe, "Y", "y", u)
                    bank_free(pe, "norm", "c", b)
                    nc.tensor.matmul(bank("norm", "c", b)[:, :], const("center"), ysb.rearrange("p k t -> p (k t)"),
                                     start=True, stop=True).then_inc(full("norm", "c", b), 1)
                elif kind == "var":
                    pe.wait_ge(squared, b + 1)
                    bank_free(pe, "var", "v", b)
                    nc.tensor.matmul(bank("var", "v", b)[:, :], const("mean8"), tmpn[:, 0],
                                     start=True, stop=True).then_inc(full("var", "v", b), 1)
                elif kind == "out1":
                    pe.wait_ge(gated, b + 1)
                    if b == 0:
                        pe.wait_ge(in_out1, 16)
                    bank_free(pe, "out1", "y", b)
                    project(bank("out1", "y", b), mat("o1"), cent).then_inc(full("out1", "y", b), 1)
                elif kind == "last":
                    pe.wait_ge(q8_ready, b + 1)
                    bank_free(pe, "last", "y", b)
                    project(bank("last", "y", b), wbf, qbf).then_inc(full("last", "y", b), 1)

        @block.vector
        def _(dve):
            steps = [0]

            def link(ins):
                steps[0] += 1
                ins.then_inc(vec_step, 1)
                dve.wait_ge(vec_step, steps[0])

            V = nc.vector
            dve.wait_ge(in_fside[0], 16)
            V.tensor_scalar(seq[:, 0, :, 0], fk[:, 0], 30.0, None, ALU.min).then_inc(clipped, 1)
            dve.wait_ge(in_vecs, 32)
            V.reduce_sum(csum, rows[:, 0:256].rearrange("p (b c) -> p b c", b=B), axis=X)
            V.tensor_scalar(cw, vecs[:, 0:8], 80.0, None, ALU.min)
            V.tensor_scalar(lamc, vecs[:, DECAY_COL:DECAY_COL + NB], 80.0, None, ALU.min)
            link(V.tensor_scalar(lam, rows[:, TD_COL:TD_COL + H1], 80.0, None, ALU.min))
            V.tensor_scalar(csum, csum, LOWEST, None, ALU.max).then_inc(csum_done, 1)
            dve.wait_ge(thc_done, 1)
            V.tensor_scalar(gain, csum, -0.2, -0.8, ALU.mult, ALU.add)
            link(V.tensor_scalar(dfac, csum, 0.5, 0.5, ALU.mult, ALU.add))
            dve.wait_ge(dw_done, 2)
            for b in range(B):
                V.tensor_scalar(dec[:, b], dw, dfac[:, b:b + 1], None, ALU.mult)
            V.tensor_scalar(lamc, lamc, 1e30, None, ALU.min)
            link(V.tensor_scalar(lam, lam, 1e30, None, ALU.min))
            def clamp(i):
                V.tensor_scalar(zbuf[:, i % B], x[:, i % B], LOWEST, None, ALU.max).then_inc(clamped, 1)

            def setup_rest():
                dve.wait_ge(in_rest, 64)
                link(V.tensor_copy(w16[0], w8))
                link(V.tensor_scalar(w16[1], w16[0], 0x80, 8, ALU.bitwise_and, ALU.logical_shift_left))
                link(V.tensor_scalar(w16[0], w16[0], 0x7F, 7, ALU.bitwise_and, ALU.logical_shift_left))
                link(V.tensor_tensor(w16[0], w16[0], w16[1], ALU.bitwise_or))
                V.tensor_scalar(wbf[:, :, :].rearrange("p k o -> p (k o)"), w16[0].bitcast(F16), 256.0, None, ALU.mult)
                link(V.tensor_copy(iscale, iscale_bf[:, 0:1]))
                V.tensor_scalar(oscale, iscale, rows[:, WS_COL:WS_COL + 1], None, ALU.mult)
                V.tensor_scalar(gam2, vecs[:, GAMMA_COL:GAMMA_COL + 2], -0.5, None, ALU.mult)
                V.tensor_scalar(bet, vecs[:, BETA_COL:BETA_COL + 2], 1.0, None, ALU.mult)
                link(V.reciprocal(rscale, iscale))
                V.tensor_scalar(rhalf, rscale, 0.5, None, ALU.mult).then_inc(lam_ready, 1)

            def rest(kind, b):
                names = ("q", "k") if kind == "qk" else ("r", "k")
                for w in range(2):
                    n = 2 * b + w + (8 if kind == "rk" else 0)
                    dve.wait_ge(part1, n + 1)
                    if n >= 2:
                        dve.wait_ge(part3, n - 1)
                    key = (kind, names[w], b)
                    if names[w] == "r":
                        V.tensor_tensor(rdec[:, b % 2],
                                        bank(*key)[:, :].rearrange("p (k t) -> p k t", k=NB)[:, :, P:T], wp, ALU.mult)
                    V.tensor_tensor(resid[:, w], bank(*key)[:, :], split[:, w, 0],
                                    ALU.subtract).then_inc(read(*key), 1)

            for kind, i in STEPS:
                b = i
                if kind == "seq":
                    dve.wait_ge(in_fside[b], 16)
                    V.tensor_scalar(seq[:, b, :, 0], fk[:, b], 30.0, None, ALU.min).then_inc(clipped, 1)
                elif kind == "clamp":
                    dve.wait_ge(in_x[b], 16)
                    clamp(b)
                elif kind == "scales":
                    setup_rest()
                elif kind == "condA":
                    l, b = divmod(i, B)
                    if i >= 2:
                        if i - 2 >= ON_VECTOR:
                            dve.wait_ge(tot_ready, i - 1 - ON_VECTOR)
                        dve.wait_ge(ratio_ready, i - 1)
                    for k in range(NB):
                        last = V.tensor_scalar(total[:, i % 2, k, 0], fk[:, b, k], vec(U_COL[l], k), 30.0,
                                               ALU.add, ALU.min)
                    last.then_inc(clipped, 1)
                    f, w = fwd[i % 2], bwd[i % 2]
                    if i < B:
                        dve.wait_ge(seq_ready, b + 1)
                    for k in range(NB):
                        decay = dec[:, b, 2 * l + k:2 * l + k + 1]
                        for m in range(2):
                            V.tensor_tensor_scan(f[:, k, m], decay.to_broadcast([P, T]), seq[:, b, k, m],
                                                 0.0, ALU.mult, ALU.add)
                            last = V.tensor_tensor_scan(w[:, k, m, 0:T - 1][:, ::-1], seq[:, b, k, m, 1:T][:, ::-1],
                                                        decay.to_broadcast([P, T - 1]), 0.0, ALU.add, ALU.mult)
                    last.then_inc(scan_done, 1)
                elif kind == "condB":
                    if i < ON_VECTOR:
                        f = fwd[i % 2]
                        dve.wait_ge(scan_done, i + 1)
                        link(V.tensor_tensor(f, f, bwd[i % 2], ALU.add))
                        dve.wait_ge(eu_ready, i + 1)
                        link(V.tensor_tensor(total[:, i % 2], total[:, i % 2], f, ALU.add))
                    else:
                        dve.wait_ge(tot_ready, i + 1 - ON_VECTOR)
                    V.tensor_scalar(total[:, i % 2, :, 1], total[:, i % 2, :, 1], 1e-8, None,
                                    ALU.max).then_inc(den_max, 1)
                elif kind == "condC":
                    num, den = total[:, i % 2, :, 0], total[:, i % 2, :, 1]
                    if i < ON_VECTOR:
                        dve.wait_ge(rec_ready, i + 1)
                        V.tensor_tensor(num, num, rec, ALU.mult)
                        V.tensor_tensor(den, den, rec, ALU.mult).then_inc(rec_used, 1)
                    dve.wait_ge(rec_used, i + 1)
                    V.scalar_tensor_tensor(ratio[:, i % 8], den, 2.0, num, ALU.subtract,
                                           ALU.mult).then_inc(ratio_ready, 1)
                elif kind == "z":
                    dve.wait_ge(sig_ready, Z_AT[i])
                    dve.wait_ge(ratio_ready, i + 1)
                    z = zbuf[:, i % B]
                    V.scalar_tensor_tensor(z, z, gain[:, i % B:i % B + 1], ratio[:, i % 8], ALU.mult,
                                           ALU.mult).then_inc(z_ready, 1)
                elif kind == "qk":
                    rest(kind, b)
                elif kind == "S":
                    b, g = divmod(i, 4)
                    slot_full(dve, "S", i)
                    src = slot("S", i)
                    V.reduce_max(mxs[:, b % 2, 1, GH * g:GH * g + GH],
                                 src[:, 0:SA].rearrange("p (h t) -> p h t", h=GH), axis=X)
                    V.reduce_max(mxs[:, b % 2, 0, GH * g:GH * g + GH],
                                 src[:, SA:SW].rearrange("p (h t) -> p h t", h=GH),
                                 axis=X).then_inc(slot_read("S", i), 1)
                elif kind == "mx":
                    r = b % 2
                    for g in range(4):
                        slot_done(dve, "S", 4 * b + g)
                    if b >= 2:
                        bank_full(dve, "mt", "t", b - 2)
                    m = [msp[:, r, :, j] for j in range(3)]
                    link(V.tensor_scalar(m[0], mxs[:, r], -1.0, None, ALU.mult))
                    link(V.scalar_tensor_tensor(mres, mxs[:, r], -1.0, m[0], ALU.mult, ALU.subtract))
                    link(V.tensor_copy(m[1], mres))
                    V.tensor_tensor(m[2], mres, m[1], ALU.subtract).then_inc(m_split, 1)
                elif kind == "post":
                    for s in range(TB):
                        key = ("post", f"t{s}", b)
                        bank_full(dve, *key)
                        if s == 0 and b >= 1:
                            bank_full(dve, "post", "zT", b - 1)
                        src = bank(*key)[:, :].rearrange("p (h d) -> p h d", h=H0)
                        link(V.reciprocal(rden[:, s], src[:, :, D0]))
                        V.tensor_tensor(znrm[:, s].rearrange("p (h d) -> p h d", h=H0), src[:, :, 0:D0],
                                        inner(rden[:, s], D0), ALU.mult).then_inc(read(*key), 1)
                    key = ("post", "o", b)
                    bank_full(dve, *key)
                    V.tensor_tensor(x[:, b], x[:, b], bank(*key)[:, :].rearrange("p (k t) -> p k t", k=NB),
                                    ALU.add).then_inc(read(*key), 1)
                    bank_done(dve, *key)
                    clamp(B + b)
                elif kind == "lg":
                    key = ("lg", "g", b)
                    if b == 0:
                        dve.wait_ge(in_consts, 32)
                    else:
                        dve.wait_ge(lgr_ready, b)
                    bank_full(dve, *key)
                    V.tensor_tensor(lmask, bank(*key)[:, 0:T].rearrange("p (e t) -> p e t", e=E),
                                    outer(const("diagm"), E), ALU.mult).then_inc(read(*key), 1)
                    bank_done(dve, *key)
                    V.reduce_sum(lgr[:, b], lmask, axis=X).then_inc(lgr_ready, 1)
                elif kind == "route":
                    key = ("route", "b", 0)
                    bank_full(dve, *key)
                    V.tensor_tensor(pr, bank(*key)[:, 0:B * E].rearrange("p (b e) -> p b e", b=B),
                                    outer(rows[:, SWB_COL:SWB_COL + E], B), ALU.add).then_inc(read(*key), 1)
                    bank_done(dve, *key)
                    link(V.reduce_max(s1, pr, axis=X))
                    V.tensor_tensor(pr, pr, inner(s1, E), ALU.subtract).then_inc(logits_ready, 1)
                    dve.wait_ge(exps_done, 1)
                    link(V.reduce_sum(s2, pr, axis=X))
                    link(V.reciprocal(s3, s2))
                    link(V.tensor_tensor(pr, pr, inner(s3, E), ALU.mult))
                    p = pr
                    for k in range(2):
                        link(V.reduce_max(gt[:, k], p, axis=X))
                        link(V.tensor_tensor(t8, p, inner(gt[:, k], E), ALU.is_equal))
                        link(V.tensor_tensor(t8, t8, outer(const("rev"), B), ALU.mult))
                        link(V.reduce_max(s1, t8, axis=X))
                        link(V.tensor_tensor(oh[:, k], t8, inner(s1, E), ALU.is_equal))
                        if k == 0:
                            link(V.scalar_tensor_tensor(t9, oh[:, 0], -2.0, pr, ALU.mult, ALU.add))
                            p = t9
                elif kind == "pick":
                    for k in range(2):
                        last = V.tensor_tensor(esel[:, k], expert[:, :, :].rearrange("p e c -> p c e"),
                                               outer(oh[:, k, b], EB), ALU.mult)
                    link(last)
                    if b >= 2:
                        bank_done(dve, "exp1", f"h{b % 2}1", 0)
                        dve.wait_ge(bd_ready, b - 1)
                    link(V.reduce_sum(ew[:, b % 2].rearrange("p k c -> p (k c)"),
                                      esel.rearrange("p k c e -> p (k c) e"), axis=X))
                    for k in range(2):
                        half = ew[:, b % 2, k, DH + 1:EB]
                        last = V.tensor_scalar(half, half, gt[:, k, b:b + 1], None, ALU.mult)
                    last.then_inc(gates_picked, 1)
                    dve.wait_ge(gates_picked, b + 1)
                    link(V.tensor_tensor(b2s[:, b:b + 1], ew[:, b % 2, 0, EB - 1:EB], ew[:, b % 2, 1, EB - 1:EB],
                                         ALU.add))
                elif kind == "exp2":
                    key = ("exp2", "o", b)
                    bank_full(dve, *key)
                    z = zbuf[:, b]
                    V.scalar_tensor_tensor(z, bank(*key)[:, :].rearrange("p (k t) -> p k t", k=NB), b2s[:, b:b + 1], z,
                                           ALU.add, ALU.add).then_inc(read(*key), 1)
                elif kind == "w3":
                    key = ("w3", "y", b)
                    bank_full(dve, *key)
                    for k in range(NB):
                        last = V.scalar_tensor_tensor(x[:, b, k], bank(*key)[:, k * T:(k + 1) * T], vec(B3_COL, k),
                                                      x[:, b, k], ALU.add, ALU.add)
                    last.then_inc(read(*key), 1)
                    bank_done(dve, *key)
                    clamp(2 * B + b)
                elif kind == "mix":
                    z = zbuf[:, b]
                    if b:
                        bank_full(dve, "g1", "g", b - 1)
                    dve.wait_ge(diff_done, b + 1)
                    for m, name in enumerate(("r", "k", "v", "g")):
                        for k in range(NB):
                            last = V.scalar_tensor_tensor(mixb[:, m, k], diff[:, k], vec(MAA_COL[name], k), z[:, k],
                                                          ALU.mult, ALU.add)
                    last.then_inc(mix_done, 1)
                elif kind == "rk":
                    if b == 0:
                        dve.wait_ge(decay_ready, 1)
                    elif b >= 2:
                        bank_full(dve, "Y", "y", 2 * b - 3)
                    rest(kind, b)
                elif kind == "kt":
                    key = ("kt", "k", b)
                    bank_full(dve, *key)
                    if b >= 1:
                        bank_full(dve, "state", "s", b - 1)
                    for k in range(NB):
                        last = V.tensor_tensor(
                            kdec[:, k * P:(k + 1) * P].rearrange("p (c h) -> p c h", c=D1),
                            bank(*key)[:, k * P:(k + 1) * P].rearrange("p (c h) -> p c h", c=D1),
                            outer(dk[:, 16 * k:16 * k + 16], D1), ALU.mult)
                    last.then_inc(read(*key), 1)
                elif kind == "state":
                    key = ("state", "s", b)
                    bank_full(dve, *key)
                    if b >= 2:
                        bank_full(dve, "Y", "y", 2 * b - 3)
                    V.tensor_tensor(state[:, b % 2], bank(*key)[:, 0:C].rearrange("p (k n) -> p k n", k=NB),
                                    outer(const("smask"), NB), ALU.mult).then_inc(read(*key), 1)
                elif kind == "g1":
                    key = ("g1", "g", b)
                    g = bank(*key)[:, :].rearrange("p (k t) -> p k t", k=NB)
                    bank_full(dve, *key)
                    if b >= 1:
                        dve.wait_ge(gated, b)
                    V.tensor_scalar(sgate, g, LOWEST, None, ALU.max).then_inc(clamped_g, 1)
                elif kind == "gate":
                    key = ("g1", "g", b)
                    g = bank(*key)[:, :].rearrange("p (k t) -> p k t", k=NB)
                    dve.wait_ge(sig_g, b + 1)
                    V.tensor_tensor(sgate, sgate, g, ALU.mult).then_inc(read(*key), 1)
                elif kind == "wmask":
                    dve.wait_ge(wtri_done, i + 1)
                    w = wmask[:, GH * i:GH * i + GH, 0:P]
                    for h in range(GH):
                        at = FA_COL + GH * i + h
                        last = V.scalar_tensor_tensor(w[:, h], ident, rows[:, at:at + 1],
                                                      w[:, h], ALU.mult, ALU.add)
                    last.then_inc(wmask_done, 1)
                elif kind == "score":
                    u, g = divmod(i, 4)
                    slot_full(dve, "score", i)
                    if u < 2:
                        dve.wait_ge(wmask_done, i + 1)
                    if u >= 2 and g == 0:
                        bank_full(dve, "Y", "y", u - 2)
                    w = wmask[:, 16 * (u % 2) + GH * g:16 * (u % 2) + GH * g + GH]
                    V.tensor_tensor(masked[:, u % 2, GH * g:GH * g + GH],
                                    slot("score", i)[:, 0:GH * T].rearrange("p (h s t) -> p h s t", h=GH, s=TB),
                                    w.unsqueeze(2).to_broadcast([P, GH, TB, P]),
                                    ALU.mult).then_inc(slot_read("score", i), 1)
                elif kind == "var":
                    dve.wait_ge(newton_in, b + 1)
                    sq, r = tmpn[:, 0], tmpn[:, 1]
                    key = ("var", "v", b)
                    V.scalar_tensor_tensor(sq, bank(*key)[:, :], EPS1, sq, ALU.add, ALU.mult).then_inc(read(*key), 1)
                    bank_done(dve, *key)
                    link(V.scalar_tensor_tensor(r, sq, 3.0, r, ALU.subtract, ALU.mult))
                    for k in range(NB):
                        last = V.scalar_tensor_tensor(cent[:, k], cent[:, k], gam2[:, k:k + 1],
                                                      tmpn[:, 1, k * T:(k + 1) * T], ALU.mult, ALU.mult)
                    link(last)
                    for k in range(NB):
                        last = V.scalar_tensor_tensor(cent[:, k], cent[:, k], bet[:, k:k + 1], sgate[:, k],
                                                      ALU.add, ALU.mult)
                    last.then_inc(gated, 1)
                elif kind == "out1":
                    key = ("out1", "y", b)
                    bank_full(dve, *key)
                    V.tensor_tensor(x[:, b], x[:, b], bank(*key)[:, :].rearrange("p (k t) -> p k t", k=NB),
                                    ALU.add).then_inc(read(*key), 1)
                    bank_done(dve, *key)
                    clamp(3 * B + b)
                elif kind == "fp8":
                    dve.wait_ge(scaled8, b + 1)
                    whole, half = tmpn[:, 0], tmpn[:, 1]
                    V.tensor_scalar(q8[:, 0], whole, 128.0, -128.0, ALU.min, ALU.max, saturate=False)
                    link(V.tensor_scalar(q8[:, 1], half, FP8_HALF, -FP8_HALF, ALU.min, ALU.max, saturate=False))
                    link(V.tensor_scalar(whole, q8[:, 1], 64.0, -64.0, ALU.min, ALU.max))
                    link(V.tensor_tensor(half, q8[:, 1], whole, ALU.subtract))
                    if b:
                        bank_full(dve, "last", "y", b - 1)
                    V.scalar_tensor_tensor(qbf[:, :, :].rearrange("p k t -> p (k t)"), half, 2.0, q8[:, 0],
                                           ALU.mult, ALU.add).then_inc(q8_ready, 1)
                elif kind == "last":
                    key = ("last", "y", b)
                    bank_full(dve, *key)
                    V.scalar_tensor_tensor(x[:, b], bank(*key)[:, :].rearrange("p (k t) -> p k t", k=NB), oscale,
                                           x[:, b], ALU.mult, ALU.add).then_inc(read(*key), 1)


def by_partition(a):
    return a.reshape(NB, P, -1).transpose(1, 0, 2)


def host_arrays(i):
    h = {k: np.asarray(v) for k, v in i.items()}

    def activations(a):
        return a.transpose(2, 0, 1).reshape(NB, P, B, T).transpose(1, 2, 0, 3)

    def order(heads, width):
        return np.concatenate([k * P + np.arange(P).reshape(heads, width).T.ravel() for k in range(NB)])

    q0 = np.arange(C).reshape(8, NB, D0).transpose(1, 2, 0).ravel()
    r1 = order(16, D1)
    mats = [h["L0_attn_Wq"][q0], h["L0_attn_Wk"][q0], h["L0_attn_Wv"], h["L0_attn_Wo"], h["L0_ffn_w3"],
            h["L1_attn_Wr"][r1], h["L1_attn_Wk"][r1], h["L1_attn_Wv"], h["L1_attn_Wg"], h["L1_attn_Wo"]]
    weights = np.stack([by_partition(m.T).reshape(P, NB * C) for m in mats], axis=1)
    cols = [h[f"{n}_{w}"] for w in "wu" for n in ("L0_cond", "L0_cond2", "L1_cond", "L1_cond2")]
    cols += [h[f"L1_attn_time_maa_{n}"].reshape(C) for n in "kvrg"]
    cols += [h["L1_attn_gamma"], h["L1_attn_beta"], h["L0_ffn_b3"]]
    cols += [np.tile(h["L1_attn_time_decay"].reshape(NB, 1, 16), (1, D1, 1)).ravel()]
    vecs = np.concatenate([c.reshape(NB, P).T for c in cols], axis=1)
    row = np.concatenate([h["cond_512"].ravel(), h["L0_ffn_switch_b"], h["L1_attn_time_decay"].ravel(),
                          h["L1_attn_time_faaaa"].ravel(), h["L1_ffn_weight_scale"].reshape(1)])
    sw = h["L0_ffn_switch_w"].reshape(E, 8, 32, NB, P)
    bank = np.concatenate([h["L0_ffn_w1"].transpose(2, 0, 1), h["L0_ffn_b1"].T[:, :, None],
                           h["L0_ffn_w2"].transpose(2, 0, 1), h["L0_ffn_b2"].T[:, :, None]], axis=2)
    t = np.arange(P)
    same = t[:, None] // D1 == t[None, :] // D1
    negd = -np.maximum(t[None, :] - t[:, None] - 1, 0)
    hmask = np.arange(32)[None, :] // D1 == np.arange(GH)[:, None]
    made = {"ident": np.eye(P), "center": np.eye(P) - same / D1, "mean8": same / D1, "ones": np.ones((P, P)),
            "tri": t[None, :] > t[:, None], "negd": negd, "diagm": t[:, None] % 32 == np.arange(32)[None, :],
            "hmask": np.broadcast_to(hmask.reshape(1, P), (P, P)),
            "bdm": t[:, None] // DH == np.arange(8)[None, :],
            "rev": np.broadcast_to(E - np.arange(E), (P, E)), "eps": np.full((P, 1), EPS1),
            "zero": np.zeros((P, 1)), "negi": np.broadcast_to(-t, (P, P)), "negj": (t - (P - 1))[:, None],
            "smask": t[:, None] % 16 == t[None, :] // D1}
    bf16 = mybir.dt.np(BF16)
    later = np.where(t[None, :] > t[:, None], NEG, 0.0)
    out = {
        "x": activations(h["x"]), "fside": activations(h["fside_BxSxS_0"]), "weights": weights, "vecs": vecs,
        "rows": np.tile(row[None, :], (P, 1)), "switch": sw.transpose(4, 3, 1, 0, 2).reshape(P, -1),
        "expert": np.tile(bank, (8, 1, 1)), "w8": by_partition(h["L1_ffn_weight"].view(np.uint8).T).reshape(P, -1),
        "iscale": np.tile(h["L1_ffn_input_scale"].reshape(1, 1), (P, 1)),
        "consts": np.concatenate([made[n] for n in CONSTS], axis=1).astype(np.float32),
        "consts_bf16": np.concatenate([np.eye(P), later, later.T], axis=1).astype(bf16),
    }
    return {k: np.ascontiguousarray(v) for k, v in out.items()}


def kernel(**inputs):
    import concourse.bacc as bacc
    from concourse.bass_utils import run_bass_kernel_spmd

    arrays = host_arrays(inputs)
    nc = bacc.Bacc("TRN2", target_bir_lowering=False, num_devices=1)
    d = {k: nc.dram_tensor(f"in_{k}", a.shape, mybir.dt.from_np(a.dtype), kind="ExternalInput").ap()
         for k, a in arrays.items()}
    d["out"] = nc.dram_tensor("out", (P, B, NB, T), F32, kind="ExternalOutput").ap()
    build(nc, d)
    result = run_bass_kernel_spmd(nc, [{f"in_{k}": a for k, a in arrays.items()}], core_ids=[0])
    out = result.results[0]["out"]
    return out.transpose(1, 3, 2, 0).reshape(B, T, C)
```
